# Optimizing a Trainium2 kernel written in Bass

```python
import numpy as np
import jax
import jax.numpy as jnp

def _softmax(x, axis=-1):
    return jax.nn.softmax(x, axis=axis)

def _gelu(x):
    return jax.nn.gelu(x, approximate=True)

def _silu(x):
    return jax.nn.silu(x)

def _sigmoid(x):
    return jax.nn.sigmoid(x)

def _layernorm(x, axis=-1, eps=1e-05):
    m = jnp.mean(x, axis=axis, keepdims=True)
    v = jnp.var(x, axis=axis, keepdims=True)
    return (x - m) / jnp.sqrt(v + eps)

def _scatter_add(tgt, idx, src, axis=0):
    return tgt.at[idx].add(src)

def _segment_sum(src, seg, n):
    return jax.ops.segment_sum(src, seg, n)
kernel_name = 'mk_gnn_resnorm_d4_gnn_r8_1c951b'

def setup_inputs(seed: int=0):
    np.random.seed(seed)
    _w = jnp.asarray

    def _rec_inputs():
        import jax
        import jax.numpy as jnp
        _gk = jax.random.key(seed)
        x = -0.0009044 + 1 * jax.random.normal(jax.random.fold_in(_gk, 1), (12500, 32), jnp.float32)
        src = jax.random.randint(jax.random.fold_in(_gk, 2), (400000,), 0, 12500, jnp.int32)
        dst = jnp.minimum((12500 * jax.random.uniform(jax.random.fold_in(_gk, 3), (400000,)) ** 2.0).astype(jnp.int32), 99999)
        _o = jnp.argsort(dst, stable=True)
        src = src[_o]
        dst = dst[_o]
        edge_attr_3 = 0.000844983 + 0.999762 * jax.random.normal(jax.random.fold_in(_gk, 11), (400000, 3), jnp.float32)
        edge_weight = jax.random.uniform(jax.random.fold_in(_gk, 13), (400000,), jnp.float32, 0.0, 0.999999)
        return (x, src, dst, edge_attr_3, edge_weight)
    x, src, dst, edge_attr_3, edge_weight = _rec_inputs()

    def _L0_gnn_setup():
        import jax, jax.numpy as jnp
        import numpy as np
        N = 6250
        E = 200000
        F_IN = 32
        F_OUT = 32
        key = jax.random.key(seed)
        k_x, k_ei, k_norm, k_w, k_b = jax.random.split(key, 5)
        x = jax.random.normal(k_x, (N, F_IN), dtype=jnp.float32)
        edge_index = jax.random.randint(k_ei, (2, E), 0, N, dtype=jnp.int64)
        norm = jax.random.uniform(k_norm, (E,), dtype=jnp.float32)
        W = jax.random.normal(k_w, (F_IN, F_OUT), dtype=jnp.float32) / np.sqrt(F_IN)
        b = jax.random.normal(k_b, (F_OUT,), dtype=jnp.float32) * 0.01
        return {'x': x, 'edge_index': edge_index, 'norm': norm, 'W': W, 'b': b}
    _L0_gnn_all = _L0_gnn_setup()
    _L0_gnn_in = {k: v for k, v in _L0_gnn_all.items() if k in ('W', 'b')}
    del _L0_gnn_all

    def _L1_gnn_setup():
        import jax, jax.numpy as jnp
        import numpy as np
        N_NODES = 6250
        DEG = 16
        N_HEAD = 4
        F_IN = 32
        F_OUT = 32
        key = jax.random.key(seed)
        k_h, k_w, k_fw, k_fb = jax.random.split(key, 4)
        h = jax.random.normal(k_h, (N_NODES, F_IN), dtype=jnp.float32)
        src = jnp.repeat(jnp.arange(N_NODES, dtype=jnp.int64), DEG)
        offs = (jnp.arange(DEG, dtype=jnp.int64) + 1) * 97
        dst = (src.reshape(N_NODES, DEG) + offs[None, :]).reshape(-1) % N_NODES
        edge_index = jnp.stack([src, dst], axis=0)
        gain = 1.414
        bound_w = gain * np.sqrt(6.0 / (F_IN + F_OUT))
        w = jax.random.uniform(k_w, (N_HEAD, F_IN, F_OUT), jnp.float32, -bound_w, bound_w)
        bound_fc = np.sqrt(1.0 / (2 * F_OUT))
        fc_w = jax.random.uniform(k_fw, (1, 2 * F_OUT), jnp.float32, -bound_fc, bound_fc)
        fc_b = jax.random.uniform(k_fb, (1,), jnp.float32, -bound_fc, bound_fc)
        bias = jnp.zeros((F_OUT,), jnp.float32)
        return {'h': h, 'edge_index': edge_index, 'w': w, 'fc_w': fc_w, 'fc_b': fc_b, 'bias': bias}
    _L1_gnn_all = _L1_gnn_setup()
    _L1_gnn_in = {k: v for k, v in _L1_gnn_all.items() if k in ('w', 'fc_w', 'fc_b', 'bias')}
    del _L1_gnn_all

    def _L2_gnn_setup():
        import jax, jax.numpy as jnp
        import numpy as np
        K = 2
        N_NODES = 12500
        N_EDGES = 200000
        D_FEAT = 32
        key = jax.random.key(seed)
        k1, k2 = jax.random.split(key)
        x = jax.random.normal(k1, (N_NODES, D_FEAT), dtype=jnp.float32)
        edge_index = jax.random.randint(k2, (2, N_EDGES), 0, N_NODES, dtype=jnp.int32)
        return {'x': x, 'edge_index': edge_index}
    _L2_gnn_all = _L2_gnn_setup()
    _L2_gnn_in = {k: v for k, v in _L2_gnn_all.items() if k in ()}
    del _L2_gnn_all

    def _L3_gnn_setup():
        import jax, jax.numpy as jnp
        import numpy as np
        from math import factorial, pi, sqrt
        MUL = 8
        RS = [(MUL, 0), (MUL, 1)]
        N_NODES = 2500
        N_EDGES = 80000
        FEAT_DIM = sum((m * (2 * l + 1) for m, l in RS))
        R_DIM = sum((mo * mi * (2 * min(lo, li) + 1) for mo, lo in RS for mi, li in RS))
        HIDDEN = 64

        def _cg(j1, j2, j3, m1, m2, m3):
            if m1 + m2 != m3:
                return 0.0
            f = factorial
            pre = sqrt((2 * j3 + 1) * f(j3 + j1 - j2) * f(j3 - j1 + j2) * f(j1 + j2 - j3) / f(j1 + j2 + j3 + 1))
            pre *= sqrt(f(j3 + m3) * f(j3 - m3) * f(j1 - m1) * f(j1 + m1) * f(j2 - m2) * f(j2 + m2))
            kmin = max(0, j2 - j3 - m1, j1 - j3 + m2)
            kmax = min(j1 + j2 - j3, j1 - m1, j2 + m2)
            s = 0.0
            for k in range(kmin, kmax + 1):
                s += (-1) ** k / (f(k) * f(j1 + j2 - j3 - k) * f(j1 - m1 - k) * f(j2 + m2 - k) * f(j3 - j2 + m1 + k) * f(j3 - j1 - m2 + k))
            return pre * s

        def _w3j_complex(l1, l2, l3):
            w = np.zeros((2 * l1 + 1, 2 * l2 + 1, 2 * l3 + 1))
            for m1 in range(-l1, l1 + 1):
                for m2 in range(-l2, l2 + 1):
                    m3 = -(m1 + m2)
                    if abs(m3) <= l3:
                        w[m1 + l1, m2 + l2, m3 + l3] = (-1) ** (l1 - l2 - m3) / sqrt(2 * l3 + 1) * _cg(l1, l2, l3, m1, m2, -m3)
            return w

        def _A(l):
            A = np.zeros((2 * l + 1, 2 * l + 1), dtype=complex)
            A[l, l] = 1.0
            for m in range(1, l + 1):
                A[l + m, l + m] = (-1) ** m / sqrt(2)
                A[l + m, l - m] = 1.0 / sqrt(2)
                A[l - m, l - m] = 1j / sqrt(2)
                A[l - m, l + m] = -1j * (-1) ** m / sqrt(2)
            return A

        def real_w3j(l1, l2, l3):
            wc = _w3j_complex(l1, l2, l3).astype(complex)
            wr = np.einsum('abc,ma,nb,oc->mno', wc, _A(l1).conj(), _A(l2).conj(), _A(l3).conj())
            i = int(np.argmax(np.abs(wr)))
            ph = wr.flat[i] / abs(wr.flat[i])
            wr = wr / ph
            assert np.abs(wr.imag).max() < 1e-10
            return np.real(wr).astype(np.float32)
        _W3J = {}
        for _mo, _lo in RS:
            for _mi, _li in RS:
                for _lf in range(abs(_lo - _li), _lo + _li + 1):
                    if (_lo, _lf, _li) not in _W3J:
                        _W3J[_lo, _lf, _li] = jnp.asarray(real_w3j(_lo, _lf, _li))
        _NORM = []
        for _mo, _lo in RS:
            _num = sum((mi * (2 * min(_lo, li) + 1) for mi, li in RS))
            _NORM.append(sqrt(4.0 * pi) * sqrt(2.0 * _lo + 1.0) / sqrt(_num))
        _F_OFFS = [0] + list(np.cumsum([mi * (2 * li + 1) for mi, li in RS]))

        def spherical_harmonics(rel_vec):
            r = rel_vec / jnp.linalg.norm(rel_vec, axis=-1, keepdims=True)
            x, y, z = (r[:, 0], r[:, 1], r[:, 2])
            y0 = jnp.full_like(x, 0.5 / sqrt(pi))[:, None]
            c1 = sqrt(3.0 / (4.0 * pi))
            y1 = c1 * jnp.stack([y, z, x], axis=-1)
            c2a = 0.5 * sqrt(15.0 / pi)
            c2b = 0.25 * sqrt(5.0 / pi)
            c2c = 0.25 * sqrt(15.0 / pi)
            y2 = jnp.stack([c2a * x * y, c2a * y * z, c2b * (3.0 * z * z - 1.0), c2a * x * z, c2c * (x * x - y * y)], axis=-1)
            return jnp.concatenate([y0, y1, y2], axis=-1)
        key = jax.random.key(seed)
        ks = jax.random.split(key, 6)
        features = jax.random.normal(ks[0], (N_NODES, FEAT_DIM), dtype=jnp.float32)
        abs_distances = jax.random.uniform(ks[1], (N_EDGES,), dtype=jnp.float32, minval=0.1, maxval=1.0)
        rel_vec = jax.random.normal(ks[2], (N_EDGES, 3), dtype=jnp.float32)
        edge_index = jax.random.randint(ks[3], (2, N_EDGES), 0, N_NODES, dtype=jnp.int32)
        w1 = jax.random.normal(ks[4], (1, HIDDEN), dtype=jnp.float32)
        b1 = jnp.zeros((HIDDEN,), jnp.float32)
        w2 = jax.random.normal(ks[5], (HIDDEN, R_DIM), dtype=jnp.float32) / sqrt(HIDDEN)
        b2 = jnp.zeros((R_DIM,), jnp.float32)
        return {'features': features, 'abs_distances': abs_distances, 'rel_vec': rel_vec, 'edge_index': edge_index, 'w1': w1, 'b1': b1, 'w2': w2, 'b2': b2}
    _L3_gnn_all = _L3_gnn_setup()
    _L3_gnn_in = {k: v for k, v in _L3_gnn_all.items() if k in ('w1', 'b1', 'w2', 'b2')}
    del _L3_gnn_all
    return {'x': x, 'src': src, 'dst': dst, 'edge_attr_3': edge_attr_3, 'edge_weight': edge_weight, 'L0_gnn_W': _L0_gnn_in['W'], 'L0_gnn_b': _L0_gnn_in['b'], 'L1_gnn_w': _L1_gnn_in['w'], 'L1_gnn_fc_w': _L1_gnn_in['fc_w'], 'L1_gnn_fc_b': _L1_gnn_in['fc_b'], 'L1_gnn_bias': _L1_gnn_in['bias'], 'L3_gnn_w1': _L3_gnn_in['w1'], 'L3_gnn_b1': _L3_gnn_in['b1'], 'L3_gnn_w2': _L3_gnn_in['w2'], 'L3_gnn_b2': _L3_gnn_in['b2']}

def reference(x, src, dst, edge_attr_3, edge_weight, L0_gnn_W, L0_gnn_b, L1_gnn_w, L1_gnn_fc_w, L1_gnn_fc_b, L1_gnn_bias, L3_gnn_w1, L3_gnn_b1, L3_gnn_w2, L3_gnn_b2):
    import jax
    import jax.numpy as jnp

    def _L0_gnn_ref(x, edge_index, norm, W, b):
        import jax, jax.numpy as jnp
        import numpy as np
        N = 6250
        E = 200000
        F_IN = 32
        F_OUT = 32
        x_j = x[edge_index[0]]
        msg = norm[:, None] * x_j
        agg = jax.ops.segment_sum(msg, edge_index[1], num_segments=x.shape[0])
        return jax.nn.relu(agg @ W + b)

    def _L1_gnn_ref(h, edge_index, w, fc_w, fc_b, bias):
        import jax, jax.numpy as jnp
        import numpy as np
        N_NODES = 6250
        DEG = 16
        N_HEAD = 4
        F_IN = 32
        F_OUT = 32
        n_head, f_in, f_out = w.shape
        n = h.shape[0]
        src, dst = (edge_index[0], edge_index[1])
        hp = jnp.einsum('nf,hfo->hno', h, w)
        w_src = fc_w[0, :f_out]
        w_dst = fc_w[0, f_out:]
        a_src = jnp.einsum('hnf,f->hn', hp, w_src)
        a_dst = jnp.einsum('hnf,f->hn', hp, w_dst)
        e = a_src[:, src] + a_dst[:, dst] + fc_b[0]
        e = jax.nn.leaky_relu(e, negative_slope=0.2)
        seg_max = jax.ops.segment_max(e.T, src, num_segments=n)
        e = jnp.exp(e - seg_max.T[:, src])
        seg_sum = jax.ops.segment_sum(e.T, src, num_segments=n)
        att = e / seg_sum.T[:, src]
        msg = att[:, :, None] * hp[:, dst, :]
        agg = jax.vmap(lambda m: jax.ops.segment_sum(m, src, num_segments=n))(msg)
        out = agg.mean(axis=0) + bias
        return out

    def _L2_gnn_ref(x, edge_index):
        import jax, jax.numpy as jnp
        import numpy as np
        K = 2
        N_NODES = 12500
        N_EDGES = 200000
        D_FEAT = 32
        n = x.shape[0]
        x = jax.nn.relu(x)
        loops = jnp.arange(n, dtype=edge_index.dtype)
        src = jnp.concatenate([edge_index[0], loops])
        dst = jnp.concatenate([edge_index[1], loops])
        deg = jax.ops.segment_sum(jnp.ones_like(src, dtype=x.dtype), dst, num_segments=n)
        dinv = jax.lax.rsqrt(jnp.maximum(deg, 1.0))
        norm = (dinv[src] * dinv[dst])[:, None]
        for _ in range(K):
            x = jax.ops.segment_sum(x[src] * norm, dst, num_segments=n)
        return x

    def _L3_gnn_ref(features, abs_distances, rel_vec, edge_index, w1, b1, w2, b2):
        import jax, jax.numpy as jnp
        import numpy as np
        from math import factorial, pi, sqrt
        MUL = 8
        RS = [(MUL, 0), (MUL, 1)]
        N_NODES = 2500
        N_EDGES = 80000
        FEAT_DIM = sum((m * (2 * l + 1) for m, l in RS))
        R_DIM = sum((mo * mi * (2 * min(lo, li) + 1) for mo, lo in RS for mi, li in RS))
        HIDDEN = 64

        def _cg(j1, j2, j3, m1, m2, m3):
            if m1 + m2 != m3:
                return 0.0
            f = factorial
            pre = sqrt((2 * j3 + 1) * f(j3 + j1 - j2) * f(j3 - j1 + j2) * f(j1 + j2 - j3) / f(j1 + j2 + j3 + 1))
            pre *= sqrt(f(j3 + m3) * f(j3 - m3) * f(j1 - m1) * f(j1 + m1) * f(j2 - m2) * f(j2 + m2))
            kmin = max(0, j2 - j3 - m1, j1 - j3 + m2)
            kmax = min(j1 + j2 - j3, j1 - m1, j2 + m2)
            s = 0.0
            for k in range(kmin, kmax + 1):
                s += (-1) ** k / (f(k) * f(j1 + j2 - j3 - k) * f(j1 - m1 - k) * f(j2 + m2 - k) * f(j3 - j2 + m1 + k) * f(j3 - j1 - m2 + k))
            return pre * s

        def _w3j_complex(l1, l2, l3):
            w = np.zeros((2 * l1 + 1, 2 * l2 + 1, 2 * l3 + 1))
            for m1 in range(-l1, l1 + 1):
                for m2 in range(-l2, l2 + 1):
                    m3 = -(m1 + m2)
                    if abs(m3) <= l3:
                        w[m1 + l1, m2 + l2, m3 + l3] = (-1) ** (l1 - l2 - m3) / sqrt(2 * l3 + 1) * _cg(l1, l2, l3, m1, m2, -m3)
            return w

        def _A(l):
            A = np.zeros((2 * l + 1, 2 * l + 1), dtype=complex)
            A[l, l] = 1.0
            for m in range(1, l + 1):
                A[l + m, l + m] = (-1) ** m / sqrt(2)
                A[l + m, l - m] = 1.0 / sqrt(2)
                A[l - m, l - m] = 1j / sqrt(2)
                A[l - m, l + m] = -1j * (-1) ** m / sqrt(2)
            return A

        def real_w3j(l1, l2, l3):
            wc = _w3j_complex(l1, l2, l3).astype(complex)
            wr = np.einsum('abc,ma,nb,oc->mno', wc, _A(l1).conj(), _A(l2).conj(), _A(l3).conj())
            i = int(np.argmax(np.abs(wr)))
            ph = wr.flat[i] / abs(wr.flat[i])
            wr = wr / ph
            assert np.abs(wr.imag).max() < 1e-10
            return np.real(wr).astype(np.float32)
        _W3J = {}
        for _mo, _lo in RS:
            for _mi, _li in RS:
                for _lf in range(abs(_lo - _li), _lo + _li + 1):
                    if (_lo, _lf, _li) not in _W3J:
                        _W3J[_lo, _lf, _li] = jnp.asarray(real_w3j(_lo, _lf, _li))
        _NORM = []
        for _mo, _lo in RS:
            _num = sum((mi * (2 * min(_lo, li) + 1) for mi, li in RS))
            _NORM.append(sqrt(4.0 * pi) * sqrt(2.0 * _lo + 1.0) / sqrt(_num))
        _F_OFFS = [0] + list(np.cumsum([mi * (2 * li + 1) for mi, li in RS]))

        def spherical_harmonics(rel_vec):
            r = rel_vec / jnp.linalg.norm(rel_vec, axis=-1, keepdims=True)
            x, y, z = (r[:, 0], r[:, 1], r[:, 2])
            y0 = jnp.full_like(x, 0.5 / sqrt(pi))[:, None]
            c1 = sqrt(3.0 / (4.0 * pi))
            y1 = c1 * jnp.stack([y, z, x], axis=-1)
            c2a = 0.5 * sqrt(15.0 / pi)
            c2b = 0.25 * sqrt(5.0 / pi)
            c2c = 0.25 * sqrt(15.0 / pi)
            y2 = jnp.stack([c2a * x * y, c2a * y * z, c2b * (3.0 * z * z - 1.0), c2a * x * z, c2c * (x * x - y * y)], axis=-1)
            return jnp.concatenate([y0, y1, y2], axis=-1)
        src, dst = (edge_index[0], edge_index[1])
        R = jax.nn.relu(abs_distances[:, None] @ w1 + b1) @ w2 + b2
        Y = spherical_harmonics(rel_vec)
        Fj = features[src]
        E = Fj.shape[0]
        msg_blocks = []
        r_off = 0
        for i, (mo, lo) in enumerate(RS):
            acc = jnp.zeros((E, mo, 2 * lo + 1), dtype=features.dtype)
            for j, (mi, li) in enumerate(RS):
                n_lf = 2 * min(lo, li) + 1
                sz = mo * mi * n_lf
                Rb = R[:, r_off:r_off + sz].reshape(E, mo, mi, n_lf)
                r_off += sz
                Fb = Fj[:, _F_OFFS[j]:_F_OFFS[j + 1]].reshape(E, mi, 2 * li + 1)
                for k, lf in enumerate(range(abs(lo - li), lo + li + 1)):
                    C = _W3J[lo, lf, li]
                    Yf = Y[:, lf * lf:(lf + 1) * (lf + 1)]
                    acc = acc + _NORM[i] * jnp.einsum('euv,ef,evi,ofi->euo', Rb[..., k], Yf, Fb, C)
            msg_blocks.append(acc.reshape(E, -1))
        msg = jnp.concatenate(msg_blocks, axis=-1)
        out = jnp.zeros((features.shape[0], msg.shape[1]), dtype=features.dtype)
        out = out.at[dst].add(msg)
        return out
    edge_index = jnp.stack([src, dst])
    x = _layernorm(x + _L0_gnn_ref(x, edge_index, edge_weight, L0_gnn_W, L0_gnn_b), axis=-1)
    x = _layernorm(x + _L1_gnn_ref(x, edge_index, L1_gnn_w, L1_gnn_fc_w, L1_gnn_fc_b, L1_gnn_bias), axis=-1)
    x = _layernorm(x + _L2_gnn_ref(x, edge_index), axis=-1)
    x = _layernorm(x + _L3_gnn_ref(x, edge_weight, edge_attr_3, edge_index, L3_gnn_w1, L3_gnn_b1, L3_gnn_w2, L3_gnn_b2), axis=-1)
    return x

_drawn_inputs = setup_inputs


def setup_inputs(seed=0):
    import zlib

    import numpy as np

    out = dict(_drawn_inputs(seed))
    spreads = {'L1_gnn_bias': (0.0, 0.1), 'L3_gnn_b1': (0.0, 0.1), 'L3_gnn_b2': (0.0, 0.1)}
    factors = {'L0_gnn_b': 5.729}
    for name, (base, spread) in spreads.items():
        noise = np.random.default_rng([zlib.crc32(name.encode()), seed]).standard_normal(out[name].shape)
        drawn = base * np.exp(spread * noise) if base else spread * noise
        out[name] = jnp.asarray(drawn.astype(out[name].dtype))
    for name, factor in factors.items():
        out[name] = (out[name] * factor).astype(out[name].dtype)
    return out
```

```python
from contextlib import ExitStack, contextmanager
from math import pi, sqrt

import concourse.bass as bass
from concourse import mybir

F32 = mybir.dt.float32
I32 = mybir.dt.int32
U16 = mybir.dt.uint16
BF16 = mybir.dt.bfloat16
ALU = mybir.AluOpType
ACT = mybir.ActivationFunctionType
AX = mybir.AxisListType

P = 128
NODES = 12500
EDGES = 400000
F = 32
HEADS = 4
HIDDEN = 64
RADIAL = 384
BINS = -(-NODES // P)
LAST = NODES - (BINS - 1) * P
COLS = EDGES // P
PER = 4
GROUP = P * PER
SLOTS = 4
NEEDED = (EDGES + BINS * (GROUP - 1)) // GROUP
TURNS = -(-NEEDED // SLOTS)
GROUPS = TURNS * SLOTS
TABLE = P * -(-GROUPS // P)
TCOLS = TABLE // P
BY_DST = 8
BY_SRC = 2
FAR = 40
BIG = 1e30
EPS = 1e-5
BATCH = 7
MUL = 8


@contextmanager
def stage(nc, k):
    made = []

    def sem(name):
        made.append(nc.alloc_semaphore(name))
        return made[-1]

    k.sem = sem
    with ExitStack() as ctx:
        yield ctx
    nc.clear_and_free_semaphores(made)
    nc.all_engine_barrier()


class Memory:
    pass


class Steps:

    def __init__(self, engine, semaphore):
        self.engine, self.semaphore, self.n = engine, semaphore, 0

    def restart(self):
        self.engine.sem_clear(self.semaphore)
        self.n = 0

    def step(self, instruction):
        instruction.then_inc(self.semaphore, 1)
        self.n += 1
        return self.n

    def wait(self, n=None):
        self.engine.wait_ge(self.semaphore, self.n if n is None else n)


def spread(ap, axis, n):
    ap = ap.unsqueeze(axis)
    shape = list(ap.shape)
    shape[axis] = n
    return ap.broadcast_to(shape)


def turn(i, slot, of):
    return i * (SLOTS // of) + slot // of + 1


def node_rows(table):
    whole = table[0:(BINS - 1) * P, :].rearrange("(b p) f -> p b f", p=P)
    return whole, table[(BINS - 1) * P:NODES, :]


def setup(nc, k):
    with stage(nc, k) as ctx:
        made = k.sem("constants_made")
        cleared = k.sem("constants_cleared")
        padded = k.sem("last_bin_cleared")
        loaded = k.sem("setup_loaded")
        block = ctx.enter_context(nc.Block())

        @block.gpsimd
        def _(pool):
            pool.iota(k.iota[:], pattern=[[1, P]], base=0, channel_multiplier=0,
                      allow_small_or_imprecise_dtypes=True).then_inc(made, 1)
            pool.iota(k.group_no[:], pattern=[[1, TCOLS]], base=0, channel_multiplier=TCOLS,
                      allow_small_or_imprecise_dtypes=True).then_inc(made, 1)
            pool.memset(k.ident[:], 0.0).then_inc(cleared, 1)
            pool.memset(k.before[:], 1.0).then_inc(cleared, 1)
            pool.memset(k.ones[:], 1.0).then_inc(made, 1)
            pool.memset(k.eps[:], EPS).then_inc(made, 1)
            pool.wait_ge(cleared, 2)
            pool.affine_select(out=k.ident[:], in_=k.ident[:], compare_op=ALU.not_equal, fill=1.0,
                               base=0, pattern=[[-1, P]], channel_multiplier=1).then_inc(made, 1)
            pool.affine_select(out=k.before[:], in_=k.before[:], compare_op=ALU.is_gt, fill=0.0,
                               base=0, pattern=[[1, P]], channel_multiplier=-1).then_inc(made, 1)
            pool.wait_ge(made, 6)

        @block.vector
        def _(dve):
            dve.memset(k.x[:, BINS - 1, :], 0.0).then_inc(padded, 1)

        @block.sync
        def _(sp):
            whole, last = node_rows(k.in_x)
            sp.dma_start(k.x[:, 0:BINS - 1, :], whole).then_inc(loaded, 16)
            sp.wait_ge(padded, 1)
            sp.dma_start(k.x[0:LAST, BINS - 1, :], last).then_inc(loaded, 16)
            sp.dma_start(k.w0[:], k.in_w0).then_inc(loaded, 16)
            sp.dma_start(k.b0[:], k.in_b0.partition_broadcast(P)).then_inc(loaded, 16)
            sp.dma_start(k.w1[:], k.in_w1.rearrange("h f o -> (h f) o")).then_inc(loaded, 16)
            sp.dma_start(k.w1_by_f[:], k.in_w1.rearrange("h f o -> f h o")).then_inc(loaded, 16)
            sp.dma_start(k.fc[:], k.in_fc[0, :].partition_broadcast(F)).then_inc(loaded, 16)
            sp.dma_start(k.fcb[:], k.in_fcb.partition_broadcast(P)).then_inc(loaded, 16)
            sp.dma_start(k.bias1[:], k.in_bias1.partition_broadcast(P)).then_inc(loaded, 16)
            sp.dma_start(k.w3a[:], k.in_w3a.rearrange("a h -> h a")).then_inc(loaded, 16)
            sp.dma_start(k.b3a[:], k.in_b3a.rearrange("(h a) -> h a", a=1)).then_inc(loaded, 16)
            sp.dma_start(k.w3[0:HIDDEN, :], k.in_w3b).then_inc(loaded, 16)
            sp.dma_start(k.w3[HIDDEN:HIDDEN + 1, :],
                         k.in_b3b.rearrange("(a r) -> a r", a=1)).then_inc(loaded, 16)
            sp.wait_ge(loaded, 16 * 13)


def pack_edges(nc, k):
    CHUNK = COLS // 5
    with stage(nc, k) as ctx:
        attr = ctx.enter_context(nc.sbuf_tensor("attr", [P, CHUNK, 3], F32))
        square = ctx.enter_context(nc.sbuf_tensor("attr_square", [P, CHUNK, 3], F32))
        weight = ctx.enter_context(nc.sbuf_tensor("weight_chunk", [P, CHUNK], F32))
        norm = ctx.enter_context(nc.sbuf_tensor("attr_norm", [P, 2, CHUNK], F32))
        keys = [ctx.enter_context(nc.sbuf_tensor(f"keys{n}", [P, COLS], I32)) for n in range(2)]
        tail = ctx.enter_context(nc.sbuf_tensor("tail", [P, PER, BY_DST], F32))
        chunk_loaded = k.sem("chunk_loaded")
        keys_loaded = k.sem("keys_loaded")
        squares_summed = k.sem("squares_summed")
        root_taken = k.sem("root_taken")
        chunk_packed = k.sem("chunk_packed")
        own = k.sem("pack_steps")
        tail_made = k.sem("tail_made")
        tail_stored = k.sem("tail_stored")
        block = ctx.enter_context(nc.Block())
        attr_in = k.in_attr.rearrange("(p t) c -> p t c", p=P)
        weight_in = k.in_weight.rearrange("(p t) -> p t", p=P)

        @block.sync
        def _(sp):
            sp.dma_start(keys[0][:], k.in_src.rearrange("(p t) -> p t", p=P)).then_inc(keys_loaded, 16)
            sp.dma_start(keys[1][:], k.in_dst.rearrange("(p t) -> p t", p=P)).then_inc(keys_loaded, 16)
            for c in range(5):
                if c:
                    sp.wait_ge(chunk_packed, c)
                sp.dma_start(attr[:], attr_in[:, c * CHUNK:(c + 1) * CHUNK, :]).then_inc(chunk_loaded, 16)
                sp.dma_start(weight[:], weight_in[:, c * CHUNK:(c + 1) * CHUNK]).then_inc(chunk_loaded, 16)
            sp.wait_ge(tail_made, 2)
            sp.dma_start(k.edges_by_dst[EDGES:EDGES + GROUP, :].rearrange("(p j) w -> p j w", p=P),
                         tail[:]).then_inc(tail_stored, 16)
            sp.dma_start(k.edges_by_src[EDGES:EDGES + GROUP, :].rearrange("(p j) w -> p j w", p=P),
                         tail[:, :, 0:BY_SRC]).then_inc(tail_stored, 16)
            sp.wait_ge(tail_stored, 32)

        @block.gpsimd
        def _(pool):
            pool.memset(tail[:], 0.0).then_inc(tail_made, 1)
            pool.wait_ge(tail_made, 1)
            pool.memset(tail[:, :, 1], -1.0).then_inc(tail_made, 1)

        @block.scalar
        def _(act):
            for c in range(5):
                act.wait_ge(squares_summed, c + 1)
                act.activation(norm[:, 1, :], norm[:, 0, :], ACT.Sqrt).then_inc(root_taken, 1)

        @block.vector
        def _(dve):
            s = Steps(dve, own)
            dve.wait_ge(keys_loaded, 32)
            s.step(dve.tensor_copy(k.rows[:, :, 0].bitcast(I32), keys[0][:]))
            s.step(dve.tensor_copy(k.rows[:, :, 1], keys[1][:]))
            for c in range(5):
                cut = slice(c * CHUNK, (c + 1) * CHUNK)
                dve.wait_ge(chunk_loaded, 32 * (c + 1))
                s.step(dve.tensor_copy(k.rows[:, cut, 2], weight[:]))
                s.step(dve.tensor_tensor(square[:], attr[:], attr[:], ALU.mult))
                s.wait()
                dve.tensor_reduce(norm[:, 0, :], square[:], AX.X, ALU.add).then_inc(squares_summed, 1)
                dve.wait_ge(root_taken, c + 1)
                s.step(dve.reciprocal(norm[:, 0, :], norm[:, 1, :]))
                s.wait()
                inverse = norm[:, 0, :].unsqueeze(2)
                s.step(dve.tensor_tensor(k.rows[:, cut, 3:5], attr[:, :, 1:3],
                                         inverse.broadcast_to([P, CHUNK, 2]), ALU.mult))
                s.step(dve.tensor_tensor(k.rows[:, cut, 5:6], attr[:, :, 0:1], inverse, ALU.mult))
                s.step(dve.tensor_tensor(k.rows[:, cut, 6:8], attr[:, :, 1:3],
                                         inverse.broadcast_to([P, CHUNK, 2]), ALU.mult))
                s.wait()
                dve.sem_inc(chunk_packed, 1)


def pack_ends(nc, k, rows):
    with stage(nc, k) as ctx:
        keys = [ctx.enter_context(nc.sbuf_tensor(f"ends{n}", [P, COLS], I32)) for n in range(2)]
        loaded = k.sem("ends_loaded")
        packed = k.sem("ends_packed")
        block = ctx.enter_context(nc.Block())

        @block.sync
        def _(sp):
            sp.dma_start(keys[0][:], k.in_dst.rearrange("(p t) -> p t", p=P)).then_inc(loaded, 16)
            sp.dma_start(keys[1][:], k.in_src.rearrange("(p t) -> p t", p=P)).then_inc(loaded, 16)

        @block.vector
        def _(dve):
            dve.wait_ge(loaded, 32)
            dve.tensor_copy(rows[:, :, 0].bitcast(I32), keys[0][:]).then_inc(packed, 1)
            dve.tensor_copy(rows[:, :, 1], keys[1][:]).then_inc(packed, 1)
            dve.wait_ge(packed, 2)


def rank_edges(nc, k, key, name):
    with stage(nc, k) as ctx:
        def sb(n, shape, dt):
            return ctx.enter_context(nc.sbuf_tensor(f"{name}_{n}", shape, dt))

        def sem(n):
            return k.sem(f"{name}_{n}")

        place = sb("place", [P, COLS], F32)
        bins = sb("bins", [P, COLS], BF16)
        mine = sb("mine", [P, COLS], U16)
        running = sb("running", [P, COLS], F32)
        count = sb("count", [P, BINS], F32)
        total = sb("total", [P, BINS], F32)
        start = sb("start", [P, BINS], F32)
        first = sb("first", [P, BINS], F32)
        groups_i = sb("groups_i", [P, BINS], I32)
        groups = sb("groups", [P, BINS], F32)
        last_group = sb("last_group", [P, BINS], F32)
        shift = sb("shift", [P, BINS], F32)
        passed = sb("passed", [P, TCOLS, BINS - 1], F32)
        shifted = sb("shifted", [P, TCOLS, BINS - 1], F32)
        bin_of = sb("bin_of", [P, TCOLS], F32)
        start_of = sb("start_of", [P, TCOLS], F32)
        entry = sb("entry", [P, TCOLS, 2], I32)
        node_of = sb("node_of", [P, TCOLS], F32)
        sums = ctx.enter_context(nc.psum_tensor(f"{name}_sums", [P, 2, 512], F32))
        key_loaded = sem("key_loaded")
        own = sem("rank_steps")
        counted = sem("counted")
        summed = sem("summed")
        table_made = sem("table_made")
        table_stored = sem("table_stored")
        table_loaded = sem("table_loaded")
        block = ctx.enter_context(nc.Block())

        @block.vector
        def _(dve):
            s = Steps(dve, own)
            dve.wait_ge(key_loaded, 16)
            s.step(dve.tensor_scalar(k.place_i[:], k.place_i[:], P.bit_length() - 1, None,
                                     ALU.logical_shift_right))
            s.step(dve.memset(place[:], 0.0))
            s.wait()
            s.step(dve.tensor_copy(bins[:], k.place_i[:]))
            s.wait()
            with dve.Fori(0, BINS) as b:
                s.restart()
                s.step(dve.tensor_scalar(mine[:], bins[:], k.iota[:, bass.ds(b, 1)], None, ALU.is_equal))
                s.wait()
                s.step(dve.tensor_reduce(count[:, bass.ds(b, 1)], mine[:], AX.X, ALU.add))
                s.wait()
            dve.sem_inc(counted, 1)
            dve.wait_ge(summed, 1)
            s.restart()
            s.step(dve.tensor_copy(total[:], sums[:, 0, 0:BINS]))
            s.wait()
            s.step(dve.tensor_tensor_scan(start[:], k.ones[:, 0:1].broadcast_to([P, BINS]), total[:],
                                          0.0, ALU.mult, ALU.add))
            s.wait()
            s.step(dve.tensor_tensor(start[:], start[:], total[:], ALU.subtract))
            s.wait()
            s.step(dve.scalar_tensor_tensor(first[:], start[:], -1.0, sums[:, 1, 0:BINS],
                                            ALU.add, ALU.add))
            s.step(dve.tensor_scalar(groups_i[:], total[:], float(GROUP - 1), None, ALU.add))
            s.wait()
            s.step(dve.tensor_scalar(groups_i[:], groups_i[:], GROUP.bit_length() - 1, None,
                                     ALU.logical_shift_right))
            s.wait()
            s.step(dve.tensor_copy(groups[:], groups_i[:]))
            s.wait()
            s.step(dve.tensor_tensor_scan(last_group[:], k.ones[:, 0:1].broadcast_to([P, BINS]),
                                          groups[:], 0.0, ALU.mult, ALU.add))
            s.wait()
            s.step(dve.tensor_tensor(shift[:], last_group[:], groups[:], ALU.subtract))
            s.wait()
            s.step(dve.scalar_tensor_tensor(shift[:], shift[:], -float(GROUP), start[:],
                                            ALU.mult, ALU.add))
            s.wait()
            s.step(dve.tensor_tensor(groups[:, 0:BINS - 1], shift[:, 1:BINS], shift[:, 0:BINS - 1],
                                     ALU.subtract))
            s.step(dve.tensor_tensor(passed[:], spread(last_group[:, 0:BINS - 1], 1, TCOLS),
                                     spread(k.group_no[:], 2, BINS - 1), ALU.is_le))
            s.wait()
            s.step(dve.tensor_tensor(shifted[:], passed[:], spread(groups[:, 0:BINS - 1], 1, TCOLS),
                                     ALU.mult))
            s.step(dve.tensor_reduce(bin_of[:], passed[:], AX.X, ALU.add))
            s.wait()
            s.step(dve.tensor_reduce(start_of[:], shifted[:], AX.X, ALU.add))
            s.wait()
            s.step(dve.scalar_tensor_tensor(start_of[:], k.group_no[:], float(GROUP), start_of[:],
                                            ALU.mult, ALU.add))
            s.wait()
            s.step(dve.tensor_scalar(entry[:, :, 0], start_of[:], float(EDGES), None, ALU.min))
            s.step(dve.tensor_copy(entry[:, :, 1], bin_of[:]))
            s.step(dve.tensor_scalar(node_of[:], bin_of[:], float(P), None, ALU.mult))
            s.wait()
            dve.sem_inc(table_made, 1)
            with dve.Fori(0, BINS) as b:
                s.restart()
                s.step(dve.tensor_scalar(mine[:], bins[:], k.iota[:, bass.ds(b, 1)], None, ALU.is_equal))
                s.wait()
                s.step(dve.tensor_tensor_scan(running[:], k.ones[:, 0:1].broadcast_to([P, COLS]), mine[:],
                                              first[:, bass.ds(b, 1)], ALU.mult, ALU.add))
                s.wait()
                s.step(dve.copy_predicated(place[:], mine[:], running[:]))
                s.wait()
            s.restart()
            s.step(dve.tensor_copy(k.place_i[:], place[:]))
            s.wait()

        @block.tensor
        def _(pe):
            pe.wait_ge(counted, 1)
            pe.matmul(sums[:, 0, 0:BINS], k.ones[:], count[:], start=True, stop=True)
            pe.matmul(sums[:, 1, 0:BINS], k.before[:], count[:], start=True, stop=True).then_inc(summed, 1)

        @block.sync
        def _(sp):
            sp.dma_start(k.place_i[:], key.rearrange("(p t) -> p t", p=P)).then_inc(key_loaded, 16)
            sp.wait_ge(table_made, 1)
            sp.dma_start(k.entry_dram[:, :].rearrange("(p c) e -> p c e", p=P), entry[:]).then_inc(table_stored, 16)
            sp.dma_start(k.node_dram[:].rearrange("(p c) -> p c", p=P), node_of[:]).then_inc(table_stored, 16)
            sp.wait_ge(table_stored, 32)
            sp.dma_start(k.entry[name][0:1, :, :], k.entry_dram.unsqueeze(0)).then_inc(table_loaded, 16)
            sp.dma_start(k.first_node[name][:], k.node_dram.partition_broadcast(P)).then_inc(table_loaded, 16)
            sp.wait_ge(table_loaded, 32)


def scatter_edges(nc, k, rows, width, table, name):
    RUN = 25
    HALF = [13, 12]
    AT = [0, 13]
    ROUNDS = COLS // RUN
    with stage(nc, k) as ctx:
        index = [ctx.enter_context(nc.sbuf_tensor(f"{name}_index{s}", [P, HALF[s]], I32)) for s in range(2)]
        row = [ctx.enter_context(nc.sbuf_tensor(f"{name}_row{s}", [P, HALF[s], width], F32)) for s in range(2)]
        staged = [k.sem(f"{name}_staged{s}") for s in range(2)]
        written = [k.sem(f"{name}_written{s}") for s in range(2)]
        block = ctx.enter_context(nc.Block())

        @block.sync
        def _(sp):
            def stage(i, s):
                at = i * RUN + AT[s]
                sp.dma_start(index[s][:], k.place_i[:, bass.ds(at, HALF[s])]).then_inc(staged[s], 16)
                sp.dma_start(row[s][:], rows[:, bass.ds(at, HALF[s]), :]).then_inc(staged[s], 16)

            stage(0, 0)
            stage(0, 1)
            with sp.Fori(0, ROUNDS - 1) as i:
                for s in range(2):
                    sp.wait_ge(written[s], (i + 1) * (16 * HALF[s]))
                    stage(i + 1, s)

        @block.gpsimd
        def _(pool):
            with pool.Fori(0, ROUNDS):
                for s in range(2):
                    pool.wait_ge(staged[s], 32)
                    pool.sem_clear(staged[s])
                    for j in range(HALF[s]):
                        pool.indirect_dma_start(
                            table, bass.IndirectOffsetOnAxis(ap=index[s][:, j:j + 1], axis=0),
                            row[s][:, j, :], None).then_inc(written[s], 16)
            for s in range(2):
                pool.wait_ge(written[s], 16 * HALF[s] * ROUNDS)


def sum_messages(nc, k, table, first):
    width = F + 1 if first else F
    name = "weighted" if first else f"hop_{k.hops}"
    k.hops += 1
    with stage(nc, k) as ctx:
        def sb(n, shape, dt):
            return [ctx.enter_context(nc.sbuf_tensor(f"{name}_{n}{s}", shape, dt)) for s in range(SLOTS)]

        def sem(n):
            return [k.sem(f"{name}_{n}{s}") for s in range(SLOTS)]

        rows = sb("rows", [P, PER, BY_DST], F32)
        far = sb("far", [P, PER, F], F32)
        hot = sb("hot", [P, PER, P], F32)
        local = sb("local", [P, PER], F32)
        message = sb("message", [P, PER, width], F32) if first else far
        weight = sb("weight", [P, PER], F32) if first else None
        part = [ctx.enter_context(nc.psum_tensor(f"{name}_part{s}", [P, 512], F32)) for s in range(SLOTS)]
        rows_in = sem("rows_in")
        rows_free = sem("rows_free")
        gathered = sem("gathered")
        far_free = sem("far_free")
        message_ready = sem("message_ready")
        message_free = sem("message_free")
        part_ready = sem("part_ready")
        part_free = sem("part_free")
        weight_saved = k.sem(f"{name}_weight_saved")
        weight_cut = k.sem(f"{name}_weight_cut")
        own = k.sem(f"{name}_vector_steps")
        added = k.sem(f"{name}_added")
        cleared = k.sem(f"{name}_cleared")
        block = ctx.enter_context(nc.Block())
        entry, first_node = k.entry["by_dst"], k.first_node["by_dst"]
        readers = 2 if first else 1

        @block.sync
        def _(sp):
            for s in range(SLOTS):
                sp.sem_inc(rows_free[s], readers)
            with sp.Fori(0, TURNS) as i:
                for s in range(SLOTS):
                    at = sp.value_load(entry[0:1, bass.ds(i * SLOTS + s, 1), 0], min_val=0, max_val=EDGES)
                    sp.wait_ge(rows_free[s], readers)
                    sp.sem_clear(rows_free[s])
                    sp.dma_start(rows[s][:], k.edges_by_dst[bass.ds(at, GROUP), :].rearrange(
                        "(p j) w -> p j w", p=P)).then_inc(rows_in[s], 16)

        @block.gpsimd
        def _(pool):
            for s in range(SLOTS):
                pool.sem_inc(far_free[s], 1)
            with pool.Fori(0, TURNS):
                for s in range(SLOTS):
                    pool.wait_ge(rows_in[s], 16)
                    pool.sem_clear(rows_in[s])
                    pool.wait_ge(far_free[s], 1)
                    pool.sem_clear(far_free[s])
                    for j in range(PER):
                        pool.indirect_dma_start(
                            far[s][:, j, :], None, table,
                            bass.IndirectOffsetOnAxis(ap=rows[s][:, j, 0:1].bitcast(I32), axis=0)
                        ).then_inc(gathered[s], 16)

        @block.vector
        def _(dve):
            own_steps = Steps(dve, own)
            dve.memset(k.sums[:], 0.0).then_inc(cleared, 1)
            if first:
                for s in range(SLOTS):
                    dve.memset(message[s][:], 1.0).then_inc(cleared, 1)
                dve.wait_ge(cleared, 1 + SLOTS)
            else:
                dve.wait_ge(cleared, 1)
            for s in range(SLOTS):
                dve.sem_inc(part_free[s], 1)
                dve.sem_inc(message_free[s], 1)

            def select(i, s):
                own_steps.restart()
                dve.wait_ge(gathered[s], (i + 1) * (16 * PER))
                dve.wait_ge(message_free[s], i + 1)
                own_steps.step(dve.tensor_scalar(local[s][:], rows[s][:, :, 1],
                                                 first_node[:, bass.ds(i * SLOTS + s, 1)], None,
                                                 ALU.subtract))
                if first:
                    own_steps.step(dve.tensor_tensor(message[s][:, :, 0:F], far[s][:],
                                                     spread(rows[s][:, :, 2], 2, F), ALU.mult))
                own_steps.wait(1)
                own_steps.step(dve.tensor_tensor(hot[s][:], spread(k.iota[:], 1, PER),
                                                 spread(local[s][:], 2, P), ALU.is_equal))
                own_steps.wait()
                dve.sem_inc(message_ready[s], 1)
                dve.sem_inc(rows_free[s], 1)
                if first:
                    dve.sem_inc(far_free[s], 1)

            def accumulate(i, s):
                at = dve.value_load(entry[0:1, bass.ds(i * SLOTS + s, 1), 1], min_val=0, max_val=BINS - 1)
                dve.wait_ge(part_ready[s], i + 1)
                if s:
                    dve.wait_ge(added, s)
                sums = k.sums[:, bass.ds(at * (F + 1), width)]
                dve.tensor_tensor(sums, sums, part[s][:, 0:width], ALU.add).then_inc(added, 1)
                dve.wait_ge(added, s + 1)
                dve.sem_inc(part_free[s], 1)

            with dve.Fori(0, TURNS) as i:
                dve.sem_clear(added)
                for s in range(SLOTS):
                    select(i, s)
                    if s:
                        accumulate(i, s - 1)
                accumulate(i, SLOTS - 1)

        @block.tensor
        def _(pe):
            with pe.Fori(0, TURNS) as i:
                for s in range(SLOTS):
                    pe.wait_ge(message_ready[s], i + 1)
                    if not first:
                        pe.wait_ge(gathered[s], (i + 1) * (16 * PER))
                    pe.wait_ge(part_free[s], i + 1)
                    for j in range(PER):
                        last = pe.matmul(part[s][:, 0:width], hot[s][:, j, :], message[s][:, j, :],
                                         start=(j == 0), stop=(j == PER - 1))
                    last.then_inc(part_ready[s], 1)
                    pe.wait_ge(part_ready[s], i + 1)
                    pe.sem_inc(message_free[s], 1)
                    if not first:
                        pe.sem_inc(far_free[s], 1)

        @block.scalar
        def _(act):
            if not first:
                return
            with act.Fori(0, TURNS) as i:
                act.sem_clear(weight_cut)
                for s in range(SLOTS):
                    act.wait_ge(gathered[s], (i + 1) * (16 * PER))
                    act.copy(weight[s][:], rows[s][:, :, 2]).then_inc(weight_cut, 1)
                    act.wait_ge(weight_cut, s + 1)
                    act.sem_inc(rows_free[s], 1)
                    act.dma_start(k.weight_by_group[bass.ds(i * SLOTS + s, 1), :].rearrange(
                        "g (p j) -> (g p) j", p=P), weight[s][:]).then_inc(weight_saved, 16)
                act.wait_ge(weight_saved, (i + 1) * (16 * SLOTS))


def project(nc, k, name, source, depth, weights, width, finish):
    with stage(nc, k) as ctx:
        def sem(n):
            return k.sem(f"{name}_{n}")

        staged = ctx.enter_context(nc.sbuf_tensor(f"{name}_staged", [P, BATCH, depth], F32))
        turned = ctx.enter_context(nc.sbuf_tensor(f"{name}_turned", [depth, BATCH, P], F32))
        turned_ps = ctx.enter_context(nc.psum_tensor(f"{name}_turned_ps", [P, 8 * P], F32))
        out = ctx.enter_context(nc.psum_tensor(f"{name}_out", [P, 512], F32))
        rows_staged, rows_turned, copied, multiplied = sem("rows_staged"), sem("rows_turned"), sem("copied"), sem("multiplied")
        own = sem("steps")
        block = ctx.enter_context(nc.Block())

        @block.vector
        def _(dve):
            s = Steps(dve, own)
            with dve.Fori(0, BINS // BATCH) as i:
                s.restart()
                source(dve, s, i, staged)
                s.wait()
                dve.sem_inc(rows_staged, 1)
                dve.wait_ge(multiplied, i + 1)
                finish(dve, s, i, out[:, 0:BATCH * width].rearrange("p (b w) -> p b w", b=BATCH))
                s.wait()

        @block.tensor
        def _(pe):
            with pe.Fori(0, BINS // BATCH) as i:
                pe.wait_ge(rows_staged, i + 1)
                for b in range(BATCH):
                    last = pe.transpose(turned_ps[0:depth, b * P:(b + 1) * P], staged[:, b, :], k.ident[:])
                last.then_inc(rows_turned, 1)
                pe.wait_ge(copied, i + 1)
                for b in range(BATCH):
                    last = pe.matmul(out[:, b * width:(b + 1) * width], turned[:, b, :], weights,
                                     start=True, stop=True)
                last.then_inc(multiplied, 1)

        @block.scalar
        def _(act):
            with act.Fori(0, BINS // BATCH) as i:
                act.wait_ge(rows_turned, i + 1)
                act.copy(turned[:].rearrange("f b p -> f (b p)"),
                         turned_ps[0:depth, 0:BATCH * P]).then_inc(copied, 1)


def normalize(nc, k, name, before=None, after=None, store=()):
    with stage(nc, k) as ctx:
        centred = ctx.enter_context(nc.sbuf_tensor(f"{name}_centred", [P, BINS, F], F32))
        square = ctx.enter_context(nc.sbuf_tensor(f"{name}_square", [P, BINS, F], F32))
        mean = ctx.enter_context(nc.sbuf_tensor(f"{name}_mean", [P, BINS], F32))
        spread_of = ctx.enter_context(nc.sbuf_tensor(f"{name}_spread", [P, BINS], F32))
        own = k.sem(f"{name}_steps")
        variance_ready = k.sem(f"{name}_variance_ready")
        deviation_ready = k.sem(f"{name}_deviation_ready")
        ready = k.sem(f"{name}_rows_ready")
        stored = k.sem(f"{name}_rows_stored")
        block = ctx.enter_context(nc.Block())

        @block.vector
        def _(dve):
            s = Steps(dve, own)
            if before:
                before(dve, s)
            s.step(dve.tensor_reduce(mean[:], k.x[:], AX.X, ALU.add))
            s.wait()
            s.step(dve.tensor_scalar(mean[:], mean[:], 1.0 / F, None, ALU.mult))
            s.wait()
            s.step(dve.tensor_tensor(centred[:], k.x[:], spread(mean[:], 2, F), ALU.subtract))
            s.wait()
            s.step(dve.tensor_tensor(square[:], centred[:], centred[:], ALU.mult))
            s.wait()
            dve.tensor_reduce(spread_of[:], square[:], AX.X, ALU.add).then_inc(variance_ready, 1)
            dve.wait_ge(deviation_ready, 1)
            s.step(dve.reciprocal(spread_of[:], mean[:]))
            s.wait()
            s.step(dve.tensor_tensor(k.x[:], centred[:], spread(spread_of[:], 2, F), ALU.mult))
            s.wait()
            if after:
                after(dve, s)
                s.wait()
            dve.sem_inc(ready, 1)

        @block.scalar
        def _(act):
            act.wait_ge(variance_ready, 1)
            act.activation(mean[:], spread_of[:], ACT.Sqrt, bias=k.eps[:], scale=1.0 / F).then_inc(deviation_ready, 1)

        @block.sync
        def _(sp):
            sp.wait_ge(ready, 1)
            for n, (table, rows) in enumerate(store):
                whole, last = node_rows(table)
                sp.dma_start(whole, rows[:, 0:BINS - 1, :]).then_inc(stored, 16)
                sp.dma_start(last, rows[0:LAST, BINS - 1, :]).then_inc(stored, 16)
            if store:
                sp.wait_ge(stored, 32 * len(store))


def first_update(nc, k):
    sums = k.sums[:].rearrange("p (b w) -> p b w", w=F + 1)

    def source(dve, s, i, staged):
        s.step(dve.tensor_copy(staged[:], sums[:, bass.ds(i * BATCH, BATCH), 0:F]))

    def finish(dve, s, i, out):
        x = k.x[:, bass.ds(i * BATCH, BATCH), :]
        s.step(dve.tensor_tensor(k.update[:], out, spread(k.b0[:], 1, BATCH), ALU.add))
        s.wait()
        s.step(dve.tensor_scalar(k.update[:], k.update[:], 0.0, None, ALU.max))
        s.wait()
        s.step(dve.tensor_tensor(x, x, k.update[:], ALU.add))

    project(nc, k, "dense", source, F, k.w0[:], F, finish)

    def after(dve, s):
        s.step(dve.tensor_copy(k.degree[:], sums[:, :, F]))
        s.step(dve.tensor_copy(k.far_rows[:, :, 0:F], k.x[:]))
        for half in range(2):
            s.step(dve.tensor_tensor(k.scorer_parts[:], k.w1_by_f[:],
                                     spread(k.fc[:, half * F:(half + 1) * F], 1, HEADS), ALU.mult))
            s.wait()
            s.step(dve.tensor_reduce(k.scorer[:, half * HEADS:(half + 1) * HEADS], k.scorer_parts[:],
                                     AX.X, ALU.add))
            s.wait()
        s.step(dve.memset(k.far_rows[:, :, F:FAR], 1.0))

    normalize(nc, k, "norm0", after=after)

    def scores_source(dve, s, i, staged):
        s.step(dve.tensor_copy(staged[:], k.x[:, bass.ds(i * BATCH, BATCH), :]))

    def scores_finish(dve, s, i, out):
        s.step(dve.tensor_scalar(k.own_score[:, bass.ds(i * BATCH, BATCH), :], out[:, :, 0:HEADS],
                                 k.fcb[:], None, ALU.add))
        s.step(dve.tensor_copy(k.far_rows[:, bass.ds(i * BATCH, BATCH), F + 1:F + 1 + HEADS],
                               out[:, :, HEADS:2 * HEADS]))

    project(nc, k, "scores", scores_source, F, k.scorer[:], 2 * HEADS, scores_finish)
    with stage(nc, k) as ctx:
        stored = k.sem("far_rows_stored")
        block = ctx.enter_context(nc.Block())

        @block.sync
        def _(sp):
            whole, last = node_rows(k.far_dram)
            sp.dma_start(whole, k.far_rows[:, 0:BINS - 1, :]).then_inc(stored, 16)
            sp.dma_start(last, k.far_rows[0:LAST, BINS - 1, :]).then_inc(stored, 16)
            sp.wait_ge(stored, 32)


def attend(nc, k):
    W = F + 1
    with stage(nc, k) as ctx:
        def sb(n, shape, dt, count):
            return [ctx.enter_context(nc.sbuf_tensor(f"att_{n}{s}", shape, dt)) for s in range(count)]

        def sem(n, count):
            return [k.sem(f"att_{n}{s}") for s in range(count)]

        rows = sb("rows", [P, PER, BY_SRC], F32, SLOTS)
        far = sb("far", [P, PER, FAR], F32, SLOTS)
        hot = sb("hot", [P, PER, P], F32, 2)
        absent = sb("absent", [P, PER, P], F32, 2)
        masked = sb("masked", [P, PER, HEADS, P], F32, 2)
        hot_turned = sb("hot_turned", [P, PER * P], F32, 2)
        local = sb("local", [P, PER], F32, 2)
        top = sb("top", [P, 4, HEADS], F32, 2)
        node_terms = sb("node_terms", [P, 2 * HEADS], F32, 2)
        rescale = sb("rescale", [P, HEADS], F32, 2)
        score = sb("score", [P, 2, PER, HEADS], F32, 2)
        share = sb("share", [P, PER, HEADS], F32, 2)
        message = sb("message", [P, PER, HEADS * W], F32, 2)
        scaled = ctx.enter_context(nc.sbuf_tensor("att_scaled", [P, HEADS, W], F32))
        masked_ps = ctx.enter_context(nc.psum_tensor("att_masked_ps", [P, HEADS, PER * P], F32))
        hot_ps = ctx.enter_context(nc.psum_tensor("att_hot_ps", [P, PER * P], F32))
        terms_ps = ctx.enter_context(nc.psum_tensor("att_terms_ps", [P, PER, P], F32))
        part = [ctx.enter_context(nc.psum_tensor(f"att_part{s}", [P, 512], F32)) for s in range(2)]
        rows_in, rows_free = sem("rows_in", SLOTS), sem("rows_free", SLOTS)
        gathered, far_free = sem("gathered", SLOTS), sem("far_free", SLOTS)
        hot_ready, absent_ready = sem("hot_ready", 2), sem("absent_ready", 2)
        masked_ready, masked_turned = sem("masked_ready", 2), sem("masked_turned", 2)
        maximum_taken = sem("maximum_taken", 1)[0]
        hot_in_psum, hot_copied = sem("hot_in_psum", 2), sem("hot_copied", 2)
        terms_ready, terms_spread = sem("terms_ready", 2), sem("terms_spread", 2)
        terms_read = sem("terms_read", 1)[0]
        score_ready, share_ready = sem("score_ready", 2), sem("share_ready", 2)
        message_ready, part_ready, part_free = sem("message_ready", 2), sem("part_ready", 2), sem("part_free", 2)
        own = sem("vector_steps", 1)[0]
        cleared = sem("cleared", 1)[0]
        block = ctx.enter_context(nc.Block())
        entry, first_node = k.entry["by_src"], k.first_node["by_src"]

        @block.sync
        def _(sp):
            for s in range(SLOTS):
                sp.sem_inc(rows_free[s], 1)
            with sp.Fori(0, TURNS) as i:
                for s in range(SLOTS):
                    at = sp.value_load(entry[0:1, bass.ds(i * SLOTS + s, 1), 0], min_val=0, max_val=EDGES)
                    sp.wait_ge(rows_free[s], 1)
                    sp.sem_clear(rows_free[s])
                    sp.dma_start(rows[s][:], k.edges_by_src[bass.ds(at, GROUP), :].rearrange(
                        "(p j) w -> p j w", p=P)).then_inc(rows_in[s], 16)

        @block.gpsimd
        def _(pool):
            for s in range(SLOTS):
                pool.sem_inc(far_free[s], 1)
            with pool.Fori(0, TURNS):
                for s in range(SLOTS):
                    pool.wait_ge(rows_in[s], 16)
                    pool.sem_clear(rows_in[s])
                    pool.wait_ge(far_free[s], 1)
                    pool.sem_clear(far_free[s])
                    for j in range(PER):
                        pool.indirect_dma_start(
                            far[s][:, j, :], None, k.far_dram,
                            bass.IndirectOffsetOnAxis(ap=rows[s][:, j, 0:1].bitcast(I32), axis=0)
                        ).then_inc(gathered[s], 16)

        @block.vector
        def _(dve):
            own_steps = Steps(dve, own)
            dve.memset(k.attention[:], 0.0).then_inc(cleared, 1)
            dve.memset(k.maximum[:], -BIG).then_inc(cleared, 1)
            dve.wait_ge(cleared, 2)
            for c in range(2):
                dve.sem_inc(part_free[c], 1)

            def select(i, s):
                c = s % 2
                own_steps.restart()
                dve.wait_ge(gathered[s], (i + 1) * (16 * PER))
                own_steps.step(dve.tensor_scalar(local[c][:], rows[s][:, :, 1],
                                                 first_node[:, bass.ds(i * SLOTS + s, 1)], None,
                                                 ALU.subtract))
                own_steps.wait()
                own_steps.step(dve.tensor_tensor(hot[c][:], spread(k.iota[:], 1, PER),
                                                 spread(local[c][:], 2, P), ALU.is_equal))
                own_steps.wait()
                dve.sem_inc(hot_ready[c], 1)
                dve.sem_inc(rows_free[s], 1)

            def mask(i, s):
                c = s % 2
                dve.wait_ge(absent_ready[c], turn(i, s, 2))
                dve.tensor_tensor(masked[c][:], spread(absent[c][:], 2, HEADS),
                                  spread(far[s][:, :, W:W + HEADS], 3, P), ALU.add).then_inc(masked_ready[c], 1)

            def raise_maximum(i, s, at):
                c = s % 2
                own_steps.restart()
                own_score = k.own_score[:].rearrange("p b h -> p (b h)")[:, bass.ds(at * HEADS, HEADS)]
                maximum = k.maximum[:, bass.ds(at * HEADS, HEADS)]
                dve.wait_ge(masked_turned[c], turn(i, s, 2))
                own_steps.step(dve.tensor_reduce(top[c][:, 0, :], masked_ps[:], AX.X, ALU.max))
                own_steps.step(dve.tensor_copy(node_terms[c][:, 0:HEADS], own_score))
                own_steps.wait()
                dve.sem_inc(maximum_taken, 1)
                own_steps.step(dve.tensor_tensor(top[c][:, 1, :], top[c][:, 0, :], own_score, ALU.add))
                own_steps.wait()
                own_steps.step(dve.scalar_tensor_tensor(top[c][:, 2, :], top[c][:, 1, :], 0.2, top[c][:, 1, :],
                                                        ALU.mult, ALU.max))
                own_steps.wait()
                own_steps.step(dve.tensor_tensor(node_terms[c][:, HEADS:2 * HEADS], top[c][:, 2, :], maximum,
                                                 ALU.max))
                own_steps.wait()
                own_steps.step(dve.tensor_tensor(top[c][:, 3, :], maximum, node_terms[c][:, HEADS:2 * HEADS],
                                                 ALU.subtract))
                own_steps.wait()
                own_steps.step(dve.tensor_copy(maximum, node_terms[c][:, HEADS:2 * HEADS]))
                own_steps.wait()
                dve.sem_inc(terms_ready[c], 1)

            def edge_scores(i, s):
                c = s % 2
                own_steps.restart()
                dve.wait_ge(terms_spread[c], turn(i, s, 2))
                own_steps.step(dve.tensor_tensor(score[c][:, 0], terms_ps[:, :, 0:HEADS],
                                                 far[s][:, :, W:W + HEADS], ALU.add))
                own_steps.wait()
                own_steps.step(dve.scalar_tensor_tensor(score[c][:, 1], score[c][:, 0], 0.2, score[c][:, 0],
                                                        ALU.mult, ALU.max))
                own_steps.wait()
                own_steps.step(dve.tensor_tensor(score[c][:, 0], score[c][:, 1],
                                                 terms_ps[:, :, HEADS:2 * HEADS], ALU.subtract))
                own_steps.wait()
                dve.sem_inc(terms_read, 1)
                own_steps.step(dve.tensor_scalar(score[c][:, 1], score[c][:, 0], 0.0, None, ALU.min))
                own_steps.wait()
                dve.sem_inc(score_ready[c], 1)

            def messages(i, s):
                c = s % 2
                own_steps.restart()
                dve.wait_ge(share_ready[c], turn(i, s, 2))
                own_steps.step(dve.tensor_tensor(
                    message[c][:].rearrange("p j (h w) -> p j h w", h=HEADS),
                    spread(far[s][:, :, 0:W], 2, HEADS), spread(share[c][:], 3, W), ALU.mult))
                own_steps.wait()
                dve.sem_inc(message_ready[c], 1)
                dve.sem_inc(far_free[s], 1)

            def accumulate(i, s, at):
                c = s % 2
                own_steps.restart()
                sums = k.attention[:, bass.ds(at * (HEADS * W), HEADS * W)]
                own_steps.step(dve.tensor_tensor(scaled[:], sums.rearrange("p (h w) -> p h w", h=HEADS),
                                                 spread(rescale[c][:], 2, W), ALU.mult))
                dve.wait_ge(part_ready[c], turn(i, s, 2))
                own_steps.wait()
                own_steps.step(dve.tensor_tensor(sums, scaled[:].rearrange("p h w -> p (h w)"),
                                                 part[c][:, 0:HEADS * W], ALU.add))
                own_steps.wait()
                dve.sem_inc(part_free[c], 1)

            with dve.Fori(0, TURNS) as i:
                for s in range(0, SLOTS, 2):
                    at = [dve.value_load(entry[0:1, bass.ds(i * SLOTS + s + d, 1), 1],
                                         min_val=0, max_val=BINS - 1) for d in range(2)]
                    select(i, s)
                    select(i, s + 1)
                    mask(i, s)
                    mask(i, s + 1)
                    raise_maximum(i, s, at[0])
                    raise_maximum(i, s + 1, at[1])
                    edge_scores(i, s)
                    edge_scores(i, s + 1)
                    messages(i, s)
                    messages(i, s + 1)
                    accumulate(i, s, at[0])
                    accumulate(i, s + 1, at[1])

        @block.tensor
        def _(pe):
            for once in range(1):
                pe.sem_inc(maximum_taken, 1)
                pe.sem_inc(terms_read, 1)

            def turn_hot(i, s):
                c = s % 2
                pe.wait_ge(hot_ready[c], turn(i, s, 2))
                if s:
                    pe.wait_ge(hot_copied[(s - 1) % 2], turn(i, s - 1, 2))
                for j in range(PER):
                    last = pe.transpose(hot_ps[:, j * P:(j + 1) * P], hot[c][:, j, :], k.ident[:])
                last.then_inc(hot_in_psum[c], 1)

            def turn_masked(i, s):
                c = s % 2
                pe.wait_ge(masked_ready[c], turn(i, s, 2))
                pe.wait_ge(maximum_taken, i * SLOTS + s + 1)
                for h in range(HEADS):
                    for j in range(PER):
                        last = pe.transpose(masked_ps[:, h, j * P:(j + 1) * P], masked[c][:, j, h, :],
                                            k.ident[:])
                last.then_inc(masked_turned[c], 1)

            def spread_terms(i, s):
                c = s % 2
                pe.wait_ge(terms_ready[c], turn(i, s, 2))
                pe.wait_ge(hot_copied[c], turn(i, s, 2))
                pe.wait_ge(terms_read, i * SLOTS + s + 1)
                for j in range(PER):
                    last = pe.matmul(terms_ps[:, j, 0:2 * HEADS], hot_turned[c][:, j * P:(j + 1) * P],
                                     node_terms[c][:], start=True, stop=True)
                last.then_inc(terms_spread[c], 1)

            def sum_nodes(i, s):
                c = s % 2
                pe.wait_ge(message_ready[c], turn(i, s, 2))
                pe.wait_ge(part_free[c], turn(i, s, 2))
                for j in range(PER):
                    last = pe.matmul(part[c][:, 0:HEADS * W], hot[c][:, j, :], message[c][:, j, :],
                                     start=(j == 0), stop=(j == PER - 1))
                last.then_inc(part_ready[c], 1)

            with pe.Fori(0, TURNS) as i:
                for s in range(0, SLOTS, 2):
                    turn_hot(i, s)
                    turn_hot(i, s + 1)
                    turn_masked(i, s)
                    turn_masked(i, s + 1)
                    spread_terms(i, s)
                    spread_terms(i, s + 1)
                    sum_nodes(i, s)
                    sum_nodes(i, s + 1)

        @block.scalar
        def _(act):
            def hide(i, s):
                c = s % 2
                act.wait_ge(hot_ready[c], turn(i, s, 2))
                act.activation(absent[c][:], hot[c][:], ACT.Copy, bias=-BIG, scale=BIG).then_inc(absent_ready[c], 1)

            def copy_hot(i, s):
                c = s % 2
                act.wait_ge(hot_in_psum[c], turn(i, s, 2))
                act.copy(hot_turned[c][:], hot_ps[:]).then_inc(hot_copied[c], 1)

            def exponents(i, s):
                c = s % 2
                act.wait_ge(terms_ready[c], turn(i, s, 2))
                act.activation(rescale[c][:], top[c][:, 3, :], ACT.Exp)
                act.wait_ge(score_ready[c], turn(i, s, 2))
                act.activation(share[c][:], score[c][:, 1], ACT.Exp).then_inc(share_ready[c], 1)

            with act.Fori(0, TURNS) as i:
                for s in range(0, SLOTS, 2):
                    hide(i, s)
                    hide(i, s + 1)
                    copy_hot(i, s)
                    copy_hot(i, s + 1)
                    exponents(i, s)
                    exponents(i, s + 1)


def attention_update(nc, k):
    W = F + 1
    sums = k.attention[:].rearrange("p (b h w) -> p b h w", h=HEADS, w=W)

    def source(dve, s, i, staged):
        part = sums[:, bass.ds(i * BATCH, BATCH), :, :]
        s.step(dve.tensor_scalar(k.denominator[:], part[:, :, :, F], 1e-30, float(HEADS), ALU.max, ALU.mult))
        s.wait()
        s.step(dve.reciprocal(k.share[:], k.denominator[:]))
        s.wait()
        for h in range(HEADS):
            s.step(dve.tensor_tensor(staged[:, :, h * F:(h + 1) * F], part[:, :, h, 0:F],
                                     k.share[:, :, h:h + 1].broadcast_to([P, BATCH, F]), ALU.mult))

    def finish(dve, s, i, out):
        x = k.x[:, bass.ds(i * BATCH, BATCH), :]
        s.step(dve.tensor_tensor(k.update[:], out, spread(k.bias1[:], 1, BATCH), ALU.add))
        s.wait()
        s.step(dve.tensor_tensor(x, x, k.update[:], ALU.add))

    project(nc, k, "heads", source, HEADS * F, k.w1[:], F, finish)

    with stage(nc, k) as ctx:
        degree_ready, root_ready, inverse_ready = (k.sem(n) for n in ("degree_ready", "root_ready", "inverse_ready"))
        block = ctx.enter_context(nc.Block())

        @block.vector
        def _(dve):
            dve.tensor_scalar(k.degree[:], k.degree[:], 1.0, None, ALU.add).then_inc(degree_ready, 1)
            dve.wait_ge(root_ready, 1)
            dve.reciprocal(k.inverse[:], k.degree_root[:]).then_inc(inverse_ready, 1)
            dve.wait_ge(inverse_ready, 1)

        @block.scalar
        def _(act):
            act.wait_ge(degree_ready, 1)
            act.activation(k.degree_root[:], k.degree[:], ACT.Sqrt).then_inc(root_ready, 1)

    def after(dve, s):
        s.step(dve.scalar_tensor_tensor(k.hop_rows[:], k.x[:], 0.0, spread(k.inverse[:], 2, F),
                                        ALU.max, ALU.mult))

    normalize(nc, k, "norm1", after=after, store=[(k.hop_dram[0], k.hop_rows)])


def between_hops(nc, k):
    sums = k.sums[:].rearrange("p (b w) -> p b w", w=F + 1)[:, :, 0:F]
    with stage(nc, k) as ctx:
        own, ready, stored = (k.sem(n) for n in ("hop_steps", "hop_rows_ready", "hop_rows_stored"))
        block = ctx.enter_context(nc.Block())

        @block.vector
        def _(dve):
            s = Steps(dve, own)
            s.step(dve.tensor_tensor(k.hop_rows[:], k.hop_rows[:], sums, ALU.add))
            for _ in range(2):
                s.wait()
                s.step(dve.tensor_tensor(k.hop_rows[:], k.hop_rows[:], spread(k.inverse[:], 2, F), ALU.mult))
            s.wait()
            dve.sem_inc(ready, 1)

        @block.sync
        def _(sp):
            sp.wait_ge(ready, 1)
            whole, last = node_rows(k.hop_dram[1])
            sp.dma_start(whole, k.hop_rows[:, 0:BINS - 1, :]).then_inc(stored, 16)
            sp.dma_start(last, k.hop_rows[0:LAST, BINS - 1, :]).then_inc(stored, 16)
            sp.wait_ge(stored, 32)


def after_hops(nc, k):
    sums = k.sums[:].rearrange("p (b w) -> p b w", w=F + 1)[:, :, 0:F]

    def before(dve, s):
        s.step(dve.tensor_tensor(k.hop_rows[:], k.hop_rows[:], sums, ALU.add))
        s.wait()
        s.step(dve.tensor_tensor(k.hop_rows[:], k.hop_rows[:], spread(k.inverse[:], 2, F), ALU.mult))
        s.wait()
        s.step(dve.tensor_tensor(k.x[:], k.x[:], k.hop_rows[:], ALU.add))
        s.wait()

    normalize(nc, k, "norm2", before=before, store=[(k.hop_dram[0], k.x)])


def radial_weights(nc, k):
    scalar_norm = sqrt(4 * pi) / sqrt(2 * MUL)
    vector_norm = sqrt(4 * pi) * sqrt(3.0) / sqrt(4 * MUL)
    flat = 0.5 / sqrt(pi)
    same = flat / sqrt(3.0)
    cross = sqrt(3.0 / (4 * pi)) / sqrt(6.0)
    tensor = sqrt(3.0 / (8 * pi))
    H1 = HIDDEN + 1
    with stage(nc, k) as ctx:
        own = k.sem("radial_steps")
        block = ctx.enter_context(nc.Block())

        @block.vector
        def _(dve):
            s = Steps(dve, own)
            a = k.radial[:, 0:256].rearrange("h (q m) -> h q m", m=2 * MUL)
            b = k.radial[:, 256:384].rearrange("h (q v) -> h q v", v=MUL)

            def paths(n):
                return k.w3[:, n * 64:(n + 1) * 64].rearrange("h (u v) -> h u v", v=MUL)

            vector_paths = k.w3[:, 192:384].rearrange("h (u v l) -> h u v l", v=MUL, l=3)
            for out, of, scale in (
                    (a[:, 0:8, 0:8], paths(0), scalar_norm * flat),
                    (a[:, 0:8, 8:16], paths(1), scalar_norm * flat),
                    (a[:, 8:16, 0:8], paths(2), vector_norm * flat),
                    (a[:, 8:16, 8:16], vector_paths[:, :, :, 2], vector_norm * tensor),
                    (b[:, 0:8, :], vector_paths[:, :, :, 0], vector_norm * same),
                    (b[:, 8:16, :], vector_paths[:, :, :, 1], vector_norm * cross)):
                s.step(dve.tensor_scalar(out, of, scale, None, ALU.mult))
            s.wait()
            s.step(dve.scalar_tensor_tensor(b[:, 0:8, :], vector_paths[:, :, :, 2],
                                            -vector_norm * tensor / 3, b[:, 0:8, :], ALU.mult, ALU.add))
            s.wait()


def convolve(nc, k):
    with stage(nc, k) as ctx:
        def sb(n, shape, count):
            return [ctx.enter_context(nc.sbuf_tensor(f"conv_{n}{s}", shape, F32)) for s in range(count)]

        def sem(n, count):
            return [k.sem(f"conv_{n}{s}") for s in range(count)]

        rows = sb("rows", [P, PER, BY_DST], SLOTS)
        far = sb("far", [P, PER, F], SLOTS)
        weights = sb("weights", [HIDDEN, P, PER], SLOTS)
        hidden = sb("hidden", [HIDDEN + 1, P, PER], 2)
        hot = sb("hot", [P, PER, P], 2)
        local = sb("local", [P, PER], 2)
        along = sb("along", [P, PER, MUL, 3], 1)[0]
        factors = sb("factors", [P, PER, 2 * MUL], 1)[0]
        products_a = sb("products_a", [P, PER, 2 * MUL, 2 * MUL], 1)[0]
        products_b = sb("products_b", [P, 3, PER, 2 * MUL, MUL], 1)[0]
        sum_a = sb("sum_a", [P, PER, 2 * MUL], 1)[0]
        sum_b = sb("sum_b", [P, 5, PER, 2 * MUL], 1)[0]
        terms = sb("terms", [P, 3, 3, PER, MUL], 1)[0]
        message = sb("message", [P, PER, F], 2)
        radial_a = ctx.enter_context(nc.psum_tensor("conv_radial_a", [P, 2, PER, 256], F32))
        radial_b = ctx.enter_context(nc.psum_tensor("conv_radial_b", [P, 2, PER, 128], F32))
        part = [ctx.enter_context(nc.psum_tensor(f"conv_part{s}", [P, 512], F32)) for s in range(2)]
        rows_in, rows_free = sem("rows_in", SLOTS), sem("rows_free", SLOTS)
        gathered, far_free = sem("gathered", SLOTS), sem("far_free", SLOTS)
        weights_in, weights_free = sem("weights_in", SLOTS), sem("weights_free", SLOTS)
        hidden_ready = sem("hidden_ready", 2)
        radial_ready, radial_free = sem("radial_ready", 2), sem("radial_free", 2)
        message_ready, part_ready, part_free = sem("message_ready", 2), sem("part_ready", 2), sem("part_free", 2)
        own, added, cleared, ones_set = (sem(n, 1)[0] for n in ("vector_steps", "added", "cleared", "ones_set"))
        block = ctx.enter_context(nc.Block())
        entry, first_node = k.entry["by_dst"], k.first_node["by_dst"]

        @block.sync
        def _(sp):
            for s in range(SLOTS):
                sp.sem_inc(rows_free[s], 1)
                sp.sem_inc(weights_free[s], 1)
            with sp.Fori(0, TURNS) as i:
                for s in range(SLOTS):
                    at = sp.value_load(entry[0:1, bass.ds(i * SLOTS + s, 1), 0], min_val=0, max_val=EDGES)
                    sp.wait_ge(rows_free[s], 1)
                    sp.sem_clear(rows_free[s])
                    sp.dma_start(rows[s][:], k.edges_by_dst[bass.ds(at, GROUP), :].rearrange(
                        "(p j) w -> p j w", p=P)).then_inc(rows_in[s], 16)
                    sp.wait_ge(weights_free[s], 1)
                    sp.sem_clear(weights_free[s])
                    sp.dma_start(weights[s][:].rearrange("h p j -> h (p j)").unsqueeze(1),
                                 k.weight_by_group[bass.ds(i * SLOTS + s, 1), :].partition_broadcast(HIDDEN)
                                 ).then_inc(weights_in[s], 16)

        @block.gpsimd
        def _(pool):
            for s in range(SLOTS):
                pool.sem_inc(far_free[s], 1)
            with pool.Fori(0, TURNS):
                for s in range(SLOTS):
                    pool.wait_ge(rows_in[s], 16)
                    pool.sem_clear(rows_in[s])
                    pool.wait_ge(far_free[s], 1)
                    pool.sem_clear(far_free[s])
                    for j in range(PER):
                        pool.indirect_dma_start(
                            far[s][:, j, :], None, k.hop_dram[0],
                            bass.IndirectOffsetOnAxis(ap=rows[s][:, j, 0:1].bitcast(I32), axis=0)
                        ).then_inc(gathered[s], 16)

        @block.scalar
        def _(act):
            for c in range(2):
                act.activation(hidden[c][HIDDEN:HIDDEN + 1, :, :],
                               k.ident[HIDDEN:HIDDEN + 1, 0:1].unsqueeze(2).broadcast_to([1, P, PER]),
                               ACT.Copy, bias=1.0, scale=0.0).then_inc(ones_set, 1)
            act.wait_ge(ones_set, 2)
            with act.Fori(0, TURNS) as i:
                for s in range(SLOTS):
                    c = s % 2
                    act.wait_ge(weights_in[s], i * 16 + 16)
                    if s >= 2:
                        act.wait_ge(radial_ready[c], turn(i, s - 2, 2))
                    else:
                        act.wait_ge(radial_free[c], turn(i, s, 2))
                    act.activation(hidden[c][0:HIDDEN, :, :], weights[s][:], ACT.Relu,
                                   bias=k.b3a[:], scale=k.w3a[:]).then_inc(hidden_ready[c], 1)
                    act.wait_ge(hidden_ready[c], turn(i, s, 2))
                    act.sem_inc(weights_free[s], 1)

        @block.tensor
        def _(pe):
            for c in range(2):
                pe.sem_inc(radial_free[c], 1)

            def radial(i, s):
                c = s % 2
                pe.wait_ge(hidden_ready[c], turn(i, s, 2))
                pe.wait_ge(radial_free[c], turn(i, s, 2))
                for j in range(PER):
                    pe.matmul(radial_a[:, c, j, :], hidden[c][:, :, j], k.radial[:, 0:256], start=True, stop=True)
                    last = pe.matmul(radial_b[:, c, j, :], hidden[c][:, :, j], k.radial[:, 256:384],
                                     start=True, stop=True)
                last.then_inc(radial_ready[c], 1)

            def sum_nodes(i, s):
                c = s % 2
                pe.wait_ge(message_ready[c], turn(i, s, 2))
                pe.wait_ge(part_free[c], turn(i, s, 2))
                for j in range(PER):
                    last = pe.matmul(part[c][:, 0:F], hot[c][:, j, :], message[c][:, j, :],
                                     start=(j == 0), stop=(j == PER - 1))
                last.then_inc(part_ready[c], 1)

            with pe.Fori(0, TURNS) as i:
                radial(i, 0)
                for s in range(SLOTS):
                    if s < SLOTS - 1:
                        radial(i, s + 1)
                    sum_nodes(i, s)

        @block.vector
        def _(dve):
            own_steps = Steps(dve, own)
            dve.memset(k.sums[:], 0.0).then_inc(cleared, 1)
            dve.wait_ge(cleared, 1)
            for c in range(2):
                dve.sem_inc(part_free[c], 1)

            def make(i, s):
                c = s % 2
                own_steps.restart()
                step, r, f = own_steps.step, rows[s][:, :, 3:8], far[s]
                vectors = f[:, :, MUL:F].rearrange("p j (v o) -> p j v o", o=3)
                dve.wait_ge(gathered[s], (i + 1) * (16 * PER))
                n = step(dve.tensor_scalar(local[c][:], rows[s][:, :, 1],
                                           first_node[:, bass.ds(i * SLOTS + s, 1)], None, ALU.subtract))
                m = step(dve.tensor_tensor(along[:], vectors, spread(r[:, :, 0:3], 2, MUL), ALU.mult))
                own_steps.wait(n)
                step(dve.tensor_tensor(hot[c][:], spread(k.iota[:], 1, PER), spread(local[c][:], 2, P),
                                       ALU.is_equal))
                own_steps.wait(m)
                step(dve.tensor_reduce(factors[:, :, MUL:2 * MUL], along[:], AX.X, ALU.add))
                n = step(dve.tensor_copy(factors[:, :, 0:MUL], f[:, :, 0:MUL]))
                dve.wait_ge(radial_ready[c], turn(i, s, 2))
                own_steps.wait(n)
                n = step(dve.tensor_tensor(products_a[:], radial_a[:, c].rearrange("p j (q m) -> p j q m", m=2 * MUL),
                                           spread(factors[:], 2, 2 * MUL), ALU.mult))
                for o in range(3):
                    m = step(dve.tensor_tensor(
                        products_b[:, o], radial_b[:, c].rearrange("p j (q v) -> p j q v", v=MUL),
                        spread(vectors[:, :, :, o], 2, 2 * MUL), ALU.mult))
                own_steps.wait(n)
                n = step(dve.tensor_reduce(sum_a[:], products_a[:], AX.X, ALU.add))
                own_steps.wait(m)
                dve.sem_inc(radial_free[c], 1)
                dve.sem_inc(far_free[s], 1)
                m = step(dve.tensor_reduce(sum_b[:, 0:3].rearrange("p o j q -> p (o j q)"),
                                           products_b[:].rearrange("p o j q v -> p (o j q) v"), AX.X, ALU.add))
                own_steps.wait(n)
                step(dve.tensor_copy(message[c][:, :, 0:MUL], sum_a[:, :, 0:MUL]))
                t = step(dve.tensor_tensor(terms[:, 0], spread(r[:, :, 0:3].rearrange("p j o -> p o j"), 3, MUL),
                                       spread(sum_a[:, :, MUL:2 * MUL], 1, 3), ALU.mult))
                own_steps.wait(m)
                n = step(dve.tensor_copy(sum_b[:, 3:5, :, MUL:2 * MUL], sum_b[:, 0:2, :, MUL:2 * MUL]))
                own_steps.wait(t)
                step(dve.tensor_tensor(terms[:, 0], terms[:, 0], sum_b[:, 0:3, :, 0:MUL], ALU.add))
                own_steps.wait(n)
                step(dve.tensor_tensor(terms[:, 1], spread(r[:, :, 1:4].rearrange("p j o -> p o j"), 3, MUL),
                                       sum_b[:, 2:5, :, MUL:2 * MUL], ALU.mult))
                n = step(dve.tensor_tensor(terms[:, 2], spread(r[:, :, 2:5].rearrange("p j o -> p o j"), 3, MUL),
                                           sum_b[:, 1:4, :, MUL:2 * MUL], ALU.mult))
                own_steps.wait(n)
                dve.sem_inc(rows_free[s], 1)
                step(dve.tensor_tensor(terms[:, 1], terms[:, 1], terms[:, 2], ALU.subtract))
                own_steps.wait()
                step(dve.tensor_tensor(message[c][:, :, MUL:F].rearrange("p j (u o) -> p o j u", o=3),
                                       terms[:, 0], terms[:, 1], ALU.add))
                own_steps.wait()
                dve.sem_inc(message_ready[c], 1)

            def accumulate(i, s):
                c = s % 2
                at = dve.value_load(entry[0:1, bass.ds(i * SLOTS + s, 1), 1], min_val=0, max_val=BINS - 1)
                dve.wait_ge(part_ready[c], turn(i, s, 2))
                sums = k.sums[:, bass.ds(at * (F + 1), F)]
                dve.tensor_tensor(sums, sums, part[c][:, 0:F], ALU.add).then_inc(added, 1)
                dve.wait_ge(added, s + 1)
                dve.sem_inc(part_free[c], 1)

            with dve.Fori(0, TURNS) as i:
                dve.sem_clear(added)
                for s in range(SLOTS):
                    make(i, s)
                    if s:
                        accumulate(i, s - 1)
                accumulate(i, SLOTS - 1)


def last_update(nc, k):
    sums = k.sums[:].rearrange("p (b w) -> p b w", w=F + 1)[:, :, 0:F]

    def before(dve, s):
        s.step(dve.tensor_tensor(k.x[:], k.x[:], sums, ALU.add))
        s.wait()

    normalize(nc, k, "norm3", before=before, store=[(k.out, k.x)])


def gnn_kernel(nc, x, src, dst, edge_attr_3, edge_weight, L0_gnn_W, L0_gnn_b, L1_gnn_w, L1_gnn_fc_w,
               L1_gnn_fc_b, L1_gnn_bias, L3_gnn_w1, L3_gnn_b1, L3_gnn_w2, L3_gnn_b2, out):
    k = Memory()
    k.in_x, k.in_src, k.in_dst, k.in_attr, k.in_weight = x, src, dst, edge_attr_3, edge_weight
    k.in_w0, k.in_b0, k.in_w1, k.in_fc, k.in_fcb, k.in_bias1 = (
        L0_gnn_W, L0_gnn_b, L1_gnn_w, L1_gnn_fc_w, L1_gnn_fc_b, L1_gnn_bias)
    k.in_w3a, k.in_b3a, k.in_w3b, k.in_b3b = L3_gnn_w1, L3_gnn_b1, L3_gnn_w2, L3_gnn_b2
    k.out = out
    k.hops = 0

    def dram(name, shape, dt):
        return nc.dram_tensor(name, shape, dt).ap()

    k.edges_by_dst = dram("edges_by_dst", [EDGES + GROUP, BY_DST], F32)
    k.edges_by_src = dram("edges_by_src", [EDGES + GROUP, BY_SRC], F32)
    k.weight_by_group = dram("weight_by_group", [GROUPS, GROUP], F32)
    k.far_dram = dram("far_rows", [NODES, FAR], F32)
    k.hop_dram = [dram(f"hop_rows{n}", [NODES, F], F32) for n in range(2)]
    k.entry_dram = dram("entries", [TABLE, 2], I32)
    k.node_dram = dram("first_nodes", [TABLE], F32)
    with ExitStack() as ctx:
        def sb(name, shape, dt=F32):
            return ctx.enter_context(nc.sbuf_tensor(name, shape, dt))

        k.iota, k.ident, k.before, k.ones = (sb(n, [P, P]) for n in ("iota", "ident", "before", "ones"))
        k.eps = sb("eps", [P, 1])
        k.group_no = sb("group_no", [P, TCOLS])
        k.x = sb("x", [P, BINS, F])
        k.w0, k.b0 = sb("w0", [F, F]), sb("b0", [P, F])
        k.w1, k.w1_by_f = sb("w1", [HEADS * F, F]), sb("w1_by_f", [F, HEADS, F])
        k.fc, k.fcb, k.bias1 = sb("fc", [F, 2 * F]), sb("fcb", [P, 1]), sb("bias1", [P, F])
        k.scorer, k.scorer_parts = sb("scorer", [F, 2 * HEADS]), sb("scorer_parts", [F, HEADS, F])
        k.w3a, k.b3a = sb("w3a", [HIDDEN, 1]), sb("b3a", [HIDDEN, 1])
        k.w3, k.radial = sb("w3", [HIDDEN + 1, RADIAL]), sb("radial", [HIDDEN + 1, RADIAL])
        k.entry = {n: sb(f"entry_{n}", [1, TABLE, 2], I32) for n in ("by_dst", "by_src")}
        k.first_node = {n: sb(f"first_node_{n}", [P, TABLE]) for n in ("by_dst", "by_src")}
        k.degree, k.degree_root, k.inverse = (sb(n, [P, BINS]) for n in ("degree", "degree_root", "inverse"))
        k.own_score = sb("own_score", [P, BINS, HEADS])
        k.maximum = sb("maximum", [P, BINS * HEADS])
        k.update = sb("update", [P, BATCH, F])
        setup(nc, k)
        with ExitStack() as sorting:
            def tmp(name, shape, dt):
                return sorting.enter_context(nc.sbuf_tensor(name, shape, dt))

            k.place_i = tmp("place_i", [P, COLS], I32)
            with nc.sbuf_tensor("rows_by_dst", [P, COLS, BY_DST], F32) as k.rows:
                pack_edges(nc, k)
                rank_edges(nc, k, k.in_dst, "by_dst")
                scatter_edges(nc, k, k.rows, BY_DST, k.edges_by_dst, "by_dst")
            with nc.sbuf_tensor("rows_by_src", [P, COLS, BY_SRC], F32) as rows:
                pack_ends(nc, k, rows)
                rank_edges(nc, k, k.in_src, "by_src")
                scatter_edges(nc, k, rows, BY_SRC, k.edges_by_src, "by_src")
        with nc.sbuf_tensor("sums_first", [P, BINS * (F + 1)], F32) as k.sums, \
                nc.sbuf_tensor("far_rows_sb", [P, BINS, FAR], F32) as k.far_rows:
            sum_messages(nc, k, k.in_x, first=True)
            first_update(nc, k)
        with nc.sbuf_tensor("hop_rows", [P, BINS, F], F32) as k.hop_rows:
            with nc.sbuf_tensor("attention", [P, BINS * HEADS * (F + 1)], F32) as k.attention, \
                    nc.sbuf_tensor("denominator", [P, BATCH, HEADS], F32) as k.denominator, \
                    nc.sbuf_tensor("share", [P, BATCH, HEADS], F32) as k.share:
                attend(nc, k)
                attention_update(nc, k)
            with nc.sbuf_tensor("sums", [P, BINS * (F + 1)], F32) as k.sums:
                sum_messages(nc, k, k.hop_dram[0], first=False)
                between_hops(nc, k)
                sum_messages(nc, k, k.hop_dram[1], first=False)
                after_hops(nc, k)
                radial_weights(nc, k)
                convolve(nc, k)
                last_update(nc, k)


_INS = ["x", "src", "dst", "edge_attr_3", "edge_weight", "L0_gnn_W", "L0_gnn_b", "L1_gnn_w", "L1_gnn_fc_w",
        "L1_gnn_fc_b", "L1_gnn_bias", "L3_gnn_w1", "L3_gnn_b1", "L3_gnn_w2", "L3_gnn_b2"]


def kernel(**inputs):
    import numpy as _np
    import concourse.bacc as _bacc
    from concourse import mybir as _mybir
    from concourse.bass_utils import run_bass_kernel_spmd as _run

    nc = _bacc.Bacc("TRN2", target_bir_lowering=False, num_devices=1)
    arrays, args = {}, []
    for name in _INS:
        a = _np.ascontiguousarray(inputs[name])
        arrays[f"in_{name}_dram"] = a
        args.append(nc.dram_tensor(f"in_{name}_dram", a.shape, _mybir.dt.from_np(a.dtype), kind="ExternalInput").ap())
    args.append(nc.dram_tensor("out_0_dram", (NODES, F), _mybir.dt.from_np(_np.dtype("float32")),
                               kind="ExternalOutput").ap())
    gnn_kernel(nc, *args)
    r = _run(nc, [arrays], core_ids=[0])
    return r.results[0]["out_0_dram"]
```

```python
from contextlib import ExitStack, contextmanager
from math import pi, sqrt

import concourse.bass as bass
from concourse import mybir

F32 = mybir.dt.float32
I32 = mybir.dt.int32
U16 = mybir.dt.uint16
BF16 = mybir.dt.bfloat16
ALU = mybir.AluOpType
ACT = mybir.ActivationFunctionType
AX = mybir.AxisListType

P = 128
NODES = 12500
EDGES = 400000
F = 32
HEADS = 4
HIDDEN = 64
RADIAL = 384
BINS = -(-NODES // P)
LAST = NODES - (BINS - 1) * P
COLS = EDGES // P
PER = 4
GROUP = P * PER
SLOTS = 4
NEEDED = (EDGES + BINS * (GROUP - 1)) // GROUP
TURNS = -(-NEEDED // SLOTS)
GROUPS = TURNS * SLOTS
TABLE = P * -(-GROUPS // P)
TCOLS = TABLE // P
BY_DST = 8
BY_SRC = 2
FAR = 40
BIG = 1e30
EPS = 1e-5
BATCH = 7
MUL = 8
COUNTING = 24
RANGE = 50.0
AHEAD = 2


@contextmanager
def stage(nc, k):
    made = []

    def sem(name):
        made.append(nc.alloc_semaphore(name))
        return made[-1]

    k.sem = sem
    with ExitStack() as ctx:
        yield ctx
    nc.clear_and_free_semaphores(made)
    nc.all_engine_barrier()


class Memory:
    pass


class Steps:

    def __init__(self, engine, semaphore):
        self.engine, self.semaphore, self.n = engine, semaphore, 0

    def restart(self):
        self.engine.sem_clear(self.semaphore)
        self.n = 0

    def step(self, instruction):
        instruction.then_inc(self.semaphore, 1)
        self.n += 1
        return self.n

    def wait(self, n=None):
        self.engine.wait_ge(self.semaphore, self.n if n is None else n)


def spread(ap, axis, n):
    ap = ap.unsqueeze(axis)
    shape = list(ap.shape)
    shape[axis] = n
    return ap.broadcast_to(shape)


def turn(i, slot, of):
    return i * (SLOTS // of) + slot // of + 1


def node_rows(table):
    whole = table[0:(BINS - 1) * P, :].rearrange("(b p) f -> p b f", p=P)
    return whole, table[(BINS - 1) * P:NODES, :]


def setup(nc, k):
    with stage(nc, k) as ctx:
        made = k.sem("constants_made")
        cleared = k.sem("constants_cleared")
        padded = k.sem("last_bin_cleared")
        loaded = k.sem("setup_loaded")
        block = ctx.enter_context(nc.Block())

        @block.gpsimd
        def _(pool):
            pool.iota(k.iota[:], pattern=[[1, P]], base=0, channel_multiplier=0,
                      allow_small_or_imprecise_dtypes=True).then_inc(made, 1)
            pool.iota(k.group_no[:], pattern=[[1, TCOLS]], base=0, channel_multiplier=TCOLS,
                      allow_small_or_imprecise_dtypes=True).then_inc(made, 1)
            pool.memset(k.ident[:], 0.0).then_inc(cleared, 1)
            pool.memset(k.before[:], 1.0).then_inc(cleared, 1)
            pool.memset(k.ones[:], 1.0).then_inc(made, 1)
            pool.memset(k.eps[:], EPS).then_inc(made, 1)
            pool.wait_ge(cleared, 2)
            pool.affine_select(out=k.ident[:], in_=k.ident[:], compare_op=ALU.not_equal, fill=1.0,
                               base=0, pattern=[[-1, P]], channel_multiplier=1).then_inc(made, 1)
            pool.affine_select(out=k.before[:], in_=k.before[:], compare_op=ALU.is_gt, fill=0.0,
                               base=0, pattern=[[1, P]], channel_multiplier=-1).then_inc(made, 1)
            pool.wait_ge(made, 6)

        @block.vector
        def _(dve):
            dve.memset(k.x[:, BINS - 1, :], 0.0).then_inc(padded, 1)
            dve.wait_ge(made, 6)
            dve.tensor_scalar(k.half_less[:], k.iota[:], -1.0, 0.5, ALU.mult, ALU.add).then_inc(padded, 1)
            dve.wait_ge(padded, 2)

        @block.sync
        def _(sp):
            whole, last = node_rows(k.in_x)
            sp.dma_start(k.x[:, 0:BINS - 1, :], whole).then_inc(loaded, 16)
            sp.wait_ge(padded, 1)
            sp.dma_start(k.x[0:LAST, BINS - 1, :], last).then_inc(loaded, 16)
            sp.dma_start(k.w0[:], k.in_w0).then_inc(loaded, 16)
            sp.dma_start(k.b0[:], k.in_b0.partition_broadcast(P)).then_inc(loaded, 16)
            sp.dma_start(k.w1[:], k.in_w1.rearrange("h f o -> (h f) o")).then_inc(loaded, 16)
            sp.dma_start(k.w1_by_f[:], k.in_w1.rearrange("h f o -> f h o")).then_inc(loaded, 16)
            sp.dma_start(k.fc[:], k.in_fc[0, :].partition_broadcast(F)).then_inc(loaded, 16)
            sp.dma_start(k.fcb[:], k.in_fcb.partition_broadcast(P)).then_inc(loaded, 16)
            sp.dma_start(k.bias1[:], k.in_bias1.partition_broadcast(P)).then_inc(loaded, 16)
            sp.dma_start(k.w3a[:], k.in_w3a.rearrange("a h -> h a")).then_inc(loaded, 16)
            sp.dma_start(k.b3a[:], k.in_b3a.rearrange("(h a) -> h a", a=1)).then_inc(loaded, 16)
            sp.dma_start(k.w3[0:HIDDEN, :], k.in_w3b).then_inc(loaded, 16)
            sp.dma_start(k.w3[HIDDEN:HIDDEN + 1, :],
                         k.in_b3b.rearrange("(a r) -> a r", a=1)).then_inc(loaded, 16)
            sp.wait_ge(loaded, 16 * 13)


def pack_edges(nc, k, q):
    CHUNKS = 5
    CHUNK = COLS // CHUNKS
    with stage(nc, k) as ctx:
        attr = ctx.enter_context(nc.sbuf_tensor("attr", [P, CHUNK, 3], F32))
        weight = ctx.enter_context(nc.sbuf_tensor("weight_chunk", [P, CHUNK], F32))
        norm = ctx.enter_context(nc.sbuf_tensor("attr_norm", [P, 2, CHUNK], F32))
        key = ctx.enter_context(nc.sbuf_tensor("edge_key", [P, COLS], I32))
        step_up = key
        tail = ctx.enter_context(nc.sbuf_tensor("tail", [P, PER, BY_DST], F32))
        ends = ctx.enter_context(nc.sbuf_tensor("edge_ends", [P, 4], F32))
        next_key = ctx.enter_context(nc.sbuf_tensor("next_key", [P, 1], I32))
        sums = ctx.enter_context(nc.psum_tensor("dst_sums", [P, 2, 512], F32))
        in_order = ctx.enter_context(nc.psum_tensor("order_flags", [P, 512], F32))
        chunk_loaded = k.sem("chunk_loaded")
        src_loaded, dst_loaded, next_loaded = (k.sem(n) for n in ("src_loaded", "dst_loaded", "next_loaded"))
        src_used, next_cleared = k.sem("src_used"), k.sem("next_cleared")
        squares_summed = k.sem("squares_summed")
        root_taken = k.sem("root_taken")
        chunk_packed = k.sem("chunk_packed")
        bins_ready, counted, counts_found = (k.sem(n) for n in ("bins_ready", "counted", "counts_found"))
        summed, order_found, order_summed = (k.sem(n) for n in ("summed", "order_found", "order_summed"))
        table_made, table_stored, table_loaded = (k.sem(n) for n in ("table_made", "table_stored", "table_loaded"))
        own, count_steps = k.sem("pack_steps"), k.sem("count_steps")
        tail_made = k.sem("tail_made")
        tail_stored = k.sem("tail_stored")
        block = ctx.enter_context(nc.Block())
        attr_in = k.in_attr.rearrange("(p t) c -> p t c", p=P)
        weight_in = k.in_weight.rearrange("(p t) -> p t", p=P)
        dst_in = k.in_dst.rearrange("(p t) -> p t", p=P)

        @block.sync
        def _(sp):
            sp.dma_start(k.place_i[:], dst_in).then_inc(dst_loaded, 16)
            sp.dma_start(key[:], k.in_src.rearrange("(p t) -> p t", p=P)).then_inc(src_loaded, 16)
            sp.wait_ge(next_cleared, 1)
            sp.dma_start(next_key[0:P - 1, :], dst_in[1:P, 0:1], allow_slow_non_contiguous=True).then_inc(next_loaded, 16)
            for c in range(CHUNKS):
                if c:
                    sp.wait_ge(chunk_packed, c)
                sp.dma_start(attr[:], attr_in[:, c * CHUNK:(c + 1) * CHUNK, :]).then_inc(chunk_loaded, 16)
                sp.dma_start(weight[:], weight_in[:, c * CHUNK:(c + 1) * CHUNK]).then_inc(chunk_loaded, 16)
            sp.wait_ge(tail_made, 2)
            sp.dma_start(k.edges_by_dst[EDGES:EDGES + GROUP, :].rearrange("(p j) w -> p j w", p=P),
                         tail[:]).then_inc(tail_stored, 16)
            sp.dma_start(k.edges_by_src[EDGES:EDGES + GROUP, :].rearrange("(p j) w -> p j w", p=P),
                         tail[:, :, 0:BY_SRC]).then_inc(tail_stored, 16)
            sp.wait_ge(tail_stored, 32)
            move_table(sp, k, q, "by_dst", table_made, table_stored, table_loaded)

        @block.gpsimd
        def _(pool):
            pool.memset(next_key[:], 1 << 20).then_inc(next_cleared, 1)
            pool.memset(tail[:], 0.0).then_inc(tail_made, 1)
            pool.wait_ge(tail_made, 1)
            pool.memset(tail[:, :, 1], -1.0).then_inc(tail_made, 1)

        @block.scalar
        def _(act):
            for c in range(CHUNKS):
                act.wait_ge(squares_summed, c + 1)
                act.activation(norm[:, 1, :], norm[:, 0, :], ACT.Sqrt).then_inc(root_taken, 1)
            act.wait_ge(bins_ready, 1)
            count_bins(act, k, q, count_steps)
            act.sem_inc(counted, 1)

        @block.tensor
        def _(pe):
            pe.wait_ge(order_found, 1)
            pe.matmul(in_order[:, 0:1], k.ones[:], ends[:, 3:4], start=True, stop=True).then_inc(order_summed, 1)
            pe.wait_ge(counts_found, 1)
            sum_counts(pe, k, q, sums, summed)

        @block.vector
        def _(dve):
            s = Steps(dve, own)
            dve.wait_ge(src_loaded, 16)
            s.step(dve.tensor_copy(k.rows[:, :, 0].bitcast(I32), key[:]))
            dve.wait_ge(dst_loaded, 16)
            s.step(dve.tensor_copy(k.rows[:, :, 1], k.place_i[:]))
            s.wait()
            difference = step_up[:].bitcast(F32)[:, 0:COLS - 1]
            s.step(dve.tensor_tensor(difference, k.place_i[:, 1:COLS], k.place_i[:, 0:COLS - 1], ALU.subtract))
            dve.wait_ge(next_loaded, 16)
            s.step(dve.tensor_tensor(ends[:, 0:1], next_key[:], k.place_i[:, COLS - 1:COLS], ALU.subtract))
            s.wait()
            s.step(dve.tensor_reduce(ends[:, 1:2], difference, AX.X, ALU.min))
            s.wait()
            s.step(dve.tensor_tensor(ends[:, 2:3], ends[:, 0:1], ends[:, 1:2], ALU.min))
            s.wait()
            s.step(dve.tensor_scalar(ends[:, 3:4], ends[:, 2:3], 0.0, None, ALU.is_ge))
            s.wait()
            dve.sem_inc(order_found, 1)
            cut_bins(dve, s, k, q)
            dve.sem_inc(bins_ready, 1)
            dve.wait_ge(order_summed, 1)
            s.step(dve.tensor_scalar(k.in_order[:], in_order[:, 0:1], P - 0.5, None, ALU.is_ge))
            for c in range(CHUNKS):
                cut = slice(c * CHUNK, (c + 1) * CHUNK)
                dve.wait_ge(chunk_loaded, 32 * (c + 1))
                s.step(dve.tensor_copy(k.rows[:, cut, 2], weight[:]))
                square = k.rows[:, cut, 3:6]
                s.step(dve.tensor_tensor(square, attr[:], attr[:], ALU.mult))
                s.wait()
                dve.tensor_reduce(norm[:, 0, :], square, AX.X, ALU.add).then_inc(squares_summed, 1)
                dve.wait_ge(root_taken, c + 1)
                s.step(dve.reciprocal(norm[:, 0, :], norm[:, 1, :]))
                s.wait()
                inverse = norm[:, 0, :].unsqueeze(2)
                s.step(dve.tensor_tensor(k.rows[:, cut, 3:5], attr[:, :, 1:3],
                                         inverse.broadcast_to([P, CHUNK, 2]), ALU.mult))
                s.step(dve.tensor_tensor(k.rows[:, cut, 5:6], attr[:, :, 0:1], inverse, ALU.mult))
                s.step(dve.tensor_tensor(k.rows[:, cut, 6:8], attr[:, :, 1:3],
                                         inverse.broadcast_to([P, CHUNK, 2]), ALU.mult))
                s.wait()
                dve.sem_inc(chunk_packed, 1)
            dve.wait_ge(counted, 1)
            find_counts(dve, s, q)
            dve.sem_inc(counts_found, 1)
            dve.wait_ge(summed, 1)
            make_table(dve, s, k, q, sums)
            dve.sem_inc(table_made, 1)


def sort_memory(nc, ctx, name):
    def sb(n, shape, dt=F32):
        return ctx.enter_context(nc.sbuf_tensor(f"{name}_{n}", shape, dt))

    q = Memory()
    q.bins, q.mine = sb("bins", [P, COLS], BF16), sb("mine", [P, COLS], U16)
    q.signs = sb("signs", [P, BINS + 1])
    q.count, q.total, q.start, q.first = (sb(n, [P, BINS]) for n in ("count", "total", "start", "first"))
    q.groups, q.last_group, q.shift = (sb(n, [P, BINS]) for n in ("groups", "last_group", "shift"))
    q.groups_i = sb("groups_i", [P, BINS], I32)
    q.passed, q.shifted = (sb(n, [P, TCOLS, BINS - 1]) for n in ("passed", "shifted"))
    q.bin_of, q.start_of, q.node_of = (sb(n, [P, TCOLS]) for n in ("bin_of", "start_of", "node_of"))
    q.entry = sb("entry_made", [P, TCOLS, 2], I32)
    return q


def cut_bins(dve, s, k, q):
    s.step(dve.tensor_scalar(k.place_i[:], k.place_i[:], P.bit_length() - 1, None, ALU.logical_shift_right))
    s.wait()
    s.step(dve.tensor_copy(q.bins[:], k.place_i[:]))
    s.wait()


def count_bins(act, k, q, steps):
    with act.Fori(0, BINS + 1) as b:
        act.sem_clear(steps)
        act.activation(q.mine[:].bitcast(BF16), q.bins[:], ACT.Sign, bias=k.half_less[:, bass.ds(b, 1)],
                       accum_out=q.signs[:, bass.ds(b, 1)]).then_inc(steps, 1)
        act.wait_ge(steps, 1)


def find_counts(dve, s, q):
    s.step(dve.tensor_scalar(q.signs[:], q.signs[:], float(COLS), 0.5, ALU.add, ALU.mult))
    s.wait()
    s.step(dve.tensor_tensor(q.count[:], q.signs[:, 0:BINS], q.signs[:, 1:BINS + 1], ALU.subtract))
    s.wait()


def sum_counts(pe, k, q, sums, summed):
    pe.matmul(sums[:, 0, 0:BINS], k.ones[:], q.count[:], start=True, stop=True)
    pe.matmul(sums[:, 1, 0:BINS], k.before[:], q.count[:], start=True, stop=True).then_inc(summed, 1)


def make_table(dve, s, k, q, sums):
    one = k.ones[:, 0:1].broadcast_to([P, BINS])
    s.step(dve.tensor_copy(q.total[:], sums[:, 0, 0:BINS]))
    s.wait()
    s.step(dve.tensor_tensor_scan(q.start[:], one, q.total[:], 0.0, ALU.mult, ALU.add))
    s.wait()
    s.step(dve.tensor_tensor(q.start[:], q.start[:], q.total[:], ALU.subtract))
    s.wait()
    s.step(dve.scalar_tensor_tensor(q.first[:], q.start[:], -1.0, sums[:, 1, 0:BINS], ALU.add, ALU.add))
    s.step(dve.tensor_scalar(q.groups_i[:], q.total[:], float(GROUP - 1), None, ALU.add))
    s.wait()
    s.step(dve.tensor_scalar(q.groups_i[:], q.groups_i[:], GROUP.bit_length() - 1, None,
                             ALU.logical_shift_right))
    s.wait()
    s.step(dve.tensor_copy(q.groups[:], q.groups_i[:]))
    s.wait()
    s.step(dve.tensor_tensor_scan(q.last_group[:], one, q.groups[:], 0.0, ALU.mult, ALU.add))
    s.wait()
    s.step(dve.tensor_tensor(q.shift[:], q.last_group[:], q.groups[:], ALU.subtract))
    s.wait()
    s.step(dve.scalar_tensor_tensor(q.shift[:], q.shift[:], -float(GROUP), q.start[:], ALU.mult, ALU.add))
    s.wait()
    s.step(dve.tensor_tensor(q.groups[:, 0:BINS - 1], q.shift[:, 1:BINS], q.shift[:, 0:BINS - 1],
                             ALU.subtract))
    s.step(dve.tensor_tensor(q.passed[:], spread(q.last_group[:, 0:BINS - 1], 1, TCOLS),
                             spread(k.group_no[:], 2, BINS - 1), ALU.is_le))
    s.wait()
    s.step(dve.tensor_tensor(q.shifted[:], q.passed[:], spread(q.groups[:, 0:BINS - 1], 1, TCOLS), ALU.mult))
    s.step(dve.tensor_reduce(q.bin_of[:], q.passed[:], AX.X, ALU.add))
    s.wait()
    s.step(dve.tensor_reduce(q.start_of[:], q.shifted[:], AX.X, ALU.add))
    s.wait()
    s.step(dve.scalar_tensor_tensor(q.start_of[:], k.group_no[:], float(GROUP), q.start_of[:],
                                    ALU.mult, ALU.add))
    s.wait()
    s.step(dve.tensor_scalar(q.entry[:, :, 0], q.start_of[:], float(EDGES), None, ALU.min))
    s.step(dve.tensor_copy(q.entry[:, :, 1], q.bin_of[:]))
    s.step(dve.tensor_scalar(q.node_of[:], q.bin_of[:], float(P), None, ALU.mult))
    s.wait()


def move_table(queue, k, q, name, made, stored, loaded):
    queue.wait_ge(made, 1)
    queue.dma_start(k.entry_dram[:, :].rearrange("(p c) e -> p c e", p=P), q.entry[:]).then_inc(stored, 16)
    queue.dma_start(k.node_dram[:].rearrange("(p c) -> p c", p=P), q.node_of[:]).then_inc(stored, 16)
    queue.wait_ge(stored, 32)
    queue.dma_start(k.entry[name][0:1, :, :], k.entry_dram.unsqueeze(0)).then_inc(loaded, 16)
    queue.dma_start(k.first_node[name][:], k.node_dram.partition_broadcast(P)).then_inc(loaded, 16)
    queue.wait_ge(loaded, 32)


def place_bin(dve, s, k, q, b):
    s.restart()
    s.step(dve.tensor_scalar(q.mine[:], q.bins[:], k.iota[:, bass.ds(b, 1)], None, ALU.is_equal))
    s.wait()
    s.step(dve.tensor_tensor_scan(q.running[:], k.ones[:, 0:1].broadcast_to([P, COLS]), q.mine[:],
                                  q.first[:, bass.ds(b, 1)], ALU.mult, ALU.add))
    s.wait()
    s.step(dve.copy_predicated(q.place[:], q.mine[:], q.running[:]))
    s.wait()


def pack_ends(nc, k, rows):
    with stage(nc, k) as ctx:
        keys = [ctx.enter_context(nc.sbuf_tensor(f"ends{n}", [P, COLS], I32)) for n in range(2)]
        loaded = k.sem("ends_loaded")
        packed = k.sem("ends_packed")
        block = ctx.enter_context(nc.Block())

        @block.sync
        def _(sp):
            sp.dma_start(keys[0][:], k.in_dst.rearrange("(p t) -> p t", p=P)).then_inc(loaded, 16)
            sp.dma_start(keys[1][:], k.in_src.rearrange("(p t) -> p t", p=P)).then_inc(loaded, 16)

        @block.vector
        def _(dve):
            dve.wait_ge(loaded, 32)
            dve.tensor_copy(rows[:, :, 0].bitcast(I32), keys[0][:]).then_inc(packed, 1)
            dve.tensor_copy(rows[:, :, 1], keys[1][:]).then_inc(packed, 1)
            dve.wait_ge(packed, 2)


RUN = 25
HALF = [13, 12]
AT = [0, 13]
ROUNDS = COLS // RUN


def scatter_memory(nc, k, ctx, width, name):
    m = Memory()
    m.index = [ctx.enter_context(nc.sbuf_tensor(f"{name}_index{s}", [P, HALF[s]], I32)) for s in range(2)]
    m.row = [ctx.enter_context(nc.sbuf_tensor(f"{name}_row{s}", [P, HALF[s], width], F32)) for s in range(2)]
    m.staged = [k.sem(f"{name}_staged{s}") for s in range(2)]
    m.written = [k.sem(f"{name}_written{s}") for s in range(2)]
    return m


def stage_rows(sp, k, m, rows):
    def fetch(i, s):
        at = i * RUN + AT[s]
        sp.dma_start(m.index[s][:], k.place_i[:, bass.ds(at, HALF[s])]).then_inc(m.staged[s], 16)
        sp.dma_start(m.row[s][:], rows[:, bass.ds(at, HALF[s]), :]).then_inc(m.staged[s], 16)

    fetch(0, 0)
    fetch(0, 1)
    with sp.Fori(0, ROUNDS - 1) as i:
        for s in range(2):
            sp.wait_ge(m.written[s], (i + 1) * (16 * HALF[s]))
            fetch(i + 1, s)


def write_rows(pool, m, table):
    with pool.Fori(0, ROUNDS):
        for s in range(2):
            pool.wait_ge(m.staged[s], 32)
            pool.sem_clear(m.staged[s])
            for j in range(HALF[s]):
                pool.indirect_dma_start(
                    table, bass.IndirectOffsetOnAxis(ap=m.index[s][:, j:j + 1], axis=0),
                    m.row[s][:, j, :], None).then_inc(m.written[s], 16)
    for s in range(2):
        pool.wait_ge(m.written[s], 16 * HALF[s] * ROUNDS)


def order_by_dst(nc, k, q):
    with stage(nc, k) as ctx:
        q.place = ctx.enter_context(nc.sbuf_tensor("dst_place", [P, COLS], F32))
        q.running = ctx.enter_context(nc.sbuf_tensor("dst_running", [P, COLS], F32))
        m = scatter_memory(nc, k, ctx, BY_DST, "dst")
        own, places_ready, copied = k.sem("dst_place_steps"), k.sem("dst_places_ready"), k.sem("dst_rows_copied")
        block = ctx.enter_context(nc.Block())

        def in_order(engine):
            return engine.value_load(k.in_order[0:1, 0:1], min_val=0, max_val=1) == 1

        @block.sync
        def _(sp):
            with sp.If(in_order(sp)):
                sp.dma_start(k.edges_by_dst[0:EDGES, :].rearrange("(p t) w -> p t w", p=P),
                             k.rows[:]).then_inc(copied, 16)
                sp.wait_ge(copied, 16)
            with sp.Else():
                sp.wait_ge(places_ready, 1)
                stage_rows(sp, k, m, k.rows)

        @block.gpsimd
        def _(pool):
            with pool.If(in_order(pool)):
                pool.nop()
            with pool.Else():
                write_rows(pool, m, k.edges_by_dst)

        @block.vector
        def _(dve):
            s = Steps(dve, own)
            with dve.If(in_order(dve)):
                dve.nop()
            with dve.Else():
                s.step(dve.memset(q.place[:], 0.0))
                s.wait()
                with dve.Fori(0, BINS) as b:
                    place_bin(dve, s, k, q, b)
                s.restart()
                s.step(dve.tensor_copy(k.place_i[:], q.place[:]))
                s.wait()
                dve.sem_inc(places_ready, 1)


def order_by_src(nc, k, rows):
    with stage(nc, k) as ctx:
        m = scatter_memory(nc, k, ctx, BY_SRC, "src")
        block = ctx.enter_context(nc.Block())

        @block.sync
        def _(sp):
            stage_rows(sp, k, m, rows)

        @block.gpsimd
        def _(pool):
            write_rows(pool, m, k.edges_by_src)


def sum_messages(nc, k, table, q=None):
    first = q is not None
    width = F + 1 if first else F
    name = "weighted" if first else f"hop_{k.hops}"
    k.hops += 1
    with stage(nc, k) as ctx:
        def sb(n, shape, dt):
            return [ctx.enter_context(nc.sbuf_tensor(f"{name}_{n}{s}", shape, dt)) for s in range(SLOTS)]

        def sem(n):
            return [k.sem(f"{name}_{n}{s}") for s in range(SLOTS)]

        rows = sb("rows", [P, PER, BY_DST], F32)
        far = sb("far", [P, PER, F], F32)
        hot = sb("hot", [P, PER, P], F32)
        local = sb("local", [P, PER], F32)
        message = sb("message", [P, PER, width], F32) if first else far
        weight = sb("weight", [P, PER], F32) if first else None
        part = [ctx.enter_context(nc.psum_tensor(f"{name}_part{s}", [P, 512], F32)) for s in range(SLOTS)]
        rows_in = sem("rows_in")
        rows_free = sem("rows_free")
        gathered = sem("gathered")
        far_free = sem("far_free")
        message_ready = sem("message_ready")
        message_free = sem("message_free")
        part_ready = sem("part_ready")
        part_free = sem("part_free")
        weight_saved = sem("weight_saved") if first else None
        if first:
            sums = ctx.enter_context(nc.psum_tensor("src_sums", [P, 2, 512], F32))
            src_loaded, bins_ready, counted, counts_found, summed, table_made, table_stored, table_loaded, \
                count_steps, sort_steps = (k.sem(f"sort_src_{n}") for n in (
                    "loaded", "bins_ready", "counted", "counts_found", "summed", "table_made",
                    "table_stored", "table_loaded", "count_steps", "sort_steps"))
        own = k.sem(f"{name}_vector_steps")
        added = k.sem(f"{name}_added")
        cleared = k.sem(f"{name}_cleared")
        block = ctx.enter_context(nc.Block())
        entry, first_node = k.entry["by_dst"], k.first_node["by_dst"]

        @block.sync
        def _(sp):
            if first:
                sp.dma_start(k.place_i[:], k.in_src.rearrange("(p t) -> p t", p=P)).then_inc(src_loaded, 16)

            def load(i, s):
                at = sp.value_load(entry[0:1, bass.ds(i * SLOTS + s, 1), 0], min_val=0, max_val=EDGES)
                sp.dma_start(rows[s][:], k.edges_by_dst[bass.ds(at, GROUP), :].rearrange(
                    "(p j) w -> p j w", p=P)).then_inc(rows_in[s], 16)

            def retire(i, s):
                sp.wait_ge(rows_free[s], 1)
                sp.sem_clear(rows_free[s])
                if first:
                    sp.dma_start(k.weight_by_group[bass.ds(i * SLOTS + s, 1), :].rearrange(
                        "g (p j) -> (g p) j", p=P), weight[s][:]).then_inc(weight_saved[s], 16)

            for s in range(SLOTS):
                load(0, s)
            with sp.Fori(0, TURNS - 1) as i:
                for s in range(SLOTS):
                    retire(i, s)
                    load(i + 1, s)
            for s in range(SLOTS):
                retire(TURNS - 1, s)
            if first:
                for s in range(SLOTS):
                    sp.wait_ge(weight_saved[s], 16 * TURNS)

        @block.gpsimd
        def _(pool):
            for s in range(SLOTS):
                pool.sem_inc(far_free[s], 1)
            with pool.Fori(0, TURNS):
                for s in range(SLOTS):
                    pool.wait_ge(rows_in[s], 16)
                    pool.sem_clear(rows_in[s])
                    pool.wait_ge(far_free[s], 1)
                    pool.sem_clear(far_free[s])
                    for j in range(PER):
                        pool.indirect_dma_start(
                            far[s][:, j, :], None, table,
                            bass.IndirectOffsetOnAxis(ap=rows[s][:, j, 0:1].bitcast(I32), axis=0)
                        ).then_inc(gathered[s], 16)

        @block.vector
        def _(dve):
            own_steps = Steps(dve, own)
            dve.memset(k.sums[:], 0.0).then_inc(cleared, 1)
            if first:
                for s in range(SLOTS):
                    dve.memset(message[s][:], 1.0).then_inc(cleared, 1)
                dve.wait_ge(cleared, 1 + SLOTS)
            else:
                dve.wait_ge(cleared, 1)
            if first:
                sort = Steps(dve, sort_steps)
                dve.wait_ge(src_loaded, 16)
                sort.step(dve.memset(q.place[:], 0.0))
                cut_bins(dve, sort, k, q)
                dve.sem_inc(bins_ready, 1)
            for s in range(SLOTS):
                dve.sem_inc(part_free[s], 1)
                dve.sem_inc(message_free[s], 1)

            def select(i, s, again=True):
                own_steps.restart()
                dve.wait_ge(gathered[s], (i + 1) * (16 * PER))
                dve.wait_ge(message_free[s], i + 1)
                own_steps.step(dve.tensor_scalar(local[s][:], rows[s][:, :, 1],
                                                 first_node[:, bass.ds(i * SLOTS + s, 1)], None,
                                                 ALU.subtract))
                if first:
                    own_steps.step(dve.tensor_tensor(message[s][:, :, 0:F], far[s][:],
                                                     spread(rows[s][:, :, 2], 2, F), ALU.mult))
                    if again:
                        dve.wait_ge(weight_saved[s], i * 16)
                    own_steps.step(dve.tensor_copy(weight[s][:], rows[s][:, :, 2]))
                own_steps.wait(1)
                own_steps.step(dve.tensor_tensor(hot[s][:], spread(k.iota[:], 1, PER),
                                                 spread(local[s][:], 2, P), ALU.is_equal))
                own_steps.wait()
                dve.sem_inc(message_ready[s], 1)
                dve.sem_inc(rows_free[s], 1)
                if first:
                    dve.sem_inc(far_free[s], 1)

            def accumulate(i, s):
                at = dve.value_load(entry[0:1, bass.ds(i * SLOTS + s, 1), 1], min_val=0, max_val=BINS - 1)
                dve.wait_ge(part_ready[s], i + 1)
                if s:
                    dve.wait_ge(added, s)
                sums = k.sums[:, bass.ds(at * (F + 1), width)]
                dve.tensor_tensor(sums, sums, part[s][:, 0:width], ALU.add).then_inc(added, 1)
                dve.wait_ge(added, s + 1)
                dve.sem_inc(part_free[s], 1)

            def one_turn(i, again=True):
                dve.sem_clear(added)
                for s in range(SLOTS):
                    select(i, s, again)
                    if s:
                        accumulate(i, s - 1)
                accumulate(i, SLOTS - 1)

            if not first:
                with dve.Fori(0, TURNS) as i:
                    one_turn(i)
                return
            one_turn(0, again=False)
            with dve.Fori(1, COUNTING) as i:
                one_turn(i)
            sort.restart()
            dve.wait_ge(counted, 1)
            find_counts(dve, sort, q)
            dve.sem_inc(counts_found, 1)
            dve.wait_ge(summed, 1)
            make_table(dve, sort, k, q, sums)
            dve.sem_inc(table_made, 1)
            with dve.Fori(COUNTING, COUNTING + BINS) as i:
                one_turn(i)
                place_bin(dve, sort, k, q, i - COUNTING)
            sort.restart()
            sort.step(dve.tensor_copy(k.place_i[:], q.place[:]))
            with dve.Fori(COUNTING + BINS, TURNS) as i:
                one_turn(i)
            sort.wait()

        @block.tensor
        def _(pe):
            def one_turn(i):
                for s in range(SLOTS):
                    pe.wait_ge(message_ready[s], i + 1)
                    if not first:
                        pe.wait_ge(gathered[s], (i + 1) * (16 * PER))
                    pe.wait_ge(part_free[s], i + 1)
                    for j in range(PER):
                        last = pe.matmul(part[s][:, 0:width], hot[s][:, j, :], message[s][:, j, :],
                                         start=(j == 0), stop=(j == PER - 1))
                    last.then_inc(part_ready[s], 1)
                    pe.wait_ge(part_ready[s], i + 1)
                    pe.sem_inc(message_free[s], 1)
                    if not first:
                        pe.sem_inc(far_free[s], 1)

            if not first:
                with pe.Fori(0, TURNS) as i:
                    one_turn(i)
                return
            with pe.Fori(0, COUNTING) as i:
                one_turn(i)
            pe.wait_ge(counts_found, 1)
            sum_counts(pe, k, q, sums, summed)
            with pe.Fori(COUNTING, TURNS) as i:
                one_turn(i)

        @block.scalar
        def _(act):
            if not first:
                return
            act.wait_ge(bins_ready, 1)
            count_bins(act, k, q, count_steps)
            act.sem_inc(counted, 1)
            move_table(act, k, q, "by_src", table_made, table_stored, table_loaded)

def project(nc, k, name, source, depth, weights, width, finish):
    with stage(nc, k) as ctx:
        def sem(n):
            return k.sem(f"{name}_{n}")

        staged = ctx.enter_context(nc.sbuf_tensor(f"{name}_staged", [P, BATCH, depth], F32))
        turned = ctx.enter_context(nc.sbuf_tensor(f"{name}_turned", [depth, BATCH, P], F32))
        turned_ps = ctx.enter_context(nc.psum_tensor(f"{name}_turned_ps", [P, 8 * P], F32))
        out = ctx.enter_context(nc.psum_tensor(f"{name}_out", [P, 512], F32))
        rows_staged, rows_turned, copied, multiplied = sem("rows_staged"), sem("rows_turned"), sem("copied"), sem("multiplied")
        own = sem("steps")
        block = ctx.enter_context(nc.Block())

        @block.vector
        def _(dve):
            s = Steps(dve, own)
            with dve.Fori(0, BINS // BATCH) as i:
                s.restart()
                source(dve, s, i, staged)
                s.wait()
                dve.sem_inc(rows_staged, 1)
                dve.wait_ge(multiplied, i + 1)
                finish(dve, s, i, out[:, 0:BATCH * width].rearrange("p (b w) -> p b w", b=BATCH))
                s.wait()

        @block.tensor
        def _(pe):
            with pe.Fori(0, BINS // BATCH) as i:
                pe.wait_ge(rows_staged, i + 1)
                for b in range(BATCH):
                    last = pe.transpose(turned_ps[0:depth, b * P:(b + 1) * P], staged[:, b, :], k.ident[:])
                last.then_inc(rows_turned, 1)
                pe.wait_ge(copied, i + 1)
                for b in range(BATCH):
                    last = pe.matmul(out[:, b * width:(b + 1) * width], turned[:, b, :], weights,
                                     start=True, stop=True)
                last.then_inc(multiplied, 1)

        @block.scalar
        def _(act):
            with act.Fori(0, BINS // BATCH) as i:
                act.wait_ge(rows_turned, i + 1)
                act.copy(turned[:].rearrange("f b p -> f (b p)"),
                         turned_ps[0:depth, 0:BATCH * P]).then_inc(copied, 1)


def normalize(nc, k, name, before=None, after=None, store=()):
    with stage(nc, k) as ctx:
        centred = ctx.enter_context(nc.sbuf_tensor(f"{name}_centred", [P, BINS, F], F32))
        square = ctx.enter_context(nc.sbuf_tensor(f"{name}_square", [P, BINS, F], F32))
        mean = ctx.enter_context(nc.sbuf_tensor(f"{name}_mean", [P, BINS], F32))
        spread_of = ctx.enter_context(nc.sbuf_tensor(f"{name}_spread", [P, BINS], F32))
        own = k.sem(f"{name}_steps")
        variance_ready = k.sem(f"{name}_variance_ready")
        deviation_ready = k.sem(f"{name}_deviation_ready")
        ready = k.sem(f"{name}_rows_ready")
        stored = k.sem(f"{name}_rows_stored")
        block = ctx.enter_context(nc.Block())

        @block.vector
        def _(dve):
            s = Steps(dve, own)
            if before:
                before(dve, s)
            s.step(dve.tensor_reduce(mean[:], k.x[:], AX.X, ALU.add))
            s.wait()
            s.step(dve.tensor_scalar(mean[:], mean[:], 1.0 / F, None, ALU.mult))
            s.wait()
            s.step(dve.tensor_tensor(centred[:], k.x[:], spread(mean[:], 2, F), ALU.subtract))
            s.wait()
            s.step(dve.tensor_tensor(square[:], centred[:], centred[:], ALU.mult))
            s.wait()
            dve.tensor_reduce(spread_of[:], square[:], AX.X, ALU.add).then_inc(variance_ready, 1)
            dve.wait_ge(deviation_ready, 1)
            s.step(dve.reciprocal(spread_of[:], mean[:]))
            s.wait()
            s.step(dve.tensor_tensor(k.x[:], centred[:], spread(spread_of[:], 2, F), ALU.mult))
            s.wait()
            if after:
                after(dve, s)
                s.wait()
            dve.sem_inc(ready, 1)

        @block.scalar
        def _(act):
            act.wait_ge(variance_ready, 1)
            act.activation(mean[:], spread_of[:], ACT.Sqrt, bias=k.eps[:], scale=1.0 / F).then_inc(deviation_ready, 1)

        @block.sync
        def _(sp):
            sp.wait_ge(ready, 1)
            for n, (table, rows) in enumerate(store):
                whole, last = node_rows(table)
                sp.dma_start(whole, rows[:, 0:BINS - 1, :]).then_inc(stored, 16)
                sp.dma_start(last, rows[0:LAST, BINS - 1, :]).then_inc(stored, 16)
            if store:
                sp.wait_ge(stored, 32 * len(store))


def first_update(nc, k):
    sums = k.sums[:].rearrange("p (b w) -> p b w", w=F + 1)

    def source(dve, s, i, staged):
        s.step(dve.tensor_copy(staged[:], sums[:, bass.ds(i * BATCH, BATCH), 0:F]))

    def finish(dve, s, i, out):
        x = k.x[:, bass.ds(i * BATCH, BATCH), :]
        s.step(dve.tensor_tensor(k.update[:], out, spread(k.b0[:], 1, BATCH), ALU.add))
        s.wait()
        s.step(dve.tensor_scalar(k.update[:], k.update[:], 0.0, None, ALU.max))
        s.wait()
        s.step(dve.tensor_tensor(x, x, k.update[:], ALU.add))

    project(nc, k, "dense", source, F, k.w0[:], F, finish)

    def after(dve, s):
        s.step(dve.tensor_copy(k.degree[:], sums[:, :, F]))
        s.step(dve.tensor_copy(k.far_rows[:, :, 0:F], k.x[:]))
        for half in range(2):
            s.step(dve.tensor_tensor(k.scorer_parts[:], k.w1_by_f[:],
                                     spread(k.fc[:, half * F:(half + 1) * F], 1, HEADS), ALU.mult))
            s.wait()
            s.step(dve.tensor_reduce(k.scorer[:, half * HEADS:(half + 1) * HEADS], k.scorer_parts[:],
                                     AX.X, ALU.add))
            s.wait()
        s.step(dve.memset(k.far_rows[:, :, F:FAR], 1.0))

    normalize(nc, k, "norm0", after=after)

    def scores_source(dve, s, i, staged):
        s.step(dve.tensor_copy(staged[:], k.x[:, bass.ds(i * BATCH, BATCH), :]))

    def scores_finish(dve, s, i, out):
        s.step(dve.tensor_scalar(k.own_score[:, bass.ds(i * BATCH, BATCH), :], out[:, :, 0:HEADS],
                                 k.fcb[:], None, ALU.add))
        s.step(dve.tensor_copy(k.far_rows[:, bass.ds(i * BATCH, BATCH), F + 1:F + 1 + HEADS],
                               out[:, :, HEADS:2 * HEADS]))

    project(nc, k, "scores", scores_source, F, k.scorer[:], 2 * HEADS, scores_finish)
    with stage(nc, k) as ctx:
        stored = k.sem("far_rows_stored")
        block = ctx.enter_context(nc.Block())

        @block.sync
        def _(sp):
            whole, last = node_rows(k.far_dram)
            sp.dma_start(whole, k.far_rows[:, 0:BINS - 1, :]).then_inc(stored, 16)
            sp.dma_start(last, k.far_rows[0:LAST, BINS - 1, :]).then_inc(stored, 16)
            sp.wait_ge(stored, 32)


def bound_scores(nc, k):
    with stage(nc, k) as ctx:
        extremes = ctx.enter_context(nc.sbuf_tensor("extremes", [P, 2 * HEADS], F32))
        extreme = ctx.enter_context(nc.sbuf_tensor("extreme", [2 * HEADS, 1], F32))
        width = ctx.enter_context(nc.sbuf_tensor("score_width", [P, HEADS + 1], F32))
        reach = ctx.enter_context(nc.sbuf_tensor("score_reach", [P, BINS, HEADS], F32))
        turned = ctx.enter_context(nc.psum_tensor("extremes_turned", [P, 512], F32))
        overall = ctx.enter_context(nc.psum_tensor("extremes_overall", [P, 512], F32))
        own, found, in_rows, reduced, shared = (k.sem(n) for n in (
            "bound_steps", "extremes_found", "extremes_in_rows", "extremes_reduced", "extremes_shared"))
        block = ctx.enter_context(nc.Block())

        @block.vector
        def _(dve):
            s = Steps(dve, own)
            a_dst = k.far_rows[:, :, F + 1:F + 1 + HEADS].rearrange("p b h -> p h b")
            s.step(dve.tensor_reduce(extremes[:, 0:HEADS], a_dst, AX.X, ALU.max))
            s.step(dve.tensor_reduce(extremes[:, HEADS:], a_dst, AX.X, ALU.min))
            s.wait()
            s.step(dve.tensor_scalar(extremes[:, HEADS:], extremes[:, HEADS:], -1.0, None, ALU.mult))
            s.wait()
            dve.sem_inc(found, 1)
            dve.wait_ge(in_rows, 1)
            s.step(dve.tensor_reduce(extreme[:], turned[0:2 * HEADS, 0:P], AX.X, ALU.max))
            s.wait()
            dve.sem_inc(reduced, 1)
            dve.wait_ge(shared, 1)
            s.step(dve.tensor_copy(extremes[:], overall[:, 0:2 * HEADS]))
            s.wait()
            s.step(dve.tensor_tensor(width[:, 0:HEADS], extremes[:, 0:HEADS], extremes[:, HEADS:], ALU.add))
            s.step(dve.tensor_tensor(reach[:], k.own_score[:], spread(extremes[:, 0:HEADS], 1, BINS), ALU.add))
            s.wait()
            s.step(dve.tensor_reduce(width[:, HEADS:], width[:, 0:HEADS], AX.X, ALU.max))
            terms = k.node_terms[:].rearrange("p (b t) -> p b t", t=2 * HEADS)
            s.step(dve.tensor_copy(terms[:, :, 0:HEADS], k.own_score[:]))
            s.step(dve.scalar_tensor_tensor(terms[:, :, HEADS:], reach[:], 0.2, reach[:], ALU.mult, ALU.max))
            s.wait()
            s.step(dve.tensor_scalar(k.bounded[:], width[:, HEADS:], RANGE, None, ALU.is_le))
            s.wait()

        @block.tensor
        def _(pe):
            pe.wait_ge(found, 1)
            pe.transpose(turned[0:2 * HEADS, 0:P], extremes[:], k.ident[:]).then_inc(in_rows, 1)
            pe.wait_ge(reduced, 1)
            pe.matmul(overall[:, 0:2 * HEADS], extreme[:].broadcast_to([2 * HEADS, P]),
                      k.ident[0:2 * HEADS, 0:2 * HEADS], start=True, stop=True).then_inc(shared, 1)


def attend(nc, k):
    W = F + 1
    with stage(nc, k) as ctx:
        def sb(n, shape, dt, count):
            return [ctx.enter_context(nc.sbuf_tensor(f"att_{n}{s}", shape, dt)) for s in range(count)]

        def sem(n, count):
            return [k.sem(f"att_{n}{s}") for s in range(count)]

        rows = sb("rows", [P, PER, BY_SRC], F32, SLOTS)
        far = sb("far", [P, PER, FAR], F32, SLOTS)
        hot = sb("hot", [P, PER, P], F32, 2)
        absent = sb("absent", [P, PER, P], F32, 2)
        masked = sb("masked", [P, PER, HEADS, P], F32, 2)
        hot_turned = sb("hot_turned", [P, PER * P], F32, 2)
        local = sb("local", [P, PER], F32, 2)
        top = sb("top", [P, 4, HEADS], F32, 2)
        node_terms = sb("node_terms", [P, 2 * HEADS], F32, 2)
        rescale = sb("rescale", [P, HEADS], F32, 2)
        score = sb("score", [P, 2, PER, HEADS], F32, 2)
        share = sb("share", [P, PER, HEADS], F32, 2)
        message = sb("message", [P, PER, HEADS * W], F32, 2)
        scaled = ctx.enter_context(nc.sbuf_tensor("att_scaled", [P, HEADS, W], F32))
        masked_ps = ctx.enter_context(nc.psum_tensor("att_masked_ps", [P, HEADS, PER * P], F32))
        hot_ps = ctx.enter_context(nc.psum_tensor("att_hot_ps", [P, PER * P], F32))
        terms_ps = ctx.enter_context(nc.psum_tensor("att_terms_ps", [P, PER, P], F32))
        part = [ctx.enter_context(nc.psum_tensor(f"att_part{s}", [P, 512], F32)) for s in range(2)]
        rows_in, rows_free = sem("rows_in", SLOTS), sem("rows_free", SLOTS)
        gathered, far_free = sem("gathered", SLOTS), sem("far_free", SLOTS)
        hot_ready, absent_ready = sem("hot_ready", 2), sem("absent_ready", 2)
        masked_ready, masked_turned = sem("masked_ready", 2), sem("masked_turned", 2)
        maximum_taken = sem("maximum_taken", 1)[0]
        hot_in_psum, hot_copied = sem("hot_in_psum", 2), sem("hot_copied", 2)
        terms_ready, terms_spread = sem("terms_ready", 2), sem("terms_spread", 2)
        terms_read = sem("terms_read", 1)[0]
        score_ready, share_ready = sem("score_ready", 2), sem("share_ready", 2)
        message_ready, part_ready, part_free = sem("message_ready", 2), sem("part_ready", 2), sem("part_free", 2)
        own = sem("vector_steps", 1)[0]
        cleared = sem("cleared", 1)[0]
        b_hot = sb("b_hot", [P, PER, P], F32, SLOTS)
        b_local = sb("b_local", [P, PER], F32, SLOTS)
        b_turned = sb("b_turned", [P, PER * P], F32, SLOTS)
        b_score = sb("b_score", [P, 2, PER, HEADS], F32, SLOTS)
        b_share = sb("b_share", [P, PER, HEADS], F32, SLOTS)
        b_message = sb("b_message", [P, PER, HEADS * W], F32, SLOTS)
        b_hot_ready, b_hot_in_psum, b_hot_copied = (
            sem("b_hot_ready", SLOTS), sem("b_hot_in_psum", SLOTS), sem("b_hot_copied", SLOTS))
        b_terms_spread, b_terms_read = sem("b_terms_spread", SLOTS), sem("b_terms_read", SLOTS)
        b_score_ready, b_share_ready = sem("b_score_ready", SLOTS), sem("b_share_ready", SLOTS)
        b_message_ready, b_part_ready = sem("b_message_ready", SLOTS), sem("b_part_ready", SLOTS)
        b_added = sem("b_added", 1)[0]
        b_terms = [terms_ps, hot_ps[:].rearrange("p (j n) -> p j n", j=PER)]
        block = ctx.enter_context(nc.Block())
        entry, first_node = k.entry["by_src"], k.first_node["by_src"]

        def load_rows(sp):
            for s in range(SLOTS):
                sp.sem_inc(rows_free[s], 1)
            with sp.Fori(0, TURNS) as i:
                for s in range(SLOTS):
                    at = sp.value_load(entry[0:1, bass.ds(i * SLOTS + s, 1), 0], min_val=0, max_val=EDGES)
                    sp.wait_ge(rows_free[s], 1)
                    sp.sem_clear(rows_free[s])
                    sp.dma_start(rows[s][:], k.edges_by_src[bass.ds(at, GROUP), :].rearrange(
                        "(p j) w -> p j w", p=P)).then_inc(rows_in[s], 16)

        def gather_far(pool):
            for s in range(SLOTS):
                pool.sem_inc(far_free[s], 1)
            with pool.Fori(0, TURNS):
                for s in range(SLOTS):
                    pool.wait_ge(rows_in[s], 16)
                    pool.sem_clear(rows_in[s])
                    pool.wait_ge(far_free[s], 1)
                    pool.sem_clear(far_free[s])
                    for j in range(PER):
                        pool.indirect_dma_start(
                            far[s][:, j, :], None, k.far_dram,
                            bass.IndirectOffsetOnAxis(ap=rows[s][:, j, 0:1].bitcast(I32), axis=0)
                        ).then_inc(gathered[s], 16)

        def general_vector(dve):
            own_steps = Steps(dve, own)
            dve.memset(k.attention[:], 0.0).then_inc(cleared, 1)
            dve.memset(k.maximum[:], -BIG).then_inc(cleared, 1)
            dve.wait_ge(cleared, 2)
            for c in range(2):
                dve.sem_inc(part_free[c], 1)

            def select(i, s):
                c = s % 2
                own_steps.restart()
                dve.wait_ge(gathered[s], (i + 1) * (16 * PER))
                own_steps.step(dve.tensor_scalar(local[c][:], rows[s][:, :, 1],
                                                 first_node[:, bass.ds(i * SLOTS + s, 1)], None,
                                                 ALU.subtract))
                own_steps.wait()
                own_steps.step(dve.tensor_tensor(hot[c][:], spread(k.iota[:], 1, PER),
                                                 spread(local[c][:], 2, P), ALU.is_equal))
                own_steps.wait()
                dve.sem_inc(hot_ready[c], 1)
                dve.sem_inc(rows_free[s], 1)

            def mask(i, s):
                c = s % 2
                dve.wait_ge(absent_ready[c], turn(i, s, 2))
                dve.tensor_tensor(masked[c][:], spread(absent[c][:], 2, HEADS),
                                  spread(far[s][:, :, W:W + HEADS], 3, P), ALU.add).then_inc(masked_ready[c], 1)

            def raise_maximum(i, s, at):
                c = s % 2
                own_steps.restart()
                own_score = k.own_score[:].rearrange("p b h -> p (b h)")[:, bass.ds(at * HEADS, HEADS)]
                maximum = k.maximum[:, bass.ds(at * HEADS, HEADS)]
                dve.wait_ge(masked_turned[c], turn(i, s, 2))
                own_steps.step(dve.tensor_reduce(top[c][:, 0, :], masked_ps[:], AX.X, ALU.max))
                own_steps.step(dve.tensor_copy(node_terms[c][:, 0:HEADS], own_score))
                own_steps.wait()
                dve.sem_inc(maximum_taken, 1)
                own_steps.step(dve.tensor_tensor(top[c][:, 1, :], top[c][:, 0, :], own_score, ALU.add))
                own_steps.wait()
                own_steps.step(dve.scalar_tensor_tensor(top[c][:, 2, :], top[c][:, 1, :], 0.2, top[c][:, 1, :],
                                                        ALU.mult, ALU.max))
                own_steps.wait()
                own_steps.step(dve.tensor_tensor(node_terms[c][:, HEADS:2 * HEADS], top[c][:, 2, :], maximum,
                                                 ALU.max))
                own_steps.wait()
                own_steps.step(dve.tensor_tensor(top[c][:, 3, :], maximum, node_terms[c][:, HEADS:2 * HEADS],
                                                 ALU.subtract))
                own_steps.wait()
                own_steps.step(dve.tensor_copy(maximum, node_terms[c][:, HEADS:2 * HEADS]))
                own_steps.wait()
                dve.sem_inc(terms_ready[c], 1)

            def edge_scores(i, s):
                c = s % 2
                own_steps.restart()
                dve.wait_ge(terms_spread[c], turn(i, s, 2))
                own_steps.step(dve.tensor_tensor(score[c][:, 0], terms_ps[:, :, 0:HEADS],
                                                 far[s][:, :, W:W + HEADS], ALU.add))
                own_steps.wait()
                own_steps.step(dve.scalar_tensor_tensor(score[c][:, 1], score[c][:, 0], 0.2, score[c][:, 0],
                                                        ALU.mult, ALU.max))
                own_steps.wait()
                own_steps.step(dve.tensor_tensor(score[c][:, 0], score[c][:, 1],
                                                 terms_ps[:, :, HEADS:2 * HEADS], ALU.subtract))
                own_steps.wait()
                dve.sem_inc(terms_read, 1)
                own_steps.step(dve.tensor_scalar(score[c][:, 1], score[c][:, 0], 0.0, None, ALU.min))
                own_steps.wait()
                dve.sem_inc(score_ready[c], 1)

            def messages(i, s):
                c = s % 2
                own_steps.restart()
                dve.wait_ge(share_ready[c], turn(i, s, 2))
                own_steps.step(dve.tensor_tensor(
                    message[c][:].rearrange("p j (h w) -> p j h w", h=HEADS),
                    spread(far[s][:, :, 0:W], 2, HEADS), spread(share[c][:], 3, W), ALU.mult))
                own_steps.wait()
                dve.sem_inc(message_ready[c], 1)
                dve.sem_inc(far_free[s], 1)

            def accumulate(i, s, at):
                c = s % 2
                own_steps.restart()
                sums = k.attention[:, bass.ds(at * (HEADS * W), HEADS * W)]
                own_steps.step(dve.tensor_tensor(scaled[:], sums.rearrange("p (h w) -> p h w", h=HEADS),
                                                 spread(rescale[c][:], 2, W), ALU.mult))
                dve.wait_ge(part_ready[c], turn(i, s, 2))
                own_steps.wait()
                own_steps.step(dve.tensor_tensor(sums, scaled[:].rearrange("p h w -> p (h w)"),
                                                 part[c][:, 0:HEADS * W], ALU.add))
                own_steps.wait()
                dve.sem_inc(part_free[c], 1)

            with dve.Fori(0, TURNS) as i:
                for s in range(0, SLOTS, 2):
                    at = [dve.value_load(entry[0:1, bass.ds(i * SLOTS + s + d, 1), 1],
                                         min_val=0, max_val=BINS - 1) for d in range(2)]
                    select(i, s)
                    select(i, s + 1)
                    mask(i, s)
                    mask(i, s + 1)
                    raise_maximum(i, s, at[0])
                    raise_maximum(i, s + 1, at[1])
                    edge_scores(i, s)
                    edge_scores(i, s + 1)
                    messages(i, s)
                    messages(i, s + 1)
                    accumulate(i, s, at[0])
                    accumulate(i, s + 1, at[1])

        def general_tensor(pe):
            for once in range(1):
                pe.sem_inc(maximum_taken, 1)
                pe.sem_inc(terms_read, 1)

            def turn_hot(i, s):
                c = s % 2
                pe.wait_ge(hot_ready[c], turn(i, s, 2))
                if s:
                    pe.wait_ge(hot_copied[(s - 1) % 2], turn(i, s - 1, 2))
                for j in range(PER):
                    last = pe.transpose(hot_ps[:, j * P:(j + 1) * P], hot[c][:, j, :], k.ident[:])
                last.then_inc(hot_in_psum[c], 1)

            def turn_masked(i, s):
                c = s % 2
                pe.wait_ge(masked_ready[c], turn(i, s, 2))
                pe.wait_ge(maximum_taken, i * SLOTS + s + 1)
                for h in range(HEADS):
                    for j in range(PER):
                        last = pe.transpose(masked_ps[:, h, j * P:(j + 1) * P], masked[c][:, j, h, :],
                                            k.ident[:])
                last.then_inc(masked_turned[c], 1)

            def spread_terms(i, s):
                c = s % 2
                pe.wait_ge(terms_ready[c], turn(i, s, 2))
                pe.wait_ge(hot_copied[c], turn(i, s, 2))
                pe.wait_ge(terms_read, i * SLOTS + s + 1)
                for j in range(PER):
                    last = pe.matmul(terms_ps[:, j, 0:2 * HEADS], hot_turned[c][:, j * P:(j + 1) * P],
                                     node_terms[c][:], start=True, stop=True)
                last.then_inc(terms_spread[c], 1)

            def sum_nodes(i, s):
                c = s % 2
                pe.wait_ge(message_ready[c], turn(i, s, 2))
                pe.wait_ge(part_free[c], turn(i, s, 2))
                for j in range(PER):
                    last = pe.matmul(part[c][:, 0:HEADS * W], hot[c][:, j, :], message[c][:, j, :],
                                     start=(j == 0), stop=(j == PER - 1))
                last.then_inc(part_ready[c], 1)

            with pe.Fori(0, TURNS) as i:
                for s in range(0, SLOTS, 2):
                    turn_hot(i, s)
                    turn_hot(i, s + 1)
                    turn_masked(i, s)
                    turn_masked(i, s + 1)
                    spread_terms(i, s)
                    spread_terms(i, s + 1)
                    sum_nodes(i, s)
                    sum_nodes(i, s + 1)

        def general_scalar(act):
            def hide(i, s):
                c = s % 2
                act.wait_ge(hot_ready[c], turn(i, s, 2))
                act.activation(absent[c][:], hot[c][:], ACT.Copy, bias=-BIG, scale=BIG).then_inc(absent_ready[c], 1)

            def copy_hot(i, s):
                c = s % 2
                act.wait_ge(hot_in_psum[c], turn(i, s, 2))
                act.copy(hot_turned[c][:], hot_ps[:]).then_inc(hot_copied[c], 1)

            def exponents(i, s):
                c = s % 2
                act.wait_ge(terms_ready[c], turn(i, s, 2))
                act.activation(rescale[c][:], top[c][:, 3, :], ACT.Exp)
                act.wait_ge(score_ready[c], turn(i, s, 2))
                act.activation(share[c][:], score[c][:, 1], ACT.Exp).then_inc(share_ready[c], 1)

            with act.Fori(0, TURNS) as i:
                for s in range(0, SLOTS, 2):
                    hide(i, s)
                    hide(i, s + 1)
                    copy_hot(i, s)
                    copy_hot(i, s + 1)
                    exponents(i, s)
                    exponents(i, s + 1)

        def bounded_vector(dve):
            own_steps = Steps(dve, own)
            dve.memset(k.attention[:], 0.0).then_inc(cleared, 1)
            dve.wait_ge(cleared, 1)
            for c in range(2):
                dve.sem_inc(part_free[c], 1)

            def select(i, s):
                own_steps.restart()
                dve.wait_ge(gathered[s], (i + 1) * (16 * PER))
                own_steps.step(dve.tensor_scalar(b_local[s][:], rows[s][:, :, 1],
                                                 first_node[:, bass.ds(i * SLOTS + s, 1)], None,
                                                 ALU.subtract))
                own_steps.wait()
                own_steps.step(dve.tensor_tensor(b_hot[s][:], spread(k.iota[:], 1, PER),
                                                 spread(b_local[s][:], 2, P), ALU.is_equal))
                own_steps.wait()
                dve.sem_inc(b_hot_ready[s], 1)
                dve.sem_inc(rows_free[s], 1)

            def edge_scores(i, s):
                own_steps.restart()
                dve.wait_ge(b_terms_spread[s], i + 1)
                own_steps.step(dve.tensor_tensor(b_score[s][:, 0], b_terms[s % 2][:, :, 0:HEADS],
                                                 far[s][:, :, W:W + HEADS], ALU.add))
                own_steps.wait()
                own_steps.step(dve.scalar_tensor_tensor(b_score[s][:, 1], b_score[s][:, 0], 0.2,
                                                        b_score[s][:, 0], ALU.mult, ALU.max))
                own_steps.wait()
                own_steps.step(dve.tensor_tensor(b_score[s][:, 0], b_score[s][:, 1],
                                                 b_terms[s % 2][:, :, HEADS:2 * HEADS], ALU.subtract))
                own_steps.wait()
                dve.sem_inc(b_terms_read[s], 1)
                own_steps.step(dve.tensor_scalar(b_score[s][:, 1], b_score[s][:, 0], 0.0, None, ALU.min))
                own_steps.wait()
                dve.sem_inc(b_score_ready[s], 1)

            def messages(i, s):
                own_steps.restart()
                dve.wait_ge(b_share_ready[s], i + 1)
                own_steps.step(dve.tensor_tensor(
                    b_message[s][:].rearrange("p j (h w) -> p j h w", h=HEADS),
                    spread(far[s][:, :, 0:W], 2, HEADS), spread(b_share[s][:], 3, W), ALU.mult))
                own_steps.wait()
                dve.sem_inc(b_message_ready[s], 1)
                dve.sem_inc(far_free[s], 1)

            def accumulate(i, s):
                at = dve.value_load(entry[0:1, bass.ds(i * SLOTS + s, 1), 1], min_val=0, max_val=BINS - 1)
                dve.wait_ge(b_part_ready[s], i + 1)
                if s:
                    dve.wait_ge(b_added, s)
                sums = k.attention[:, bass.ds(at * (HEADS * W), HEADS * W)]
                dve.tensor_tensor(sums, sums, part[s % 2][:, 0:HEADS * W], ALU.add).then_inc(b_added, 1)
                dve.wait_ge(b_added, s + 1)
                dve.sem_inc(part_free[s % 2], 1)

            with dve.Fori(0, TURNS) as i:
                dve.sem_clear(b_added)
                for s in range(SLOTS + 1):
                    if s < SLOTS:
                        select(i, s)
                    if s >= 1:
                        edge_scores(i, s - 1)
                        if s >= 2:
                            accumulate(i, s - 2)
                        messages(i, s - 1)
                accumulate(i, SLOTS - 1)

        def bounded_tensor(pe):
            def turn_hot(i, s):
                pe.wait_ge(b_hot_ready[s], i + 1)
                for j in range(PER):
                    last = pe.transpose(masked_ps[:, s, j * P:(j + 1) * P], b_hot[s][:, j, :], k.ident[:])
                last.then_inc(b_hot_in_psum[s], 1)

            def spread_terms(i, s):
                at = pe.value_load(entry[0:1, bass.ds(i * SLOTS + s, 1), 1], min_val=0, max_val=BINS - 1)
                pe.wait_ge(b_hot_copied[s], i + 1)
                pe.wait_ge(b_terms_read[s], i + 1)
                for j in range(PER):
                    last = pe.matmul(b_terms[s % 2][:, j, 0:2 * HEADS], b_turned[s][:, j * P:(j + 1) * P],
                                     k.node_terms[:, bass.ds(at * 8, 8)], start=True, stop=True)
                last.then_inc(b_terms_spread[s], 1)

            def sum_nodes(i, s):
                pe.wait_ge(b_message_ready[s], i + 1)
                pe.wait_ge(part_free[s % 2], turn(i, s, 2))
                for j in range(PER):
                    last = pe.matmul(part[s % 2][:, 0:HEADS * W], b_hot[s][:, j, :], b_message[s][:, j, :],
                                     start=(j == 0), stop=(j == PER - 1))
                last.then_inc(b_part_ready[s], 1)

            for s in range(SLOTS):
                pe.sem_inc(b_terms_read[s], 1)
            with pe.Fori(0, TURNS) as i:
                for s in range(SLOTS):
                    turn_hot(i, s)
                    spread_terms(i, s)
                    if s >= 1:
                        sum_nodes(i, s - 1)
                sum_nodes(i, SLOTS - 1)

        def bounded_scalar(act):
            def copy_hot(i, s):
                act.wait_ge(b_hot_in_psum[s], i + 1)
                act.copy(b_turned[s][:], masked_ps[:, s, :]).then_inc(b_hot_copied[s], 1)

            def exponents(i, s):
                act.wait_ge(b_score_ready[s], i + 1)
                act.activation(b_share[s][:], b_score[s][:, 1], ACT.Exp).then_inc(b_share_ready[s], 1)

            with act.Fori(0, TURNS) as i:
                for s in range(SLOTS):
                    copy_hot(i, s)
                    if s >= 1:
                        exponents(i, s - 1)
                exponents(i, SLOTS - 1)

        def bounded(engine):
            return engine.value_load(k.bounded[0:1, 0:1], min_val=0, max_val=1) == 1

        @block.sync
        def _(sp):
            load_rows(sp)

        @block.gpsimd
        def _(pool):
            gather_far(pool)

        @block.vector
        def _(dve):
            with dve.If(bounded(dve)):
                bounded_vector(dve)
            with dve.Else():
                general_vector(dve)

        @block.tensor
        def _(pe):
            with pe.If(bounded(pe)):
                bounded_tensor(pe)
            with pe.Else():
                general_tensor(pe)

        @block.scalar
        def _(act):
            with act.If(bounded(act)):
                bounded_scalar(act)
            with act.Else():
                general_scalar(act)


def attention_update(nc, k):
    W = F + 1
    sums = k.attention[:].rearrange("p (b h w) -> p b h w", h=HEADS, w=W)

    def source(dve, s, i, staged):
        part = sums[:, bass.ds(i * BATCH, BATCH), :, :]
        s.step(dve.tensor_scalar(k.denominator[:], part[:, :, :, F], 1e-30, float(HEADS), ALU.max, ALU.mult))
        s.wait()
        s.step(dve.reciprocal(k.share[:], k.denominator[:]))
        s.wait()
        for h in range(HEADS):
            s.step(dve.tensor_tensor(staged[:, :, h * F:(h + 1) * F], part[:, :, h, 0:F],
                                     k.share[:, :, h:h + 1].broadcast_to([P, BATCH, F]), ALU.mult))

    def finish(dve, s, i, out):
        x = k.x[:, bass.ds(i * BATCH, BATCH), :]
        s.step(dve.tensor_tensor(k.update[:], out, spread(k.bias1[:], 1, BATCH), ALU.add))
        s.wait()
        s.step(dve.tensor_tensor(x, x, k.update[:], ALU.add))

    project(nc, k, "heads", source, HEADS * F, k.w1[:], F, finish)

    with stage(nc, k) as ctx:
        degree_ready, root_ready, inverse_ready = (k.sem(n) for n in ("degree_ready", "root_ready", "inverse_ready"))
        block = ctx.enter_context(nc.Block())

        @block.vector
        def _(dve):
            dve.tensor_scalar(k.degree[:], k.degree[:], 1.0, None, ALU.add).then_inc(degree_ready, 1)
            dve.wait_ge(root_ready, 1)
            dve.reciprocal(k.inverse[:], k.degree_root[:]).then_inc(inverse_ready, 1)
            dve.wait_ge(inverse_ready, 1)

        @block.scalar
        def _(act):
            act.wait_ge(degree_ready, 1)
            act.activation(k.degree_root[:], k.degree[:], ACT.Sqrt).then_inc(root_ready, 1)

    def after(dve, s):
        s.step(dve.scalar_tensor_tensor(k.hop_rows[:], k.x[:], 0.0, spread(k.inverse[:], 2, F),
                                        ALU.max, ALU.mult))

    normalize(nc, k, "norm1", after=after, store=[(k.hop_dram[0], k.hop_rows)])


def between_hops(nc, k):
    sums = k.sums[:].rearrange("p (b w) -> p b w", w=F + 1)[:, :, 0:F]
    with stage(nc, k) as ctx:
        own, ready, stored = (k.sem(n) for n in ("hop_steps", "hop_rows_ready", "hop_rows_stored"))
        block = ctx.enter_context(nc.Block())

        @block.vector
        def _(dve):
            s = Steps(dve, own)
            s.step(dve.tensor_tensor(k.hop_rows[:], k.hop_rows[:], sums, ALU.add))
            for _ in range(2):
                s.wait()
                s.step(dve.tensor_tensor(k.hop_rows[:], k.hop_rows[:], spread(k.inverse[:], 2, F), ALU.mult))
            s.wait()
            dve.sem_inc(ready, 1)

        @block.sync
        def _(sp):
            sp.wait_ge(ready, 1)
            whole, last = node_rows(k.hop_dram[1])
            sp.dma_start(whole, k.hop_rows[:, 0:BINS - 1, :]).then_inc(stored, 16)
            sp.dma_start(last, k.hop_rows[0:LAST, BINS - 1, :]).then_inc(stored, 16)
            sp.wait_ge(stored, 32)


def after_hops(nc, k):
    sums = k.sums[:].rearrange("p (b w) -> p b w", w=F + 1)[:, :, 0:F]

    def before(dve, s):
        s.step(dve.tensor_tensor(k.hop_rows[:], k.hop_rows[:], sums, ALU.add))
        s.wait()
        s.step(dve.tensor_tensor(k.hop_rows[:], k.hop_rows[:], spread(k.inverse[:], 2, F), ALU.mult))
        s.wait()
        s.step(dve.tensor_tensor(k.x[:], k.x[:], k.hop_rows[:], ALU.add))
        s.wait()

    normalize(nc, k, "norm2", before=before, store=[(k.hop_dram[0], k.x)])


def radial_weights(nc, k):
    scalar_norm = sqrt(4 * pi) / sqrt(2 * MUL)
    vector_norm = sqrt(4 * pi) * sqrt(3.0) / sqrt(4 * MUL)
    flat = 0.5 / sqrt(pi)
    same = flat / sqrt(3.0)
    cross = sqrt(3.0 / (4 * pi)) / sqrt(6.0)
    tensor = sqrt(3.0 / (8 * pi))
    H1 = HIDDEN + 1
    with stage(nc, k) as ctx:
        own = k.sem("radial_steps")
        block = ctx.enter_context(nc.Block())

        @block.vector
        def _(dve):
            s = Steps(dve, own)
            a = k.radial[:, 0:256].rearrange("h (q m) -> h q m", m=2 * MUL)
            b = k.radial[:, 256:384].rearrange("h (q v) -> h q v", v=MUL)

            def paths(n):
                return k.w3[:, n * 64:(n + 1) * 64].rearrange("h (u v) -> h u v", v=MUL)

            vector_paths = k.w3[:, 192:384].rearrange("h (u v l) -> h u v l", v=MUL, l=3)
            for out, of, scale in (
                    (a[:, 0:8, 0:8], paths(0), scalar_norm * flat),
                    (a[:, 0:8, 8:16], paths(1), scalar_norm * flat),
                    (a[:, 8:16, 0:8], paths(2), vector_norm * flat),
                    (a[:, 8:16, 8:16], vector_paths[:, :, :, 2], vector_norm * tensor),
                    (b[:, 0:8, :], vector_paths[:, :, :, 0], vector_norm * same),
                    (b[:, 8:16, :], vector_paths[:, :, :, 1], vector_norm * cross)):
                s.step(dve.tensor_scalar(out, of, scale, None, ALU.mult))
            s.wait()
            s.step(dve.scalar_tensor_tensor(b[:, 0:8, :], vector_paths[:, :, :, 2],
                                            -vector_norm * tensor / 3, b[:, 0:8, :], ALU.mult, ALU.add))
            s.wait()


def convolve(nc, k):
    with stage(nc, k) as ctx:
        def sb(n, shape, count):
            return [ctx.enter_context(nc.sbuf_tensor(f"conv_{n}{s}", shape, F32)) for s in range(count)]

        def sem(n, count):
            return [k.sem(f"conv_{n}{s}") for s in range(count)]

        rows = sb("rows", [P, PER, BY_DST], SLOTS)
        far = sb("far", [P, PER, F], SLOTS)
        weights = sb("weights", [HIDDEN, P, PER], SLOTS)
        hidden = sb("hidden", [HIDDEN + 1, P, PER], 2)
        away = sb("away", [P, PER, P], 1)[0]
        hot = sb("hot", [P, PER, P], 2)
        minus_local = sb("minus_local", [P, PER], 2)
        along = sb("along", [P, PER, MUL, 3], 2)
        factors = sb("factors", [P, PER, 2 * MUL], 2)
        products_a = sb("products_a", [P, PER, 2 * MUL, 2 * MUL], 1)[0]
        folded_a = sb("folded_a", [P, PER, 2 * MUL, MUL], 1)[0]
        products_b = sb("products_b", [P, 3, PER, 2 * MUL, MUL], 1)[0]
        message = sb("message", [P, PER, 5, MUL], 2)
        sum_b = sb("sum_b", [P, 5, PER, 2 * MUL], 2)
        crossed = sb("crossed", [P, 2, 3, PER, MUL], 2)
        radial_a = ctx.enter_context(nc.psum_tensor("conv_radial_a", [P, 2, PER, 256], F32))
        radial_b = ctx.enter_context(nc.psum_tensor("conv_radial_b", [P, 2, PER, 128], F32))
        part = [ctx.enter_context(nc.psum_tensor(f"conv_part{s}", [P, 512], F32)) for s in range(2)]
        rows_in, rows_free = sem("rows_in", SLOTS), sem("rows_free", SLOTS)
        gathered, far_free = sem("gathered", SLOTS), sem("far_free", SLOTS)
        weights_in, weights_free = sem("weights_in", SLOTS), sem("weights_free", SLOTS)
        hidden_ready = sem("hidden_ready", 2)
        radial_ready, radial_free = sem("radial_ready", 2), sem("radial_free", 2)
        factors_ready, factors_free = sem("factors_ready", 2), sem("factors_free", 2)
        hot_ready = sem("hot_ready", 2)
        sum_b_ready, sum_b_wrapped = sem("sum_b_ready", 2), sem("sum_b_wrapped", 2)
        message_ready, part_ready, part_free = sem("message_ready", 2), sem("part_ready", 2), sem("part_free", 2)
        products_made, folded = sem("products_made", 1)[0], sem("folded", 1)[0]
        own, copied, ones_set = (sem(n, 1)[0] for n in ("vector_steps", "scalar_steps", "ones_set"))
        block = ctx.enter_context(nc.Block())
        entry, first_node = k.entry["by_dst"], k.first_node["by_dst"]

        def turns(engine, one_turn):
            one_turn(0, True, False)
            with engine.Fori(1, TURNS - 1) as i:
                one_turn(i, False, False)
            one_turn(TURNS - 1, False, True)

        @block.sync
        def _(sp):
            for s in range(SLOTS):
                sp.sem_inc(rows_free[s], 2)
                sp.sem_inc(weights_free[s], 1)
            with sp.Fori(0, TURNS) as i:
                for s in range(SLOTS):
                    at = sp.value_load(entry[0:1, bass.ds(i * SLOTS + s, 1), 0], min_val=0, max_val=EDGES)
                    sp.wait_ge(rows_free[s], 2)
                    sp.sem_clear(rows_free[s])
                    sp.dma_start(rows[s][:], k.edges_by_dst[bass.ds(at, GROUP), :].rearrange(
                        "(p j) w -> p j w", p=P)).then_inc(rows_in[s], 16)
                    sp.wait_ge(weights_free[s], 1)
                    sp.sem_clear(weights_free[s])
                    sp.dma_start(weights[s][:].rearrange("h p j -> h (p j)").unsqueeze(1),
                                 k.weight_by_group[bass.ds(i * SLOTS + s, 1), :].partition_broadcast(HIDDEN)
                                 ).then_inc(weights_in[s], 16)

        @block.gpsimd
        def _(pool):
            for s in range(SLOTS):
                pool.sem_inc(far_free[s], 2)

            def gather(s, columns):
                for j in columns:
                    pool.indirect_dma_start(
                        far[s][:, j, :], None, k.hop_dram[0],
                        bass.IndirectOffsetOnAxis(ap=rows[s][:, j, 0:1].bitcast(I32), axis=0)
                    ).then_inc(gathered[s], 16)

            def gather_and_fold(s, fold=True):
                pool.wait_ge(rows_in[s], 16)
                pool.sem_clear(rows_in[s])
                pool.wait_ge(far_free[s], 2)
                pool.sem_clear(far_free[s])
                gather(s, range(PER // 2))
                if fold:
                    fold_products()
                gather(s, range(PER // 2, PER))

            def fold_products():
                pool.wait_ge(products_made, 1)
                pool.sem_clear(products_made)
                pool.tensor_tensor(folded_a[:], products_a[:, :, :, 0:MUL], products_a[:, :, :, MUL:2 * MUL],
                                   ALU.add).then_inc(folded, 1)

            for s in range(AHEAD):
                gather_and_fold(s, fold=False)
            for s in range(AHEAD, SLOTS):
                gather_and_fold(s)
            with pool.Fori(1, TURNS):
                for s in range(SLOTS):
                    gather_and_fold(s)
            for s in range(AHEAD):
                fold_products()

        @block.scalar
        def _(act):
            for c in range(2):
                act.activation(hidden[c][HIDDEN:HIDDEN + 1, :, :],
                               k.ident[HIDDEN:HIDDEN + 1, 0:1].unsqueeze(2).broadcast_to([1, P, PER]),
                               ACT.Copy, bias=1.0, scale=0.0).then_inc(ones_set, 1)
                act.sem_inc(factors_free[c], 1)
            act.wait_ge(ones_set, 2)

            def hide(i, s, again):
                c, slot = s % 2, s % SLOTS
                act.wait_ge(weights_in[slot], (i + s // SLOTS) * 16 + 16)
                if again:
                    act.wait_ge(radial_ready[c], turn(i, s - 2, 2))
                act.activation(hidden[c][0:HIDDEN, :, :], weights[slot][:], ACT.Relu,
                               bias=k.b3a[:], scale=k.w3a[:]).then_inc(hidden_ready[c], 1)

            def hidden_done(i, s):
                act.wait_ge(hidden_ready[s % 2], turn(i, s, 2))
                act.sem_inc(weights_free[s % SLOTS], 1)

            def wrap(i, s):
                c = s % 2
                act.wait_ge(sum_b_ready[c], turn(i, s, 2))
                act.copy(sum_b[c][:, 3:5, :, MUL:2 * MUL],
                         sum_b[c][:, 0:2, :, MUL:2 * MUL]).then_inc(sum_b_wrapped[c], 1)

            def one_turn(i, first, last):
                for s in range(SLOTS):
                    c = s % 2
                    ahead = not (last and s == SLOTS - 1)
                    if ahead:
                        hide(i, s + 1, again=not (first and s == 0))
                    act.wait_ge(gathered[s], (i + 1) * (16 * PER))
                    act.wait_ge(factors_free[c], turn(i, s, 2))
                    act.copy(factors[c][:, :, 0:MUL], far[s][:, :, 0:MUL]).then_inc(copied, 1)
                    act.activation(minus_local[c][:], rows[s][:, :, 1], ACT.Identity,
                                   bias=first_node[:, bass.ds(i * SLOTS + s, 1)], scale=-1.0).then_inc(copied, 1)
                    act.wait_ge(copied, 1)
                    act.sem_inc(factors_ready[c], 1)
                    act.sem_inc(far_free[s], 1)
                    act.wait_ge(copied, 2)
                    act.sem_inc(rows_free[s], 1)
                    for j in range(PER):
                        act.activation(away[:, j, :], k.iota[:], ACT.Abs,
                                       bias=minus_local[c][:, j:j + 1]).then_inc(copied, 1)
                    if not (first and s == 0):
                        wrap(i, s - 1)
                    if ahead:
                        hidden_done(i, s + 1)
                    if not (first and s < 2):
                        act.wait_ge(part_ready[c], turn(i, s - 2, 2))
                    act.wait_ge(copied, 2 + PER)
                    act.activation(hot[c][:], away[:], ACT.Relu, bias=k.ones[:, 0:1], scale=-1.0
                                   ).then_inc(hot_ready[c], 1)
                    act.sem_clear(copied)
                    act.wait_ge(hot_ready[c], turn(i, s, 2))

            hide(0, 0, again=False)
            hidden_done(0, 0)
            turns(act, one_turn)
            wrap(TURNS - 1, SLOTS - 1)

        @block.tensor
        def _(pe):
            for c in range(2):
                pe.sem_inc(radial_free[c], 1)

            def radial(i, s):
                c = s % 2
                pe.wait_ge(hidden_ready[c], turn(i, s, 2))
                pe.wait_ge(radial_free[c], turn(i, s, 2))
                for j in range(PER):
                    pe.matmul(radial_a[:, c, j, :], hidden[c][:, :, j], k.radial[:, 0:256], start=True, stop=True)
                    last = pe.matmul(radial_b[:, c, j, :], hidden[c][:, :, j], k.radial[:, 256:384],
                                     start=True, stop=True)
                last.then_inc(radial_ready[c], 1)

            def sum_nodes(i, s):
                c = s % 2
                pe.wait_ge(hot_ready[c], turn(i, s, 2))
                pe.wait_ge(message_ready[c], turn(i, s, 2))
                pe.wait_ge(part_free[c], turn(i, s, 2))
                for j in range(PER):
                    last = pe.matmul(part[c][:, 0:F], hot[c][:, j, :],
                                     message[c][:, j, 0:4, :].rearrange("p a u -> p (a u)"),
                                     start=(j == 0), stop=(j == PER - 1))
                last.then_inc(part_ready[c], 1)

            def one_turn(i, first, last):
                for s in range(SLOTS):
                    if not (last and s == SLOTS - 1):
                        radial(i, s + 1)
                    if not (first and s == 0):
                        sum_nodes(i, s - 1)

            radial(0, 0)
            turns(pe, one_turn)
            sum_nodes(TURNS - 1, SLOTS - 1)

        @block.vector
        def _(dve):
            steps = Steps(dve, own)
            step, wait = steps.step, steps.wait
            step(dve.memset(k.sums[:], 0.0))
            wait()
            for c in range(2):
                dve.sem_inc(part_free[c], 1)

            def finish_a(i, s):
                c = s % 2
                dve.wait_ge(folded, i * SLOTS + s + 1)
                return step(dve.tensor_reduce(
                    message[c][:, :, 0:5:4, :], folded_a[:].rearrange("p j (h q) m -> p j h q m", h=2),
                    AX.X, ALU.add))

            def finish_b(i, s):
                dve.wait_ge(radial_free[s % 2], turn(i, s, 2) + 1)
                dve.sem_inc(far_free[s % SLOTS], 1)
                dve.tensor_reduce(sum_b[s % 2][:, 0:3].rearrange("p o j q -> p (o j q)"),
                                  products_b[:].rearrange("p o j q v -> p (o j q) v"),
                                  AX.X, ALU.add).then_inc(sum_b_ready[s % 2], 1)

            def turned(s, at):
                return spread(rows[s % SLOTS][:, :, 3 + at:6 + at].rearrange("p j o -> p o j"), 3, MUL)

            def vector_out(s):
                return message[s % 2][:, :, 1:4, :].rearrange("p j o u -> p o j u")

            def along_r(s):
                return step(dve.tensor_tensor(vector_out(s), turned(s, 0),
                                              spread(message[s % 2][:, :, 4, :], 1, 3), ALU.mult))

            def add_own(s):
                return step(dve.tensor_tensor(vector_out(s), vector_out(s),
                                              sum_b[s % 2][:, 0:3, :, 0:MUL], ALU.add))

            def add_cross(s, part_no, op):
                return dve.tensor_tensor(vector_out(s), vector_out(s), crossed[s % 2][:, part_no], op)

            def cross(s, part_no, r_at, g_at):
                c = s % 2
                return step(dve.tensor_tensor(crossed[c][:, part_no], turned(s, r_at),
                                              sum_b[c][:, g_at:g_at + 3, :, MUL:2 * MUL], ALU.mult))

            def bin_of(i, s):
                return dve.value_load(entry[0:1, bass.ds(i * SLOTS + s, 1), 1], min_val=0, max_val=BINS - 1)

            def accumulate(i, s, at):
                c = s % 2
                dve.wait_ge(part_ready[c], turn(i, s, 2))
                sums = k.sums[:, bass.ds(at * (F + 1), F)]
                return step(dve.tensor_tensor(sums, sums, part[c][:, 0:F], ALU.add))

            def one_group(i, s, before, added):
                c, f = s % 2, far[s]
                p = s - 1
                vectors = f[:, :, MUL:F].rearrange("p j (v o) -> p j v o", o=3)
                dve.wait_ge(gathered[s], (i + 1) * (16 * PER))
                n_along = step(dve.tensor_tensor(along[c][:], vectors, spread(rows[s][:, :, 3:6], 2, MUL),
                                                 ALU.mult))
                if before:
                    finish_b(i, p)
                if added:
                    at = bin_of(i, s - 2)
                if before:
                    n_a = finish_a(i, p)
                wait(n_along)
                n_factors = step(dve.tensor_reduce(factors[c][:, :, MUL:2 * MUL], along[c][:], AX.X, ALU.add))
                if before:
                    wait(n_a)
                    n_out = along_r(p)
                dve.wait_ge(factors_ready[c], turn(i, s, 2))
                dve.wait_ge(radial_ready[c], turn(i, s, 2))
                wait(n_factors)
                n_products = step(dve.tensor_tensor(
                    products_a[:], radial_a[:, c].rearrange("p j (q m) -> p j q m", m=2 * MUL),
                    spread(factors[c][:], 2, 2 * MUL), ALU.mult))
                if before:
                    dve.wait_ge(sum_b_wrapped[p % 2], turn(i, p, 2))
                    cross(p, 0, 1, 2)
                    n_cross = cross(p, 1, 2, 1)
                    wait(n_out)
                    n_out = add_own(p)

                def product_b(o):
                    return dve.tensor_tensor(
                        products_b[:, o], radial_b[:, c].rearrange("p j (q v) -> p j q v", v=MUL),
                        spread(vectors[:, :, :, o], 2, 2 * MUL), ALU.mult)

                step(product_b(0))
                wait(n_products)
                dve.sem_inc(products_made, 1)
                dve.sem_inc(factors_free[c], 1)
                if before:
                    wait(n_out)
                    dve.sem_inc(rows_free[p % SLOTS], 1)
                    n_out = step(add_cross(p, 0, ALU.add))
                if added:
                    n_added = accumulate(i, s - 2, at)
                step(product_b(1))
                if before:
                    wait(n_out)
                    add_cross(p, 1, ALU.subtract).then_inc(message_ready[p % 2], 1)
                if added:
                    wait(n_added)
                    dve.sem_inc(part_free[c], 1)
                product_b(2).then_inc(radial_free[c], 1)

            def one_turn(i, first, last):
                steps.restart()
                for s in range(SLOTS):
                    one_group(i, s, before=not (first and s == 0), added=not (first and s < 2))
                wait()

            turns(dve, one_turn)
            steps.restart()
            i, s = TURNS - 1, SLOTS - 1
            finish_b(i, s)
            n_a = finish_a(i, s)
            wait(n_a)
            along_r(s)
            dve.wait_ge(sum_b_wrapped[s % 2], turn(i, s, 2))
            cross(s, 0, 1, 2)
            cross(s, 1, 2, 1)
            wait()
            add_own(s)
            wait()
            step(add_cross(s, 0, ALU.add))
            wait()
            add_cross(s, 1, ALU.subtract).then_inc(message_ready[s % 2], 1)
            accumulate(i, s - 1, bin_of(i, s - 1))
            wait()
            accumulate(i, s, bin_of(i, s))
            wait()


def last_update(nc, k):
    sums = k.sums[:].rearrange("p (b w) -> p b w", w=F + 1)[:, :, 0:F]

    def before(dve, s):
        s.step(dve.tensor_tensor(k.x[:, :, 0:MUL], k.x[:, :, 0:MUL], sums[:, :, 0:MUL], ALU.add))
        vectors = k.x[:, :, MUL:F].rearrange("p b (u o) -> p b u o", o=3)
        s.step(dve.tensor_tensor(vectors, vectors,
                                 sums[:, :, MUL:F].rearrange("p b (o u) -> p b u o", o=3), ALU.add))
        s.wait()

    normalize(nc, k, "norm3", before=before, store=[(k.out, k.x)])


def gnn_kernel(nc, x, src, dst, edge_attr_3, edge_weight, L0_gnn_W, L0_gnn_b, L1_gnn_w, L1_gnn_fc_w,
               L1_gnn_fc_b, L1_gnn_bias, L3_gnn_w1, L3_gnn_b1, L3_gnn_w2, L3_gnn_b2, out):
    k = Memory()
    k.in_x, k.in_src, k.in_dst, k.in_attr, k.in_weight = x, src, dst, edge_attr_3, edge_weight
    k.in_w0, k.in_b0, k.in_w1, k.in_fc, k.in_fcb, k.in_bias1 = (
        L0_gnn_W, L0_gnn_b, L1_gnn_w, L1_gnn_fc_w, L1_gnn_fc_b, L1_gnn_bias)
    k.in_w3a, k.in_b3a, k.in_w3b, k.in_b3b = L3_gnn_w1, L3_gnn_b1, L3_gnn_w2, L3_gnn_b2
    k.out = out
    k.hops = 0

    def dram(name, shape, dt):
        return nc.dram_tensor(name, shape, dt).ap()

    k.edges_by_dst = dram("edges_by_dst", [EDGES + GROUP, BY_DST], F32)
    k.edges_by_src = dram("edges_by_src", [EDGES + GROUP, BY_SRC], F32)
    k.weight_by_group = dram("weight_by_group", [GROUPS, GROUP], F32)
    k.far_dram = dram("far_rows", [NODES, FAR], F32)
    k.hop_dram = [dram(f"hop_rows{n}", [NODES, F], F32) for n in range(2)]
    k.entry_dram = dram("entries", [TABLE, 2], I32)
    k.node_dram = dram("first_nodes", [TABLE], F32)
    with ExitStack() as ctx:
        def sb(name, shape, dt=F32):
            return ctx.enter_context(nc.sbuf_tensor(name, shape, dt))

        k.iota, k.ident, k.before, k.ones = (sb(n, [P, P]) for n in ("iota", "ident", "before", "ones"))
        k.half_less = sb("half_less", [P, P])
        k.in_order = sb("in_order", [P, 1], I32)
        k.eps = sb("eps", [P, 1])
        k.group_no = sb("group_no", [P, TCOLS])
        k.x = sb("x", [P, BINS, F])
        k.w0, k.b0 = sb("w0", [F, F]), sb("b0", [P, F])
        k.w1, k.w1_by_f = sb("w1", [HEADS * F, F]), sb("w1_by_f", [F, HEADS, F])
        k.fc, k.fcb, k.bias1 = sb("fc", [F, 2 * F]), sb("fcb", [P, 1]), sb("bias1", [P, F])
        k.scorer, k.scorer_parts = sb("scorer", [F, 2 * HEADS]), sb("scorer_parts", [F, HEADS, F])
        k.w3a, k.b3a = sb("w3a", [HIDDEN, 1]), sb("b3a", [HIDDEN, 1])
        k.w3, k.radial = sb("w3", [HIDDEN + 1, RADIAL]), sb("radial", [HIDDEN + 1, RADIAL])
        k.entry = {n: sb(f"entry_{n}", [1, TABLE, 2], I32) for n in ("by_dst",)}
        k.first_node = {n: sb(f"first_node_{n}", [P, TABLE]) for n in ("by_dst",)}
        k.degree, k.degree_root, k.inverse = (sb(n, [P, BINS]) for n in ("degree", "degree_root", "inverse"))
        k.own_score = sb("own_score", [P, BINS, HEADS])
        k.maximum = sb("maximum", [P, BINS * HEADS])
        k.node_terms, k.bounded = sb("node_terms", [P, BINS * 2 * HEADS]), sb("bounded", [P, 1], I32)
        k.update = sb("update", [P, BATCH, F])
        setup(nc, k)
        k.place_i = ctx.enter_context(nc.sbuf_tensor("place_i", [P, COLS], I32))
        with ExitStack() as sorting:
            k.rows = sorting.enter_context(nc.sbuf_tensor("rows_by_dst", [P, COLS, BY_DST], F32))
            by_dst = sort_memory(nc, sorting, "dst")
            pack_edges(nc, k, by_dst)
            order_by_dst(nc, k, by_dst)
        k.entry["by_src"] = sb("entry_by_src", [1, TABLE, 2], I32)
        k.first_node["by_src"] = sb("first_node_by_src", [P, TABLE])
        with nc.sbuf_tensor("sums_first", [P, BINS * (F + 1)], F32) as k.sums, \
                nc.sbuf_tensor("far_rows_sb", [P, BINS, FAR], F32) as k.far_rows:
            with ExitStack() as sorting:
                by_src = sort_memory(nc, sorting, "src")
                by_src.place = sorting.enter_context(nc.sbuf_tensor("src_place", [P, COLS], F32))
                by_src.running = sorting.enter_context(nc.sbuf_tensor("src_running", [P, COLS], F32))
                sum_messages(nc, k, k.in_x, by_src)
            with nc.sbuf_tensor("rows_by_src", [P, COLS, BY_SRC], F32) as rows:
                pack_ends(nc, k, rows)
                order_by_src(nc, k, rows)
            first_update(nc, k)
            bound_scores(nc, k)
        with nc.sbuf_tensor("hop_rows", [P, BINS, F], F32) as k.hop_rows:
            with nc.sbuf_tensor("attention", [P, BINS * HEADS * (F + 1)], F32) as k.attention, \
                    nc.sbuf_tensor("denominator", [P, BATCH, HEADS], F32) as k.denominator, \
                    nc.sbuf_tensor("share", [P, BATCH, HEADS], F32) as k.share:
                attend(nc, k)
                attention_update(nc, k)
            with nc.sbuf_tensor("sums", [P, BINS * (F + 1)], F32) as k.sums:
                sum_messages(nc, k, k.hop_dram[0])
                between_hops(nc, k)
                sum_messages(nc, k, k.hop_dram[1])
                after_hops(nc, k)
                radial_weights(nc, k)
                convolve(nc, k)
                last_update(nc, k)


_INS = ["x", "src", "dst", "edge_attr_3", "edge_weight", "L0_gnn_W", "L0_gnn_b", "L1_gnn_w", "L1_gnn_fc_w",
        "L1_gnn_fc_b", "L1_gnn_bias", "L3_gnn_w1", "L3_gnn_b1", "L3_gnn_w2", "L3_gnn_b2"]


def kernel(**inputs):
    import numpy as _np
    import concourse.bacc as _bacc
    from concourse import mybir as _mybir
    from concourse.bass_utils import run_bass_kernel_spmd as _run

    nc = _bacc.Bacc("TRN2", target_bir_lowering=False, num_devices=1)
    arrays, args = {}, []
    for name in _INS:
        a = _np.ascontiguousarray(inputs[name])
        arrays[f"in_{name}_dram"] = a
        args.append(nc.dram_tensor(f"in_{name}_dram", a.shape, _mybir.dt.from_np(a.dtype), kind="ExternalInput").ap())
    args.append(nc.dram_tensor("out_0_dram", (NODES, F), _mybir.dt.from_np(_np.dtype("float32")),
                               kind="ExternalOutput").ap())
    gnn_kernel(nc, *args)
    r = _run(nc, [arrays], core_ids=[0])
    return r.results[0]["out_0_dram"]
```

```python
from contextlib import ExitStack, contextmanager
from math import pi, sqrt

import concourse.bass as bass
from concourse import mybir

F32 = mybir.dt.float32
I32 = mybir.dt.int32
U16 = mybir.dt.uint16
BF16 = mybir.dt.bfloat16
ALU = mybir.AluOpType
ACT = mybir.ActivationFunctionType
AX = mybir.AxisListType

P = 128
NODES = 12500
EDGES = 400000
F = 32
HEADS = 4
HIDDEN = 64
RADIAL = 384
BINS = -(-NODES // P)
LAST = NODES - (BINS - 1) * P
COLS = EDGES // P
PER = 4
GROUP = P * PER
SLOTS = 4
PIECES = {"by_dst": 2, "by_src": 1}


def turns_for(pieces):
    piece = GROUP // pieces
    return -(-((EDGES + BINS * (piece - 1)) // piece) // (pieces * SLOTS))


TURNS = {name: turns_for(pieces) for name, pieces in PIECES.items()}
HALVES, PIECE, COLUMNS = PIECES["by_dst"], GROUP // PIECES["by_dst"], PER // PIECES["by_dst"]
TABLE = P * -(-max(TURNS[n] * SLOTS * PIECES[n] for n in PIECES) // P)
TCOLS = TABLE // P
BY_DST = 8
BY_SRC = 2
FAR = 40
BIG = 1e30
EPS = 1e-5
BATCH = 7
MUL = 8
COUNTING = 24
RANGE = 50.0
AHEAD = 2


@contextmanager
def stage(nc, k):
    made = []

    def sem(name):
        made.append(nc.alloc_semaphore(name))
        return made[-1]

    k.sem = sem
    with ExitStack() as ctx:
        yield ctx
    nc.clear_and_free_semaphores(made)
    nc.all_engine_barrier()


class Memory:
    pass


class Steps:

    def __init__(self, engine, semaphore):
        self.engine, self.semaphore, self.n = engine, semaphore, 0

    def restart(self):
        self.engine.sem_clear(self.semaphore)
        self.n = 0

    def step(self, instruction):
        instruction.then_inc(self.semaphore, 1)
        self.n += 1
        return self.n

    def wait(self, n=None):
        self.engine.wait_ge(self.semaphore, self.n if n is None else n)


def spread(ap, axis, n):
    ap = ap.unsqueeze(axis)
    shape = list(ap.shape)
    shape[axis] = n
    return ap.broadcast_to(shape)


def turn(i, slot, of):
    return i * (SLOTS // of) + slot // of + 1


def turns(engine, name, one_turn):
    one_turn(0, True, False)
    with engine.Fori(1, TURNS[name] - 1) as i:
        one_turn(i, False, False)
    one_turn(TURNS[name] - 1, False, True)


def node_rows(table):
    whole = table[0:(BINS - 1) * P, :].rearrange("(b p) f -> p b f", p=P)
    return whole, table[(BINS - 1) * P:NODES, :]


def setup(nc, k):
    with stage(nc, k) as ctx:
        made = k.sem("constants_made")
        cleared = k.sem("constants_cleared")
        padded = k.sem("last_bin_cleared")
        loaded = k.sem("setup_loaded")
        block = ctx.enter_context(nc.Block())

        @block.gpsimd
        def _(pool):
            pool.iota(k.iota[:], pattern=[[1, P]], base=0, channel_multiplier=0,
                      allow_small_or_imprecise_dtypes=True).then_inc(made, 1)
            pool.iota(k.piece_no[:], pattern=[[1, TCOLS]], base=0, channel_multiplier=TCOLS,
                      allow_small_or_imprecise_dtypes=True).then_inc(made, 1)
            pool.memset(k.ident[:], 0.0).then_inc(cleared, 1)
            pool.memset(k.before[:], 1.0).then_inc(cleared, 1)
            pool.memset(k.ones[:], 1.0).then_inc(made, 1)
            pool.memset(k.eps[:], EPS).then_inc(made, 1)
            pool.wait_ge(cleared, 2)
            pool.affine_select(out=k.ident[:], in_=k.ident[:], compare_op=ALU.not_equal, fill=1.0,
                               base=0, pattern=[[-1, P]], channel_multiplier=1).then_inc(made, 1)
            pool.affine_select(out=k.before[:], in_=k.before[:], compare_op=ALU.is_gt, fill=0.0,
                               base=0, pattern=[[1, P]], channel_multiplier=-1).then_inc(made, 1)
            pool.wait_ge(made, 6)

        @block.vector
        def _(dve):
            dve.memset(k.x[:, BINS - 1, :], 0.0).then_inc(padded, 1)
            dve.wait_ge(made, 6)
            dve.tensor_scalar(k.half_less[:], k.iota[:], -1.0, 0.5, ALU.mult, ALU.add).then_inc(padded, 1)
            dve.wait_ge(padded, 2)

        @block.sync
        def _(sp):
            whole, last = node_rows(k.in_x)
            sp.dma_start(k.x[:, 0:BINS - 1, :], whole).then_inc(loaded, 16)
            sp.wait_ge(padded, 1)
            sp.dma_start(k.x[0:LAST, BINS - 1, :], last).then_inc(loaded, 16)
            sp.dma_start(k.w0[:], k.in_w0).then_inc(loaded, 16)
            sp.dma_start(k.b0[:], k.in_b0.partition_broadcast(P)).then_inc(loaded, 16)
            sp.dma_start(k.w1[:], k.in_w1.rearrange("h f o -> (h f) o")).then_inc(loaded, 16)
            sp.dma_start(k.w1_by_f[:], k.in_w1.rearrange("h f o -> f h o")).then_inc(loaded, 16)
            sp.dma_start(k.fc[:], k.in_fc[0, :].partition_broadcast(F)).then_inc(loaded, 16)
            sp.dma_start(k.fcb[:], k.in_fcb.partition_broadcast(P)).then_inc(loaded, 16)
            sp.dma_start(k.bias1[:], k.in_bias1.partition_broadcast(P)).then_inc(loaded, 16)
            sp.dma_start(k.w3a[:], k.in_w3a.rearrange("a h -> h a")).then_inc(loaded, 16)
            sp.dma_start(k.b3a[:], k.in_b3a.rearrange("(h a) -> h a", a=1)).then_inc(loaded, 16)
            sp.dma_start(k.w3[0:HIDDEN, :], k.in_w3b).then_inc(loaded, 16)
            sp.dma_start(k.w3[HIDDEN:HIDDEN + 1, :],
                         k.in_b3b.rearrange("(a r) -> a r", a=1)).then_inc(loaded, 16)
            sp.wait_ge(loaded, 16 * 13)


def pack_edges(nc, k, q):
    CHUNKS = 5
    CHUNK = COLS // CHUNKS
    with stage(nc, k) as ctx:
        attr = ctx.enter_context(nc.sbuf_tensor("attr", [P, CHUNK, 3], F32))
        weight = ctx.enter_context(nc.sbuf_tensor("weight_chunk", [P, CHUNK], F32))
        norm = ctx.enter_context(nc.sbuf_tensor("attr_norm", [P, 2, CHUNK], F32))
        key = ctx.enter_context(nc.sbuf_tensor("edge_key", [P, COLS], I32))
        tail = ctx.enter_context(nc.sbuf_tensor("tail", [P, PER, BY_DST], F32))
        ends = ctx.enter_context(nc.sbuf_tensor("edge_ends", [P, 4], F32))
        next_key = ctx.enter_context(nc.sbuf_tensor("next_key", [P, 1], I32))
        sums = ctx.enter_context(nc.psum_tensor("dst_sums", [P, 2, 512], F32))
        in_order = ctx.enter_context(nc.psum_tensor("order_flags", [P, 512], F32))
        chunk_loaded = k.sem("chunk_loaded")
        src_loaded, dst_loaded, next_loaded = (k.sem(n) for n in ("src_loaded", "dst_loaded", "next_loaded"))
        src_used, next_cleared = k.sem("src_used"), k.sem("next_cleared")
        squares_summed = k.sem("squares_summed")
        root_taken = k.sem("root_taken")
        chunk_packed = k.sem("chunk_packed")
        bins_ready, counted, counts_found = (k.sem(n) for n in ("bins_ready", "counted", "counts_found"))
        summed, order_found, order_summed = (k.sem(n) for n in ("summed", "order_found", "order_summed"))
        table_made, table_stored, table_loaded = (k.sem(n) for n in ("table_made", "table_stored", "table_loaded"))
        own, count_steps = k.sem("pack_steps"), k.sem("count_steps")
        tail_made = k.sem("tail_made")
        tail_stored = k.sem("tail_stored")
        block = ctx.enter_context(nc.Block())
        attr_in = k.in_attr.rearrange("(p t) c -> p t c", p=P)
        weight_in = k.in_weight.rearrange("(p t) -> p t", p=P)
        dst_in = k.in_dst.rearrange("(p t) -> p t", p=P)

        @block.sync
        def _(sp):
            sp.dma_start(k.place_i[:], dst_in).then_inc(dst_loaded, 16)
            sp.dma_start(key[:], k.in_src.rearrange("(p t) -> p t", p=P)).then_inc(src_loaded, 16)
            sp.wait_ge(next_cleared, 1)
            sp.dma_start(next_key[0:P - 1, :], dst_in[1:P, 0:1], allow_slow_non_contiguous=True).then_inc(next_loaded, 16)
            for c in range(CHUNKS):
                if c:
                    sp.wait_ge(chunk_packed, c)
                sp.dma_start(attr[:], attr_in[:, c * CHUNK:(c + 1) * CHUNK, :]).then_inc(chunk_loaded, 16)
                sp.dma_start(weight[:], weight_in[:, c * CHUNK:(c + 1) * CHUNK]).then_inc(chunk_loaded, 16)
            sp.wait_ge(tail_made, 2)
            sp.dma_start(k.edges_by_dst[EDGES:EDGES + GROUP, :].rearrange("(p j) w -> p j w", p=P),
                         tail[:]).then_inc(tail_stored, 16)
            sp.dma_start(k.edges_by_src[EDGES:EDGES + GROUP, :].rearrange("(p j) w -> p j w", p=P),
                         tail[:, :, 0:BY_SRC]).then_inc(tail_stored, 16)
            sp.wait_ge(tail_stored, 32)
            move_table(sp, k, q, "by_dst", table_made, table_stored, table_loaded)

        @block.gpsimd
        def _(pool):
            pool.memset(next_key[:], 1 << 20).then_inc(next_cleared, 1)
            pool.memset(tail[:], 0.0).then_inc(tail_made, 1)
            pool.wait_ge(tail_made, 1)
            pool.memset(tail[:, :, 1], -1.0).then_inc(tail_made, 1)

        @block.scalar
        def _(act):
            act.wait_ge(bins_ready, 1)
            for c in range(CHUNKS):
                act.wait_ge(squares_summed, c + 1)
                act.activation(norm[:, 1, :], norm[:, 0, :], ACT.Sqrt).then_inc(root_taken, 1)
                count_bins(act, k, q, count_steps, (BINS + 1) * c // CHUNKS, (BINS + 1) * (c + 1) // CHUNKS)
            act.sem_inc(counted, 1)

        @block.tensor
        def _(pe):
            pe.wait_ge(order_found, 1)
            pe.matmul(in_order[:, 0:1], k.ones[:], ends[:, 3:4], start=True, stop=True).then_inc(order_summed, 1)
            pe.wait_ge(counts_found, 1)
            sum_counts(pe, k, q, sums, summed)

        @block.vector
        def _(dve):
            s = Steps(dve, own)
            dve.wait_ge(src_loaded, 16)
            s.step(dve.tensor_copy(k.rows[:, :, 0].bitcast(I32), key[:]))
            dve.wait_ge(dst_loaded, 16)
            s.step(dve.tensor_copy(k.rows[:, :, 1], k.place_i[:]))
            s.wait()
            difference = key[:].bitcast(F32)[:, 0:COLS - 1]
            s.step(dve.tensor_tensor(difference, k.place_i[:, 1:COLS], k.place_i[:, 0:COLS - 1], ALU.subtract))
            dve.wait_ge(next_loaded, 16)
            s.step(dve.tensor_tensor(ends[:, 0:1], next_key[:], k.place_i[:, COLS - 1:COLS], ALU.subtract))
            s.wait()
            s.step(dve.tensor_reduce(ends[:, 1:2], difference, AX.X, ALU.min))
            s.wait()
            s.step(dve.tensor_tensor(ends[:, 2:3], ends[:, 0:1], ends[:, 1:2], ALU.min))
            s.wait()
            s.step(dve.tensor_scalar(ends[:, 3:4], ends[:, 2:3], 0.0, None, ALU.is_ge))
            s.wait()
            dve.sem_inc(order_found, 1)
            cut_bins(dve, s, k, q)
            dve.sem_inc(bins_ready, 1)
            dve.wait_ge(order_summed, 1)
            s.step(dve.tensor_scalar(k.in_order[:], in_order[:, 0:1], P - 0.5, None, ALU.is_ge))
            for c in range(CHUNKS):
                cut = slice(c * CHUNK, (c + 1) * CHUNK)
                dve.wait_ge(chunk_loaded, 32 * (c + 1))
                s.step(dve.tensor_copy(k.rows[:, cut, 2], weight[:]))
                square = k.rows[:, cut, 3:6]
                s.step(dve.tensor_tensor(square, attr[:], attr[:], ALU.mult))
                s.wait()
                dve.tensor_reduce(norm[:, 0, :], square, AX.X, ALU.add).then_inc(squares_summed, 1)
                dve.wait_ge(root_taken, c + 1)
                s.step(dve.reciprocal(norm[:, 0, :], norm[:, 1, :]))
                s.wait()
                inverse = norm[:, 0, :].unsqueeze(2)
                s.step(dve.tensor_tensor(k.rows[:, cut, 3:5], attr[:, :, 1:3],
                                         inverse.broadcast_to([P, CHUNK, 2]), ALU.mult))
                s.step(dve.tensor_tensor(k.rows[:, cut, 5:6], attr[:, :, 0:1], inverse, ALU.mult))
                s.step(dve.tensor_tensor(k.rows[:, cut, 6:8], attr[:, :, 1:3],
                                         inverse.broadcast_to([P, CHUNK, 2]), ALU.mult))
                s.wait()
                dve.sem_inc(chunk_packed, 1)
            dve.wait_ge(counted, 1)
            find_counts(dve, s, q)
            dve.sem_inc(counts_found, 1)
            dve.wait_ge(summed, 1)
            make_table(dve, s, k, q, sums, "by_dst")
            dve.sem_inc(table_made, 1)


def sort_memory(nc, ctx, name):
    def sb(n, shape, dt=F32):
        return ctx.enter_context(nc.sbuf_tensor(f"{name}_{n}", shape, dt))

    q = Memory()
    q.bins, q.mine = sb("bins", [P, COLS], BF16), sb("mine", [P, COLS], U16)
    q.signs = sb("signs", [P, BINS + 1])
    q.count, q.total, q.start, q.first = (sb(n, [P, BINS]) for n in ("count", "total", "start", "first"))
    q.pieces, q.last_piece, q.shift = (sb(n, [P, BINS]) for n in ("pieces", "last_piece", "shift"))
    q.pieces_i = sb("pieces_i", [P, BINS], I32)
    q.passed = sb("passed", [P, TCOLS, BINS - 1])
    q.bin_of, q.start_of, q.node_of = (sb(n, [P, TCOLS]) for n in ("bin_of", "start_of", "node_of"))
    q.entry = sb("entry_made", [P, TCOLS, 2], I32)
    return q


def cut_bins(dve, s, k, q):
    s.step(dve.tensor_scalar(k.place_i[:], k.place_i[:], P.bit_length() - 1, None, ALU.logical_shift_right))
    s.wait()
    s.step(dve.tensor_copy(q.bins[:], k.place_i[:]))
    s.wait()


def count_bins(act, k, q, steps, first=0, end=BINS + 1):
    with act.Fori(first, end) as b:
        act.sem_clear(steps)
        act.activation(q.mine[:].bitcast(BF16), q.bins[:], ACT.Sign, bias=k.half_less[:, bass.ds(b, 1)],
                       accum_out=q.signs[:, bass.ds(b, 1)]).then_inc(steps, 1)
        act.wait_ge(steps, 1)


def find_counts(dve, s, q):
    s.step(dve.tensor_scalar(q.signs[:], q.signs[:], float(COLS), 0.5, ALU.add, ALU.mult))
    s.wait()
    s.step(dve.tensor_tensor(q.count[:], q.signs[:, 0:BINS], q.signs[:, 1:BINS + 1], ALU.subtract))
    s.wait()


def sum_counts(pe, k, q, sums, summed):
    pe.matmul(sums[:, 0, 0:BINS], k.ones[:], q.count[:], start=True, stop=True)
    pe.matmul(sums[:, 1, 0:BINS], k.before[:], q.count[:], start=True, stop=True).then_inc(summed, 1)


def make_table(dve, s, k, q, sums, name):
    piece = GROUP // PIECES[name]
    one = k.ones[:, 0:1].broadcast_to([P, BINS])
    s.step(dve.tensor_copy(q.total[:], sums[:, 0, 0:BINS]))
    s.wait()
    s.step(dve.tensor_tensor_scan(q.start[:], one, q.total[:], 0.0, ALU.mult, ALU.add))
    s.wait()
    s.step(dve.tensor_tensor(q.start[:], q.start[:], q.total[:], ALU.subtract))
    s.wait()
    s.step(dve.scalar_tensor_tensor(q.first[:], q.start[:], -1.0, sums[:, 1, 0:BINS], ALU.add, ALU.add))
    s.step(dve.tensor_scalar(q.pieces_i[:], q.total[:], float(piece - 1), None, ALU.add))
    s.wait()
    s.step(dve.tensor_scalar(q.pieces_i[:], q.pieces_i[:], piece.bit_length() - 1, None,
                             ALU.logical_shift_right))
    s.wait()
    s.step(dve.tensor_copy(q.pieces[:], q.pieces_i[:]))
    s.wait()
    s.step(dve.tensor_tensor_scan(q.last_piece[:], one, q.pieces[:], 0.0, ALU.mult, ALU.add))
    s.wait()
    s.step(dve.tensor_tensor(q.shift[:], q.last_piece[:], q.pieces[:], ALU.subtract))
    s.wait()
    s.step(dve.scalar_tensor_tensor(q.shift[:], q.shift[:], -float(piece), q.start[:], ALU.mult, ALU.add))
    s.wait()
    s.step(dve.tensor_tensor(q.pieces[:, 0:BINS - 1], q.shift[:, 1:BINS], q.shift[:, 0:BINS - 1],
                             ALU.subtract))
    s.step(dve.tensor_tensor(q.passed[:], spread(q.last_piece[:, 0:BINS - 1], 1, TCOLS),
                             spread(k.piece_no[:], 2, BINS - 1), ALU.is_le))
    s.wait()
    s.step(dve.tensor_reduce(q.bin_of[:], q.passed[:], AX.X, ALU.add))
    s.wait()
    s.step(dve.tensor_tensor(q.passed[:], q.passed[:], spread(q.pieces[:, 0:BINS - 1], 1, TCOLS), ALU.mult))
    s.wait()
    s.step(dve.tensor_reduce(q.start_of[:], q.passed[:], AX.X, ALU.add))
    s.wait()
    s.step(dve.scalar_tensor_tensor(q.start_of[:], k.piece_no[:], float(piece), q.start_of[:],
                                    ALU.mult, ALU.add))
    s.wait()
    s.step(dve.tensor_scalar(q.entry[:, :, 0], q.start_of[:], float(EDGES), None, ALU.min))
    s.step(dve.tensor_copy(q.entry[:, :, 1], q.bin_of[:]))
    s.step(dve.tensor_scalar(q.node_of[:], q.bin_of[:], float(P), None, ALU.mult))
    s.wait()


def move_table(queue, k, q, name, made, stored, loaded):
    queue.wait_ge(made, 1)
    queue.dma_start(k.entry_dram[:, :].rearrange("(p c) e -> p c e", p=P), q.entry[:]).then_inc(stored, 16)
    queue.dma_start(k.node_dram[:].rearrange("(p c) -> p c", p=P), q.node_of[:]).then_inc(stored, 16)
    queue.wait_ge(stored, 32)
    queue.dma_start(k.entry[name][0:1, :, :], k.entry_dram.unsqueeze(0)).then_inc(loaded, 16)
    queue.dma_start(k.first_node[name][:], k.node_dram.partition_broadcast(P)).then_inc(loaded, 16)
    queue.wait_ge(loaded, 32)


def mark_bin(dve, s, q, number):
    s.restart()
    s.step(dve.tensor_scalar(q.mine[:], q.bins[:], number, None, ALU.is_equal))


def rank_bin(dve, s, k, q, first):
    s.wait()
    s.step(dve.tensor_tensor_scan(q.running[:], k.ones[:, 0:1].broadcast_to([P, COLS]), q.mine[:],
                                  first, ALU.mult, ALU.add))


def keep_places(dve, s, q):
    s.wait()
    s.step(dve.copy_predicated(q.place[:], q.mine[:], q.running[:]))


def place_bin(dve, s, k, q, b):
    mark_bin(dve, s, q, k.iota[:, bass.ds(b, 1)])
    rank_bin(dve, s, k, q, q.first[:, bass.ds(b, 1)])
    keep_places(dve, s, q)
    s.wait()


def pack_ends(nc, k, rows):
    with stage(nc, k) as ctx:
        keys = [ctx.enter_context(nc.sbuf_tensor(f"ends{n}", [P, COLS], I32)) for n in range(2)]
        loaded = k.sem("ends_loaded")
        packed = k.sem("ends_packed")
        block = ctx.enter_context(nc.Block())

        @block.sync
        def _(sp):
            sp.dma_start(keys[0][:], k.in_dst.rearrange("(p t) -> p t", p=P)).then_inc(loaded, 16)
            sp.dma_start(keys[1][:], k.in_src.rearrange("(p t) -> p t", p=P)).then_inc(loaded, 16)

        @block.vector
        def _(dve):
            dve.wait_ge(loaded, 32)
            dve.tensor_copy(rows[:, :, 0].bitcast(I32), keys[0][:]).then_inc(packed, 1)
            dve.tensor_copy(rows[:, :, 1], keys[1][:]).then_inc(packed, 1)
            dve.wait_ge(packed, 2)


RUN = 25
HALF = [13, 12]
AT = [0, 13]
ROUNDS = COLS // RUN


def scatter_memory(nc, k, ctx, width, name):
    m = Memory()
    m.index = [ctx.enter_context(nc.sbuf_tensor(f"{name}_index{s}", [P, HALF[s]], I32)) for s in range(2)]
    m.row = [ctx.enter_context(nc.sbuf_tensor(f"{name}_row{s}", [P, HALF[s], width], F32)) for s in range(2)]
    m.staged = [k.sem(f"{name}_staged{s}") for s in range(2)]
    m.written = [k.sem(f"{name}_written{s}") for s in range(2)]
    return m


def stage_rows(sp, k, m, rows):
    def fetch(i, s):
        at = i * RUN + AT[s]
        sp.dma_start(m.index[s][:], k.place_i[:, bass.ds(at, HALF[s])]).then_inc(m.staged[s], 16)
        sp.dma_start(m.row[s][:], rows[:, bass.ds(at, HALF[s]), :]).then_inc(m.staged[s], 16)

    fetch(0, 0)
    fetch(0, 1)
    with sp.Fori(0, ROUNDS - 1) as i:
        for s in range(2):
            sp.wait_ge(m.written[s], (i + 1) * (16 * HALF[s]))
            fetch(i + 1, s)


def write_rows(pool, m, table):
    with pool.Fori(0, ROUNDS):
        for s in range(2):
            pool.wait_ge(m.staged[s], 32)
            pool.sem_clear(m.staged[s])
            for j in range(HALF[s]):
                pool.indirect_dma_start(
                    table, bass.IndirectOffsetOnAxis(ap=m.index[s][:, j:j + 1], axis=0),
                    m.row[s][:, j, :], None).then_inc(m.written[s], 16)
    for s in range(2):
        pool.wait_ge(m.written[s], 16 * HALF[s] * ROUNDS)


def order_by_dst(nc, k, q):
    with stage(nc, k) as ctx:
        q.place = ctx.enter_context(nc.sbuf_tensor("dst_place", [P, COLS], F32))
        q.running = ctx.enter_context(nc.sbuf_tensor("dst_running", [P, COLS], F32))
        m = scatter_memory(nc, k, ctx, BY_DST, "dst")
        own, places_ready, copied = k.sem("dst_place_steps"), k.sem("dst_places_ready"), k.sem("dst_rows_copied")
        block = ctx.enter_context(nc.Block())

        def in_order(engine):
            return engine.value_load(k.in_order[0:1, 0:1], min_val=0, max_val=1) == 1

        @block.sync
        def _(sp):
            with sp.If(in_order(sp)):
                sp.dma_start(k.edges_by_dst[0:EDGES, :].rearrange("(p t) w -> p t w", p=P),
                             k.rows[:]).then_inc(copied, 16)
                sp.wait_ge(copied, 16)
            with sp.Else():
                sp.wait_ge(places_ready, 1)
                stage_rows(sp, k, m, k.rows)

        @block.gpsimd
        def _(pool):
            with pool.If(in_order(pool)):
                pool.nop()
            with pool.Else():
                write_rows(pool, m, k.edges_by_dst)

        @block.vector
        def _(dve):
            s = Steps(dve, own)
            with dve.If(in_order(dve)):
                dve.nop()
            with dve.Else():
                s.step(dve.memset(q.place[:], 0.0))
                s.wait()
                with dve.Fori(0, BINS) as b:
                    place_bin(dve, s, k, q, b)
                s.restart()
                s.step(dve.tensor_copy(k.place_i[:], q.place[:]))
                s.wait()
                dve.sem_inc(places_ready, 1)


def order_by_src(nc, k, rows):
    with stage(nc, k) as ctx:
        m = scatter_memory(nc, k, ctx, BY_SRC, "src")
        vector, tensor, scalar = first_update_parts(nc, k, ctx)
        block = ctx.enter_context(nc.Block())

        @block.sync
        def _(sp):
            stage_rows(sp, k, m, rows)

        @block.gpsimd
        def _(pool):
            write_rows(pool, m, k.edges_by_src)

        @block.vector
        def _(dve):
            vector(dve)

        @block.tensor
        def _(pe):
            tensor(pe)

        @block.scalar
        def _(act):
            scalar(act)


def load_pieces(sp, k, i, s, rows, loaded):
    for h in range(HALVES):
        at = sp.value_load(k.entry["by_dst"][0:1, bass.ds((i * SLOTS + s) * HALVES + h, 1), 0],
                           min_val=0, max_val=EDGES)
        sp.dma_start(rows[:, h * COLUMNS:(h + 1) * COLUMNS, :],
                     k.edges_by_dst[bass.ds(at, PIECE), :].rearrange("(p j) w -> p j w", p=P)).then_inc(loaded, 16)


def bin_of(engine, k, i, s, h):
    return engine.value_load(k.entry["by_dst"][0:1, bass.ds((i * SLOTS + s) * HALVES + h, 1), 1],
                             min_val=0, max_val=BINS - 1)


def sum_messages(nc, k, table, q=None):
    first = q is not None
    width = F + 1 if first else F
    name = "weighted" if first else f"hop_{k.hops}"
    k.hops += 1
    with stage(nc, k) as ctx:
        def sb(n, shape, dt):
            return [ctx.enter_context(nc.sbuf_tensor(f"{name}_{n}{s}", shape, dt)) for s in range(SLOTS)]

        def sem(n):
            return [k.sem(f"{name}_{n}{s}") for s in range(SLOTS)]

        rows = sb("rows", [P, PER, BY_DST], F32)
        far = sb("far", [P, PER, F], F32)
        hot = sb("hot", [P, PER, P], F32)
        local = sb("local", [P, PER], F32)
        message = sb("message", [P, PER, width], F32) if first else far
        weight = sb("weight", [P, PER], F32) if first else None
        part = [ctx.enter_context(nc.psum_tensor(f"{name}_part{s}", [P, 512], F32)) for s in range(SLOTS)]
        rows_in = sem("rows_in")
        rows_free = sem("rows_free")
        gathered = sem("gathered")
        far_free = sem("far_free")
        message_ready = sem("message_ready")
        message_free = sem("message_free")
        part_ready = sem("part_ready")
        part_free = sem("part_free")
        weight_saved = sem("weight_saved") if first else None
        if first:
            sums = ctx.enter_context(nc.psum_tensor("src_sums", [P, 2, 512], F32))
            src_loaded, bins_ready, counted, counts_found, summed, table_made, table_stored, table_loaded, \
                count_steps, sort_steps = (k.sem(f"sort_src_{n}") for n in (
                    "loaded", "bins_ready", "counted", "counts_found", "summed", "table_made",
                    "table_stored", "table_loaded", "count_steps", "sort_steps"))
        own = k.sem(f"{name}_vector_steps")
        added = k.sem(f"{name}_added")
        cleared = k.sem(f"{name}_cleared")
        block = ctx.enter_context(nc.Block())
        entry, first_node = k.entry["by_dst"], k.first_node["by_dst"]

        @block.sync
        def _(sp):
            if first:
                sp.dma_start(k.place_i[:], k.in_src.rearrange("(p t) -> p t", p=P)).then_inc(src_loaded, 16)

            def load(i, s):
                load_pieces(sp, k, i, s, rows[s], rows_in[s])

            def retire(i, s):
                sp.wait_ge(rows_free[s], 1)
                sp.sem_clear(rows_free[s])
                if first:
                    sp.dma_start(k.weight_by_group[bass.ds(i * SLOTS + s, 1), :].rearrange(
                        "g (p j) -> (g p) j", p=P), weight[s][:]).then_inc(weight_saved[s], 16)

            for s in range(SLOTS):
                load(0, s)
            with sp.Fori(0, TURNS["by_dst"] - 1) as i:
                for s in range(SLOTS):
                    retire(i, s)
                    load(i + 1, s)
            for s in range(SLOTS):
                retire(TURNS["by_dst"] - 1, s)
            if first:
                for s in range(SLOTS):
                    sp.wait_ge(weight_saved[s], 16 * TURNS["by_dst"])

        @block.gpsimd
        def _(pool):
            for s in range(SLOTS):
                pool.sem_inc(far_free[s], 1)
            with pool.Fori(0, TURNS["by_dst"]):
                for s in range(SLOTS):
                    pool.wait_ge(rows_in[s], 16 * HALVES)
                    pool.sem_clear(rows_in[s])
                    pool.wait_ge(far_free[s], 1)
                    pool.sem_clear(far_free[s])
                    for j in range(PER):
                        pool.indirect_dma_start(
                            far[s][:, j, :], None, table,
                            bass.IndirectOffsetOnAxis(ap=rows[s][:, j, 0:1].bitcast(I32), axis=0)
                        ).then_inc(gathered[s], 16)

        @block.vector
        def _(dve):
            own_steps = Steps(dve, own)
            dve.memset(k.sums[:], 0.0).then_inc(cleared, 1)
            if first:
                for s in range(SLOTS):
                    dve.memset(message[s][:], 1.0).then_inc(cleared, 1)
                dve.wait_ge(cleared, 1 + SLOTS)
            else:
                dve.wait_ge(cleared, 1)
            if first:
                sort = Steps(dve, sort_steps)
                dve.wait_ge(src_loaded, 16)
                sort.step(dve.memset(q.place[:], 0.0))
                cut_bins(dve, sort, k, q)
                dve.sem_inc(bins_ready, 1)
            for s in range(SLOTS):
                dve.sem_inc(part_free[s], 1)
                dve.sem_inc(message_free[s], 1)

            def select(i, s, again=True):
                own_steps.restart()
                dve.wait_ge(gathered[s], (i + 1) * (16 * PER))
                dve.wait_ge(message_free[s], i + 1)
                own_steps.step(dve.tensor_tensor(
                    local[s][:].rearrange("p (h j) -> p h j", h=HALVES),
                    rows[s][:, :, 1].rearrange("p (h j) -> p h j", h=HALVES),
                    spread(first_node[:, bass.ds((i * SLOTS + s) * HALVES, HALVES)], 2, COLUMNS), ALU.subtract))
                if first:
                    own_steps.step(dve.tensor_tensor(message[s][:, :, 0:F], far[s][:],
                                                     spread(rows[s][:, :, 2], 2, F), ALU.mult))
                    if again:
                        dve.wait_ge(weight_saved[s], i * 16)
                    own_steps.step(dve.tensor_copy(weight[s][:], rows[s][:, :, 2]))
                own_steps.wait(1)
                own_steps.step(dve.tensor_tensor(hot[s][:], spread(k.iota[:], 1, PER),
                                                 spread(local[s][:], 2, P), ALU.is_equal))
                own_steps.wait()
                dve.sem_inc(message_ready[s], 1)
                dve.sem_inc(rows_free[s], 1)
                if first:
                    dve.sem_inc(far_free[s], 1)

            def bins_of(i, s):
                return [bin_of(dve, k, i, s, h) for h in range(HALVES)]

            def accumulate(i, s, bins):
                dve.wait_ge(part_ready[s], i + 1)
                for h, at in enumerate(bins):
                    n = s * HALVES + h
                    if n:
                        dve.wait_ge(added, n)
                    sums = k.sums[:, bass.ds(at * (F + 1), width)]
                    dve.tensor_tensor(sums, sums, part[s][:, h * width:(h + 1) * width],
                                      ALU.add).then_inc(added, 1)
                dve.wait_ge(added, (s + 1) * HALVES)
                dve.sem_inc(part_free[s], 1)

            def one_turn(i, again=True, place=None):
                dve.sem_clear(added)
                bins = {}
                for s in range(SLOTS):
                    select(i, s, again)
                    if place is not None:
                        if s == 0:
                            mark_bin(dve, sort, q, k.iota[:, bass.ds(place, 1)])
                        elif s == 1:
                            rank_bin(dve, sort, k, q, q.first[:, bass.ds(place, 1)])
                        elif s == SLOTS - 1:
                            keep_places(dve, sort, q)
                    if s % 2:
                        for n in (s - 1, s):
                            bins[n] = bins_of(i, n)
                        accumulate(i, s - 1, bins[s - 1])
                    elif s:
                        accumulate(i, s - 1, bins[s - 1])
                accumulate(i, SLOTS - 1, bins[SLOTS - 1])
                if place is not None:
                    sort.wait()

            if not first:
                with dve.Fori(0, TURNS["by_dst"]) as i:
                    one_turn(i)
                return
            one_turn(0, again=False)
            with dve.Fori(1, COUNTING) as i:
                one_turn(i)
            sort.restart()
            dve.wait_ge(counted, 1)
            find_counts(dve, sort, q)
            dve.sem_inc(counts_found, 1)
            dve.wait_ge(summed, 1)
            make_table(dve, sort, k, q, sums, "by_src")
            dve.sem_inc(table_made, 1)
            with dve.Fori(COUNTING, COUNTING + BINS) as i:
                one_turn(i, place=i - COUNTING)
            sort.restart()
            sort.step(dve.tensor_copy(k.place_i[:], q.place[:]))
            with dve.Fori(COUNTING + BINS, TURNS["by_dst"]) as i:
                one_turn(i)
            sort.wait()

        @block.tensor
        def _(pe):
            def one_turn(i):
                for s in range(SLOTS):
                    pe.wait_ge(message_ready[s], i + 1)
                    if not first:
                        pe.wait_ge(gathered[s], (i + 1) * (16 * PER))
                    pe.wait_ge(part_free[s], i + 1)
                    for j in range(PER):
                        h = j // COLUMNS
                        last = pe.matmul(part[s][:, h * width:(h + 1) * width], hot[s][:, j, :],
                                         message[s][:, j, :], start=(j % COLUMNS == 0),
                                         stop=(j % COLUMNS == COLUMNS - 1))
                    last.then_inc(part_ready[s], 1)
                    pe.wait_ge(part_ready[s], i + 1)
                    pe.sem_inc(message_free[s], 1)
                    if not first:
                        pe.sem_inc(far_free[s], 1)

            if not first:
                with pe.Fori(0, TURNS["by_dst"]) as i:
                    one_turn(i)
                return
            with pe.Fori(0, COUNTING) as i:
                one_turn(i)
            pe.wait_ge(counts_found, 1)
            sum_counts(pe, k, q, sums, summed)
            with pe.Fori(COUNTING, TURNS["by_dst"]) as i:
                one_turn(i)

        @block.scalar
        def _(act):
            if not first:
                return
            act.wait_ge(bins_ready, 1)
            count_bins(act, k, q, count_steps)
            act.sem_inc(counted, 1)
            move_table(act, k, q, "by_src", table_made, table_stored, table_loaded)

def project_parts(nc, k, ctx, name, source, depth, weights, width, finish):
    def sem(n):
        return k.sem(f"{name}_{n}")

    staged = ctx.enter_context(nc.sbuf_tensor(f"{name}_staged", [P, BATCH, depth], F32))
    turned = ctx.enter_context(nc.sbuf_tensor(f"{name}_turned", [depth, BATCH, P], F32))
    turned_ps = ctx.enter_context(nc.psum_tensor(f"{name}_turned_ps", [P, 8 * P], F32))
    out = ctx.enter_context(nc.psum_tensor(f"{name}_out", [P, 512], F32))
    rows_staged, rows_turned, copied, multiplied = sem("rows_staged"), sem("rows_turned"), sem("copied"), sem("multiplied")
    own = sem("steps")

    def vector(dve):
        s = Steps(dve, own)
        with dve.Fori(0, BINS // BATCH) as i:
            s.restart()
            source(dve, s, i, staged)
            s.wait()
            dve.sem_inc(rows_staged, 1)
            dve.wait_ge(multiplied, i + 1)
            finish(dve, s, i, out[:, 0:BATCH * width].rearrange("p (b w) -> p b w", b=BATCH))
            s.wait()

    def tensor(pe):
        with pe.Fori(0, BINS // BATCH) as i:
            pe.wait_ge(rows_staged, i + 1)
            for b in range(BATCH):
                last = pe.transpose(turned_ps[0:depth, b * P:(b + 1) * P], staged[:, b, :], k.ident[:])
            last.then_inc(rows_turned, 1)
            pe.wait_ge(copied, i + 1)
            for b in range(BATCH):
                last = pe.matmul(out[:, b * width:(b + 1) * width], turned[:, b, :], weights,
                                 start=True, stop=True)
            last.then_inc(multiplied, 1)

    def scalar(act):
        with act.Fori(0, BINS // BATCH) as i:
            act.wait_ge(rows_turned, i + 1)
            act.copy(turned[:].rearrange("f b p -> f (b p)"),
                     turned_ps[0:depth, 0:BATCH * P]).then_inc(copied, 1)

    return vector, tensor, scalar


def project(nc, k, *what):
    with stage(nc, k) as ctx:
        vector, tensor, scalar = project_parts(nc, k, ctx, *what)
        block = ctx.enter_context(nc.Block())

        @block.vector
        def _(dve):
            vector(dve)

        @block.tensor
        def _(pe):
            tensor(pe)

        @block.scalar
        def _(act):
            scalar(act)


def normalize_parts(nc, k, ctx, name, before=None, after=None):
    centred = ctx.enter_context(nc.sbuf_tensor(f"{name}_centred", [P, BINS, F], F32))
    square = ctx.enter_context(nc.sbuf_tensor(f"{name}_square", [P, BINS, F], F32))
    mean = ctx.enter_context(nc.sbuf_tensor(f"{name}_mean", [P, BINS], F32))
    spread_of = ctx.enter_context(nc.sbuf_tensor(f"{name}_spread", [P, BINS], F32))
    own = k.sem(f"{name}_steps")
    variance_ready = k.sem(f"{name}_variance_ready")
    deviation_ready = k.sem(f"{name}_deviation_ready")
    ready = k.sem(f"{name}_rows_ready")

    def vector(dve):
        s = Steps(dve, own)
        if before:
            before(dve, s)
        s.step(dve.tensor_reduce(mean[:], k.x[:], AX.X, ALU.add))
        s.wait()
        s.step(dve.tensor_scalar(mean[:], mean[:], 1.0 / F, None, ALU.mult))
        s.wait()
        s.step(dve.tensor_tensor(centred[:], k.x[:], spread(mean[:], 2, F), ALU.subtract))
        s.wait()
        s.step(dve.tensor_tensor(square[:], centred[:], centred[:], ALU.mult))
        s.wait()
        dve.tensor_reduce(spread_of[:], square[:], AX.X, ALU.add).then_inc(variance_ready, 1)
        dve.wait_ge(deviation_ready, 1)
        s.step(dve.reciprocal(spread_of[:], mean[:]))
        s.wait()
        s.step(dve.tensor_tensor(k.x[:], centred[:], spread(spread_of[:], 2, F), ALU.mult))
        s.wait()
        if after:
            after(dve, s)
            s.wait()
        dve.sem_inc(ready, 1)

    def scalar(act):
        act.wait_ge(variance_ready, 1)
        act.activation(mean[:], spread_of[:], ACT.Sqrt, bias=k.eps[:], scale=1.0 / F).then_inc(deviation_ready, 1)

    return vector, scalar, ready


def normalize(nc, k, name, before=None, after=None, store=()):
    with stage(nc, k) as ctx:
        vector, scalar, ready = normalize_parts(nc, k, ctx, name, before, after)
        stored = k.sem(f"{name}_rows_stored")
        block = ctx.enter_context(nc.Block())

        @block.vector
        def _(dve):
            vector(dve)

        @block.scalar
        def _(act):
            scalar(act)

        @block.sync
        def _(sp):
            sp.wait_ge(ready, 1)
            for n, (table, rows) in enumerate(store):
                whole, last = node_rows(table)
                sp.dma_start(whole, rows[:, 0:BINS - 1, :]).then_inc(stored, 16)
                sp.dma_start(last, rows[0:LAST, BINS - 1, :]).then_inc(stored, 16)
            if store:
                sp.wait_ge(stored, 32 * len(store))


def first_update_parts(nc, k, ctx):
    sums = k.sums[:].rearrange("p (b w) -> p b w", w=F + 1)

    def source(dve, s, i, staged):
        s.step(dve.tensor_copy(staged[:], sums[:, bass.ds(i * BATCH, BATCH), 0:F]))

    def finish(dve, s, i, out):
        x = k.x[:, bass.ds(i * BATCH, BATCH), :]
        s.step(dve.tensor_tensor(k.update[:], out, spread(k.b0[:], 1, BATCH), ALU.add))
        s.wait()
        s.step(dve.tensor_scalar(k.update[:], k.update[:], 0.0, None, ALU.max))
        s.wait()
        s.step(dve.tensor_tensor(x, x, k.update[:], ALU.add))

    dense = project_parts(nc, k, ctx, "dense", source, F, k.w0[:], F, finish)

    def after(dve, s):
        s.step(dve.tensor_copy(k.degree[:], sums[:, :, F]))
        s.step(dve.tensor_copy(k.far_rows[:, :, 0:F], k.x[:]))
        for half in range(2):
            s.step(dve.tensor_tensor(k.scorer_parts[:], k.w1_by_f[:],
                                     spread(k.fc[:, half * F:(half + 1) * F], 1, HEADS), ALU.mult))
            s.wait()
            s.step(dve.tensor_reduce(k.scorer[:, half * HEADS:(half + 1) * HEADS], k.scorer_parts[:],
                                     AX.X, ALU.add))
            s.wait()
        s.step(dve.memset(k.far_rows[:, :, F:FAR], 1.0))

    norm = normalize_parts(nc, k, ctx, "norm0", after=after)

    def scores_source(dve, s, i, staged):
        s.step(dve.tensor_copy(staged[:], k.x[:, bass.ds(i * BATCH, BATCH), :]))

    def scores_finish(dve, s, i, out):
        s.step(dve.tensor_scalar(k.own_score[:, bass.ds(i * BATCH, BATCH), :], out[:, :, 0:HEADS],
                                 k.fcb[:], None, ALU.add))
        s.step(dve.tensor_copy(k.far_rows[:, bass.ds(i * BATCH, BATCH), F + 1:F + 1 + HEADS],
                               out[:, :, HEADS:2 * HEADS]))

    scores = project_parts(nc, k, ctx, "scores", scores_source, F, k.scorer[:], 2 * HEADS, scores_finish)
    bound = bound_parts(nc, k, ctx)
    ready, stored = k.sem("far_rows_ready"), k.sem("far_rows_stored")

    def vector(dve):
        dense[0](dve)
        norm[0](dve)
        scores[0](dve)
        dve.sem_inc(ready, 1)
        bound[0](dve)

    def tensor(pe):
        dense[1](pe)
        scores[1](pe)
        bound[1](pe)

    def scalar(act):
        dense[2](act)
        norm[1](act)
        scores[2](act)
        act.wait_ge(ready, 1)
        whole, last = node_rows(k.far_dram)
        act.dma_start(whole, k.far_rows[:, 0:BINS - 1, :]).then_inc(stored, 16)
        act.dma_start(last, k.far_rows[0:LAST, BINS - 1, :]).then_inc(stored, 16)
        act.wait_ge(stored, 32)

    return vector, tensor, scalar


def bound_parts(nc, k, ctx):
    extremes = ctx.enter_context(nc.sbuf_tensor("extremes", [P, 2 * HEADS], F32))
    extreme = ctx.enter_context(nc.sbuf_tensor("extreme", [2 * HEADS, 1], F32))
    width = ctx.enter_context(nc.sbuf_tensor("score_width", [P, HEADS + 1], F32))
    reach = ctx.enter_context(nc.sbuf_tensor("score_reach", [P, BINS, HEADS], F32))
    turned = ctx.enter_context(nc.psum_tensor("extremes_turned", [P, 512], F32))
    overall = ctx.enter_context(nc.psum_tensor("extremes_overall", [P, 512], F32))
    own, found, in_rows, reduced, shared = (k.sem(n) for n in (
        "bound_steps", "extremes_found", "extremes_in_rows", "extremes_reduced", "extremes_shared"))

    def vector(dve):
        s = Steps(dve, own)
        a_dst = k.far_rows[:, :, F + 1:F + 1 + HEADS].rearrange("p b h -> p h b")
        s.step(dve.tensor_reduce(extremes[:, 0:HEADS], a_dst, AX.X, ALU.max))
        s.step(dve.tensor_reduce(extremes[:, HEADS:], a_dst, AX.X, ALU.min))
        s.wait()
        s.step(dve.tensor_scalar(extremes[:, HEADS:], extremes[:, HEADS:], -1.0, None, ALU.mult))
        s.wait()
        dve.sem_inc(found, 1)
        dve.wait_ge(in_rows, 1)
        s.step(dve.tensor_reduce(extreme[:], turned[0:2 * HEADS, 0:P], AX.X, ALU.max))
        s.wait()
        dve.sem_inc(reduced, 1)
        dve.wait_ge(shared, 1)
        s.step(dve.tensor_copy(extremes[:], overall[:, 0:2 * HEADS]))
        s.wait()
        s.step(dve.tensor_tensor(width[:, 0:HEADS], extremes[:, 0:HEADS], extremes[:, HEADS:], ALU.add))
        s.step(dve.tensor_tensor(reach[:], k.own_score[:], spread(extremes[:, 0:HEADS], 1, BINS), ALU.add))
        s.wait()
        s.step(dve.tensor_reduce(width[:, HEADS:], width[:, 0:HEADS], AX.X, ALU.max))
        terms = k.node_terms[:].rearrange("p (b t) -> p b t", t=2 * HEADS)
        s.step(dve.tensor_copy(terms[:, :, 0:HEADS], k.own_score[:]))
        s.step(dve.scalar_tensor_tensor(terms[:, :, HEADS:], reach[:], 0.2, reach[:], ALU.mult, ALU.max))
        s.wait()
        s.step(dve.tensor_scalar(k.bounded[:], width[:, HEADS:], RANGE, None, ALU.is_le))
        s.wait()

    def tensor(pe):
        pe.wait_ge(found, 1)
        pe.transpose(turned[0:2 * HEADS, 0:P], extremes[:], k.ident[:]).then_inc(in_rows, 1)
        pe.wait_ge(reduced, 1)
        pe.matmul(overall[:, 0:2 * HEADS], extreme[:].broadcast_to([2 * HEADS, P]),
                  k.ident[0:2 * HEADS, 0:2 * HEADS], start=True, stop=True).then_inc(shared, 1)

    return vector, tensor


def attend(nc, k):
    W = F + 1
    with stage(nc, k) as ctx:
        def sb(n, shape, dt, count):
            return [ctx.enter_context(nc.sbuf_tensor(f"att_{n}{s}", shape, dt)) for s in range(count)]

        def sem(n, count):
            return [k.sem(f"att_{n}{s}") for s in range(count)]

        rows = sb("rows", [P, PER, BY_SRC], F32, SLOTS)
        far = sb("far", [P, PER, FAR], F32, SLOTS)
        hot = sb("hot", [P, PER, P], F32, 2)
        absent = sb("absent", [P, PER, P], F32, 2)
        masked = sb("masked", [P, PER, HEADS, P], F32, 2)
        hot_turned = sb("hot_turned", [P, PER * P], F32, 2)
        local = sb("local", [P, PER], F32, 2)
        top = sb("top", [P, 4, HEADS], F32, 2)
        node_terms = sb("node_terms", [P, 2 * HEADS], F32, 2)
        rescale = sb("rescale", [P, HEADS], F32, 2)
        score = sb("score", [P, 2, PER, HEADS], F32, 2)
        share = sb("share", [P, PER, HEADS], F32, 2)
        message = sb("message", [P, PER, HEADS * W], F32, 2)
        scaled = ctx.enter_context(nc.sbuf_tensor("att_scaled", [P, HEADS, W], F32))
        masked_ps = ctx.enter_context(nc.psum_tensor("att_masked_ps", [P, HEADS, PER * P], F32))
        hot_ps = ctx.enter_context(nc.psum_tensor("att_hot_ps", [P, PER * P], F32))
        terms_ps = ctx.enter_context(nc.psum_tensor("att_terms_ps", [P, PER, P], F32))
        part = [ctx.enter_context(nc.psum_tensor(f"att_part{s}", [P, 512], F32)) for s in range(2)]
        rows_in, rows_free = sem("rows_in", SLOTS), sem("rows_free", SLOTS)
        gathered, far_free = sem("gathered", SLOTS), sem("far_free", SLOTS)
        hot_ready, absent_ready = sem("hot_ready", 2), sem("absent_ready", 2)
        masked_ready, masked_turned = sem("masked_ready", 2), sem("masked_turned", 2)
        maximum_taken = sem("maximum_taken", 1)[0]
        hot_in_psum, hot_copied = sem("hot_in_psum", 2), sem("hot_copied", 2)
        terms_ready, terms_spread = sem("terms_ready", 2), sem("terms_spread", 2)
        terms_read = sem("terms_read", 1)[0]
        score_ready, share_ready = sem("score_ready", 2), sem("share_ready", 2)
        message_ready, part_ready, part_free = sem("message_ready", 2), sem("part_ready", 2), sem("part_free", 2)
        own = sem("vector_steps", 1)[0]
        cleared = sem("cleared", 1)[0]
        b_hot = sb("b_hot", [P, PER, P], F32, SLOTS)
        b_local = sb("b_local", [P, PER], F32, SLOTS)
        b_turned = sb("b_turned", [P, PER * P], F32, SLOTS)
        b_score = sb("b_score", [P, 2, PER, HEADS], F32, SLOTS)
        b_share = sb("b_share", [P, PER, HEADS], F32, SLOTS)
        b_message = sb("b_message", [P, PER, HEADS * W], F32, SLOTS)
        b_hot_ready, b_hot_in_psum, b_hot_copied = (
            sem("b_hot_ready", SLOTS), sem("b_hot_in_psum", SLOTS), sem("b_hot_copied", SLOTS))
        b_terms_spread, b_terms_read = sem("b_terms_spread", SLOTS), sem("b_terms_read", SLOTS)
        b_score_ready, b_share_ready = sem("b_score_ready", SLOTS), sem("b_share_ready", SLOTS)
        b_message_ready, b_part_ready = sem("b_message_ready", SLOTS), sem("b_part_ready", SLOTS)
        b_terms = [terms_ps, hot_ps[:].rearrange("p (j n) -> p j n", j=PER)]
        block = ctx.enter_context(nc.Block())
        entry, first_node = k.entry["by_src"], k.first_node["by_src"]

        def load_rows(sp):
            for s in range(SLOTS):
                sp.sem_inc(rows_free[s], 1)
            with sp.Fori(0, TURNS["by_src"]) as i:
                for s in range(SLOTS):
                    at = sp.value_load(entry[0:1, bass.ds(i * SLOTS + s, 1), 0], min_val=0, max_val=EDGES)
                    sp.wait_ge(rows_free[s], 1)
                    sp.sem_clear(rows_free[s])
                    sp.dma_start(rows[s][:], k.edges_by_src[bass.ds(at, GROUP), :].rearrange(
                        "(p j) w -> p j w", p=P)).then_inc(rows_in[s], 16)

        def gather_far(pool):
            for s in range(SLOTS):
                pool.sem_inc(far_free[s], 1)
            with pool.Fori(0, TURNS["by_src"]):
                for s in range(SLOTS):
                    pool.wait_ge(rows_in[s], 16)
                    pool.sem_clear(rows_in[s])
                    pool.wait_ge(far_free[s], 1)
                    pool.sem_clear(far_free[s])
                    for j in range(PER):
                        pool.indirect_dma_start(
                            far[s][:, j, :], None, k.far_dram,
                            bass.IndirectOffsetOnAxis(ap=rows[s][:, j, 0:1].bitcast(I32), axis=0)
                        ).then_inc(gathered[s], 16)

        def general_vector(dve):
            own_steps = Steps(dve, own)
            dve.memset(k.attention[:], 0.0).then_inc(cleared, 1)
            dve.memset(k.maximum[:], -BIG).then_inc(cleared, 1)
            dve.wait_ge(cleared, 2)
            for c in range(2):
                dve.sem_inc(part_free[c], 1)

            def select(i, s):
                c = s % 2
                own_steps.restart()
                dve.wait_ge(gathered[s], (i + 1) * (16 * PER))
                own_steps.step(dve.tensor_scalar(local[c][:], rows[s][:, :, 1],
                                                 first_node[:, bass.ds(i * SLOTS + s, 1)], None,
                                                 ALU.subtract))
                own_steps.wait()
                own_steps.step(dve.tensor_tensor(hot[c][:], spread(k.iota[:], 1, PER),
                                                 spread(local[c][:], 2, P), ALU.is_equal))
                own_steps.wait()
                dve.sem_inc(hot_ready[c], 1)
                dve.sem_inc(rows_free[s], 1)

            def mask(i, s):
                c = s % 2
                dve.wait_ge(absent_ready[c], turn(i, s, 2))
                dve.tensor_tensor(masked[c][:], spread(absent[c][:], 2, HEADS),
                                  spread(far[s][:, :, W:W + HEADS], 3, P), ALU.add).then_inc(masked_ready[c], 1)

            def raise_maximum(i, s, at):
                c = s % 2
                own_steps.restart()
                own_score = k.own_score[:].rearrange("p b h -> p (b h)")[:, bass.ds(at * HEADS, HEADS)]
                maximum = k.maximum[:, bass.ds(at * HEADS, HEADS)]
                dve.wait_ge(masked_turned[c], turn(i, s, 2))
                own_steps.step(dve.tensor_reduce(top[c][:, 0, :], masked_ps[:], AX.X, ALU.max))
                own_steps.step(dve.tensor_copy(node_terms[c][:, 0:HEADS], own_score))
                own_steps.wait()
                dve.sem_inc(maximum_taken, 1)
                own_steps.step(dve.tensor_tensor(top[c][:, 1, :], top[c][:, 0, :], own_score, ALU.add))
                own_steps.wait()
                own_steps.step(dve.scalar_tensor_tensor(top[c][:, 2, :], top[c][:, 1, :], 0.2, top[c][:, 1, :],
                                                        ALU.mult, ALU.max))
                own_steps.wait()
                own_steps.step(dve.tensor_tensor(node_terms[c][:, HEADS:2 * HEADS], top[c][:, 2, :], maximum,
                                                 ALU.max))
                own_steps.wait()
                own_steps.step(dve.tensor_tensor(top[c][:, 3, :], maximum, node_terms[c][:, HEADS:2 * HEADS],
                                                 ALU.subtract))
                own_steps.wait()
                own_steps.step(dve.tensor_copy(maximum, node_terms[c][:, HEADS:2 * HEADS]))
                own_steps.wait()
                dve.sem_inc(terms_ready[c], 1)

            def edge_scores(i, s):
                c = s % 2
                own_steps.restart()
                dve.wait_ge(terms_spread[c], turn(i, s, 2))
                own_steps.step(dve.tensor_tensor(score[c][:, 0], terms_ps[:, :, 0:HEADS],
                                                 far[s][:, :, W:W + HEADS], ALU.add))
                own_steps.wait()
                own_steps.step(dve.scalar_tensor_tensor(score[c][:, 1], score[c][:, 0], 0.2, score[c][:, 0],
                                                        ALU.mult, ALU.max))
                own_steps.wait()
                own_steps.step(dve.tensor_tensor(score[c][:, 0], score[c][:, 1],
                                                 terms_ps[:, :, HEADS:2 * HEADS], ALU.subtract))
                own_steps.wait()
                dve.sem_inc(terms_read, 1)
                own_steps.step(dve.tensor_scalar(score[c][:, 1], score[c][:, 0], 0.0, None, ALU.min))
                own_steps.wait()
                dve.sem_inc(score_ready[c], 1)

            def messages(i, s):
                c = s % 2
                own_steps.restart()
                dve.wait_ge(share_ready[c], turn(i, s, 2))
                own_steps.step(dve.tensor_tensor(
                    message[c][:].rearrange("p j (h w) -> p j h w", h=HEADS),
                    spread(far[s][:, :, 0:W], 2, HEADS), spread(share[c][:], 3, W), ALU.mult))
                own_steps.wait()
                dve.sem_inc(message_ready[c], 1)
                dve.sem_inc(far_free[s], 1)

            def accumulate(i, s, at):
                c = s % 2
                own_steps.restart()
                sums = k.attention[:, bass.ds(at * (HEADS * W), HEADS * W)]
                own_steps.step(dve.tensor_tensor(scaled[:], sums.rearrange("p (h w) -> p h w", h=HEADS),
                                                 spread(rescale[c][:], 2, W), ALU.mult))
                dve.wait_ge(part_ready[c], turn(i, s, 2))
                own_steps.wait()
                own_steps.step(dve.tensor_tensor(sums, scaled[:].rearrange("p h w -> p (h w)"),
                                                 part[c][:, 0:HEADS * W], ALU.add))
                own_steps.wait()
                dve.sem_inc(part_free[c], 1)

            with dve.Fori(0, TURNS["by_src"]) as i:
                for s in range(0, SLOTS, 2):
                    at = [dve.value_load(entry[0:1, bass.ds(i * SLOTS + s + d, 1), 1],
                                         min_val=0, max_val=BINS - 1) for d in range(2)]
                    select(i, s)
                    select(i, s + 1)
                    mask(i, s)
                    mask(i, s + 1)
                    raise_maximum(i, s, at[0])
                    raise_maximum(i, s + 1, at[1])
                    edge_scores(i, s)
                    edge_scores(i, s + 1)
                    messages(i, s)
                    messages(i, s + 1)
                    accumulate(i, s, at[0])
                    accumulate(i, s + 1, at[1])

        def general_tensor(pe):
            for once in range(1):
                pe.sem_inc(maximum_taken, 1)
                pe.sem_inc(terms_read, 1)

            def turn_hot(i, s):
                c = s % 2
                pe.wait_ge(hot_ready[c], turn(i, s, 2))
                if s:
                    pe.wait_ge(hot_copied[(s - 1) % 2], turn(i, s - 1, 2))
                for j in range(PER):
                    last = pe.transpose(hot_ps[:, j * P:(j + 1) * P], hot[c][:, j, :], k.ident[:])
                last.then_inc(hot_in_psum[c], 1)

            def turn_masked(i, s):
                c = s % 2
                pe.wait_ge(masked_ready[c], turn(i, s, 2))
                pe.wait_ge(maximum_taken, i * SLOTS + s + 1)
                for h in range(HEADS):
                    for j in range(PER):
                        last = pe.transpose(masked_ps[:, h, j * P:(j + 1) * P], masked[c][:, j, h, :],
                                            k.ident[:])
                last.then_inc(masked_turned[c], 1)

            def spread_terms(i, s):
                c = s % 2
                pe.wait_ge(terms_ready[c], turn(i, s, 2))
                pe.wait_ge(hot_copied[c], turn(i, s, 2))
                pe.wait_ge(terms_read, i * SLOTS + s + 1)
                for j in range(PER):
                    last = pe.matmul(terms_ps[:, j, 0:2 * HEADS], hot_turned[c][:, j * P:(j + 1) * P],
                                     node_terms[c][:], start=True, stop=True)
                last.then_inc(terms_spread[c], 1)

            def sum_nodes(i, s):
                c = s % 2
                pe.wait_ge(message_ready[c], turn(i, s, 2))
                pe.wait_ge(part_free[c], turn(i, s, 2))
                for j in range(PER):
                    last = pe.matmul(part[c][:, 0:HEADS * W], hot[c][:, j, :], message[c][:, j, :],
                                     start=(j == 0), stop=(j == PER - 1))
                last.then_inc(part_ready[c], 1)

            with pe.Fori(0, TURNS["by_src"]) as i:
                for s in range(0, SLOTS, 2):
                    turn_hot(i, s)
                    turn_hot(i, s + 1)
                    turn_masked(i, s)
                    turn_masked(i, s + 1)
                    spread_terms(i, s)
                    spread_terms(i, s + 1)
                    sum_nodes(i, s)
                    sum_nodes(i, s + 1)

        def general_scalar(act):
            def hide(i, s):
                c = s % 2
                act.wait_ge(hot_ready[c], turn(i, s, 2))
                act.activation(absent[c][:], hot[c][:], ACT.Copy, bias=-BIG, scale=BIG).then_inc(absent_ready[c], 1)

            def copy_hot(i, s):
                c = s % 2
                act.wait_ge(hot_in_psum[c], turn(i, s, 2))
                act.copy(hot_turned[c][:], hot_ps[:]).then_inc(hot_copied[c], 1)

            def exponents(i, s):
                c = s % 2
                act.wait_ge(terms_ready[c], turn(i, s, 2))
                act.activation(rescale[c][:], top[c][:, 3, :], ACT.Exp)
                act.wait_ge(score_ready[c], turn(i, s, 2))
                act.activation(share[c][:], score[c][:, 1], ACT.Exp).then_inc(share_ready[c], 1)

            with act.Fori(0, TURNS["by_src"]) as i:
                for s in range(0, SLOTS, 2):
                    hide(i, s)
                    hide(i, s + 1)
                    copy_hot(i, s)
                    copy_hot(i, s + 1)
                    exponents(i, s)
                    exponents(i, s + 1)

        def bounded_vector(dve):
            steps = Steps(dve, own)
            step, wait = steps.step, steps.wait
            step(dve.memset(k.attention[:], 0.0))
            wait()
            for c in range(2):
                dve.sem_inc(part_free[c], 1)

            def local_node(i, s):
                dve.wait_ge(gathered[s], (i + 1) * (16 * PER))
                return step(dve.tensor_scalar(b_local[s][:], rows[s][:, :, 1],
                                              first_node[:, bass.ds(i * SLOTS + s, 1)], None, ALU.subtract))

            def one_hot(s):
                dve.tensor_tensor(b_hot[s][:], spread(k.iota[:], 1, PER),
                                  spread(b_local[s][:], 2, P), ALU.is_equal).then_inc(b_hot_ready[s], 1)
                dve.sem_inc(rows_free[s], 1)

            def raw_score(i, s):
                dve.wait_ge(b_terms_spread[s % SLOTS], turn(i, s, SLOTS))
                return step(dve.tensor_tensor(b_score[s % SLOTS][:, 0], b_terms[s % 2][:, :, 0:HEADS],
                                              far[s % SLOTS][:, :, W:W + HEADS], ALU.add))

            def leaky_score(s):
                score = b_score[s % SLOTS]
                return step(dve.scalar_tensor_tensor(score[:, 1], score[:, 0], 0.2, score[:, 0], ALU.mult, ALU.max))

            def less_bound(s):
                score = b_score[s % SLOTS]
                return step(dve.tensor_tensor(score[:, 0], score[:, 1], b_terms[s % 2][:, :, HEADS:2 * HEADS],
                                              ALU.subtract))

            def cap_score(s):
                score = b_score[s % SLOTS]
                dve.tensor_scalar(score[:, 1], score[:, 0], 0.0, None, ALU.min).then_inc(b_score_ready[s % SLOTS], 1)

            def messages(i, s):
                s, i = s % SLOTS, i + s // SLOTS
                dve.wait_ge(b_share_ready[s], i + 1)
                dve.tensor_tensor(
                    b_message[s][:].rearrange("p j (h w) -> p j h w", h=HEADS),
                    spread(far[s][:, :, 0:W], 2, HEADS), spread(b_share[s][:], 3, W),
                    ALU.mult).then_inc(b_message_ready[s], 1)

            def free_far(i, s):
                dve.wait_ge(b_message_ready[s % SLOTS], turn(i, s, SLOTS))
                dve.sem_inc(far_free[s % SLOTS], 1)

            def bin_of(i, s):
                return dve.value_load(entry[0:1, bass.ds(i * SLOTS + s, 1), 1], min_val=0, max_val=BINS - 1)

            def accumulate(i, s, at):
                dve.wait_ge(b_part_ready[s % SLOTS], turn(i, s, SLOTS))
                sums = k.attention[:, bass.ds(at * (HEADS * W), HEADS * W)]
                return step(dve.tensor_tensor(sums, sums, part[s % 2][:, 0:HEADS * W], ALU.add))

            def one_group(i, s, groups):
                if groups > 2:
                    messages(i, s - 2)
                n_local = local_node(i, s)
                if groups > 2:
                    free_far(i, s - 2)
                if groups > 1:
                    n_raw = raw_score(i, s - 1)
                wait(n_local)
                one_hot(s)
                if groups > 3:
                    at = bin_of(i, s - 3)
                if groups > 1:
                    wait(n_raw)
                    n_leaky = leaky_score(s - 1)
                if groups > 1:
                    wait(n_leaky)
                    n_less = less_bound(s - 1)
                if groups > 3:
                    n_added = accumulate(i, s - 3, at)
                if groups > 1:
                    wait(n_less)
                    dve.sem_inc(b_terms_read[(s - 1) % SLOTS], 1)
                    cap_score(s - 1)
                if groups > 3:
                    wait(n_added)
                    dve.sem_inc(part_free[(s - 3) % 2], 1)

            def one_turn(i, first, last):
                steps.restart()
                for s in range(SLOTS):
                    one_group(i, s, groups=s + 1 if first else SLOTS)
                wait()

            turns(dve, "by_src", one_turn)
            steps.restart()
            i, s = TURNS["by_src"] - 1, SLOTS - 1
            wait(raw_score(i, s))
            wait(leaky_score(s))
            wait(less_bound(s))
            dve.sem_inc(b_terms_read[s], 1)
            cap_score(s)
            for s in range(SLOTS - 3, SLOTS):
                if s > SLOTS - 3:
                    messages(i, s)
                wait(accumulate(i, s, bin_of(i, s)))
                dve.sem_inc(part_free[s % 2], 1)

        def bounded_tensor(pe):
            def turn_hot(i, s):
                pe.wait_ge(b_hot_ready[s], i + 1)
                for j in range(PER):
                    last = pe.transpose(masked_ps[:, s, j * P:(j + 1) * P], b_hot[s][:, j, :], k.ident[:])
                last.then_inc(b_hot_in_psum[s], 1)

            def spread_terms(i, s):
                at = pe.value_load(entry[0:1, bass.ds(i * SLOTS + s, 1), 1], min_val=0, max_val=BINS - 1)
                s, i = s % SLOTS, i + s // SLOTS
                pe.wait_ge(b_hot_copied[s], i + 1)
                pe.wait_ge(b_terms_read[(s - 2) % SLOTS], i + 1)
                for j in range(PER):
                    last = pe.matmul(b_terms[s % 2][:, j, 0:2 * HEADS], b_turned[s][:, j * P:(j + 1) * P],
                                     k.node_terms[:, bass.ds(at * (2 * HEADS), 2 * HEADS)], start=True, stop=True)
                last.then_inc(b_terms_spread[s], 1)

            def sum_nodes(i, s):
                s, i = s % SLOTS, i + s // SLOTS
                pe.wait_ge(b_message_ready[s], i + 1)
                pe.wait_ge(part_free[s % 2], turn(i, s, 2))
                for j in range(PER):
                    last = pe.matmul(part[s % 2][:, 0:HEADS * W], b_hot[s][:, j, :], b_message[s][:, j, :],
                                     start=(j == 0), stop=(j == PER - 1))
                last.then_inc(b_part_ready[s], 1)

            def one_turn(i, first, last):
                for s in range(SLOTS):
                    if not (first and s < 1):
                        spread_terms(i, s - 1)
                    turn_hot(i, s)
                    if not (first and s < 2):
                        sum_nodes(i, s - 2)

            for s in range(SLOTS // 2, SLOTS):
                pe.sem_inc(b_terms_read[s], 1)
            turns(pe, "by_src", one_turn)
            spread_terms(TURNS["by_src"] - 1, SLOTS - 1)
            for s in range(SLOTS - 2, SLOTS):
                sum_nodes(TURNS["by_src"] - 1, s)

        def bounded_scalar(act):
            def copy_hot(i, s):
                act.wait_ge(b_hot_in_psum[s], i + 1)
                act.copy(b_turned[s][:], masked_ps[:, s, :]).then_inc(b_hot_copied[s], 1)

            def exponents(i, s):
                act.wait_ge(b_score_ready[s % SLOTS], turn(i, s, SLOTS))
                act.activation(b_share[s % SLOTS][:], b_score[s % SLOTS][:, 1],
                               ACT.Exp).then_inc(b_share_ready[s % SLOTS], 1)

            def one_turn(i, first, last):
                for s in range(SLOTS):
                    copy_hot(i, s)
                    if not (first and s < 1):
                        exponents(i, s - 1)

            turns(act, "by_src", one_turn)
            exponents(TURNS["by_src"] - 1, SLOTS - 1)

        def bounded(engine):
            return engine.value_load(k.bounded[0:1, 0:1], min_val=0, max_val=1) == 1

        @block.sync
        def _(sp):
            load_rows(sp)

        @block.gpsimd
        def _(pool):
            gather_far(pool)

        @block.vector
        def _(dve):
            with dve.If(bounded(dve)):
                bounded_vector(dve)
            with dve.Else():
                general_vector(dve)

        @block.tensor
        def _(pe):
            with pe.If(bounded(pe)):
                bounded_tensor(pe)
            with pe.Else():
                general_tensor(pe)

        @block.scalar
        def _(act):
            with act.If(bounded(act)):
                bounded_scalar(act)
            with act.Else():
                general_scalar(act)


def attention_update(nc, k):
    W = F + 1
    sums = k.attention[:].rearrange("p (b h w) -> p b h w", h=HEADS, w=W)

    def source(dve, s, i, staged):
        part = sums[:, bass.ds(i * BATCH, BATCH), :, :]
        s.step(dve.tensor_scalar(k.denominator[:], part[:, :, :, F], 1e-30, float(HEADS), ALU.max, ALU.mult))
        s.wait()
        s.step(dve.reciprocal(k.share[:], k.denominator[:]))
        s.wait()
        for h in range(HEADS):
            s.step(dve.tensor_tensor(staged[:, :, h * F:(h + 1) * F], part[:, :, h, 0:F],
                                     k.share[:, :, h:h + 1].broadcast_to([P, BATCH, F]), ALU.mult))

    def finish(dve, s, i, out):
        x = k.x[:, bass.ds(i * BATCH, BATCH), :]
        s.step(dve.tensor_tensor(k.update[:], out, spread(k.bias1[:], 1, BATCH), ALU.add))
        s.wait()
        s.step(dve.tensor_tensor(x, x, k.update[:], ALU.add))

    project(nc, k, "heads", source, HEADS * F, k.w1[:], F, finish)

    with stage(nc, k) as ctx:
        degree_ready, root_ready, inverse_ready = (k.sem(n) for n in ("degree_ready", "root_ready", "inverse_ready"))
        block = ctx.enter_context(nc.Block())

        @block.vector
        def _(dve):
            dve.tensor_scalar(k.degree[:], k.degree[:], 1.0, None, ALU.add).then_inc(degree_ready, 1)
            dve.wait_ge(root_ready, 1)
            dve.reciprocal(k.inverse[:], k.degree_root[:]).then_inc(inverse_ready, 1)
            dve.wait_ge(inverse_ready, 1)

        @block.scalar
        def _(act):
            act.wait_ge(degree_ready, 1)
            act.activation(k.degree_root[:], k.degree[:], ACT.Sqrt).then_inc(root_ready, 1)

    def after(dve, s):
        s.step(dve.scalar_tensor_tensor(k.hop_rows[:], k.x[:], 0.0, spread(k.inverse[:], 2, F),
                                        ALU.max, ALU.mult))

    normalize(nc, k, "norm1", after=after, store=[(k.hop_dram[0], k.hop_rows)])


def between_hops(nc, k):
    sums = k.sums[:].rearrange("p (b w) -> p b w", w=F + 1)[:, :, 0:F]
    with stage(nc, k) as ctx:
        own, ready, stored = (k.sem(n) for n in ("hop_steps", "hop_rows_ready", "hop_rows_stored"))
        block = ctx.enter_context(nc.Block())

        @block.vector
        def _(dve):
            s = Steps(dve, own)
            s.step(dve.tensor_tensor(k.hop_rows[:], k.hop_rows[:], sums, ALU.add))
            for _ in range(2):
                s.wait()
                s.step(dve.tensor_tensor(k.hop_rows[:], k.hop_rows[:], spread(k.inverse[:], 2, F), ALU.mult))
            s.wait()
            dve.sem_inc(ready, 1)

        @block.sync
        def _(sp):
            sp.wait_ge(ready, 1)
            whole, last = node_rows(k.hop_dram[1])
            sp.dma_start(whole, k.hop_rows[:, 0:BINS - 1, :]).then_inc(stored, 16)
            sp.dma_start(last, k.hop_rows[0:LAST, BINS - 1, :]).then_inc(stored, 16)
            sp.wait_ge(stored, 32)


def after_hops(nc, k):
    sums = k.sums[:].rearrange("p (b w) -> p b w", w=F + 1)[:, :, 0:F]

    def before(dve, s):
        s.step(dve.tensor_tensor(k.hop_rows[:], k.hop_rows[:], sums, ALU.add))
        s.wait()
        s.step(dve.tensor_tensor(k.hop_rows[:], k.hop_rows[:], spread(k.inverse[:], 2, F), ALU.mult))
        s.wait()
        s.step(dve.tensor_tensor(k.x[:], k.x[:], k.hop_rows[:], ALU.add))
        s.wait()

    normalize(nc, k, "norm2", before=before, store=[(k.hop_dram[0], k.x)])


def radial_weights(nc, k):
    scalar_norm = sqrt(4 * pi) / sqrt(2 * MUL)
    vector_norm = sqrt(4 * pi) * sqrt(3.0) / sqrt(4 * MUL)
    flat = 0.5 / sqrt(pi)
    same = flat / sqrt(3.0)
    cross = sqrt(3.0 / (4 * pi)) / sqrt(6.0)
    tensor = sqrt(3.0 / (8 * pi))
    H1 = HIDDEN + 1
    with stage(nc, k) as ctx:
        own = k.sem("radial_steps")
        block = ctx.enter_context(nc.Block())

        @block.vector
        def _(dve):
            s = Steps(dve, own)
            a = k.radial[:, 0:256].rearrange("h (q m) -> h q m", m=2 * MUL)
            b = k.radial[:, 256:384].rearrange("h (q v) -> h q v", v=MUL)

            def paths(n):
                return k.w3[:, n * 64:(n + 1) * 64].rearrange("h (u v) -> h u v", v=MUL)

            vector_paths = k.w3[:, 192:384].rearrange("h (u v l) -> h u v l", v=MUL, l=3)
            for out, of, scale in (
                    (a[:, 0:8, 0:8], paths(0), scalar_norm * flat),
                    (a[:, 0:8, 8:16], paths(1), scalar_norm * flat),
                    (a[:, 8:16, 0:8], paths(2), vector_norm * flat),
                    (a[:, 8:16, 8:16], vector_paths[:, :, :, 2], vector_norm * tensor),
                    (b[:, 0:8, :], vector_paths[:, :, :, 0], vector_norm * same),
                    (b[:, 8:16, :], vector_paths[:, :, :, 1], vector_norm * cross)):
                s.step(dve.tensor_scalar(out, of, scale, None, ALU.mult))
            s.wait()
            s.step(dve.scalar_tensor_tensor(b[:, 0:8, :], vector_paths[:, :, :, 2],
                                            -vector_norm * tensor / 3, b[:, 0:8, :], ALU.mult, ALU.add))
            s.wait()


def convolve(nc, k):
    with stage(nc, k) as ctx:
        def sb(n, shape, count):
            return [ctx.enter_context(nc.sbuf_tensor(f"conv_{n}{s}", shape, F32)) for s in range(count)]

        def sem(n, count):
            return [k.sem(f"conv_{n}{s}") for s in range(count)]

        rows = sb("rows", [P, PER, BY_DST], SLOTS)
        far = sb("far", [P, PER, F], SLOTS)
        weights = sb("weights", [HIDDEN, P, PER], SLOTS)
        hidden = sb("hidden", [HIDDEN + 1, P, PER], 2)
        away = sb("away", [P, PER, P], 1)[0]
        hot = sb("hot", [P, PER, P], 2)
        minus_local = sb("minus_local", [P, PER], 2)
        along = sb("along", [P, PER, MUL, 3], 2)
        factors = sb("factors", [P, PER, 2 * MUL], 2)
        products_a = sb("products_a", [P, PER, 2 * MUL, 2 * MUL], 1)[0]
        folded_a = sb("folded_a", [P, PER, 2 * MUL, MUL], 1)[0]
        products_b = sb("products_b", [P, 3, PER, 2 * MUL, MUL], 1)[0]
        message = sb("message", [P, PER, 5, MUL], 2)
        sum_b = sb("sum_b", [P, 5, PER, 2 * MUL], 2)
        crossed = sb("crossed", [P, 2, 3, PER, MUL], 2)
        radial_a = ctx.enter_context(nc.psum_tensor("conv_radial_a", [P, 2, PER, 256], F32))
        radial_b = ctx.enter_context(nc.psum_tensor("conv_radial_b", [P, 2, PER, 128], F32))
        part = [ctx.enter_context(nc.psum_tensor(f"conv_part{s}", [P, 512], F32)) for s in range(2)]
        rows_in, rows_free = sem("rows_in", SLOTS), sem("rows_free", SLOTS)
        gathered, far_free = sem("gathered", SLOTS), sem("far_free", SLOTS)
        weights_in, weights_free = sem("weights_in", SLOTS), sem("weights_free", SLOTS)
        hidden_ready = sem("hidden_ready", 2)
        radial_ready, radial_free = sem("radial_ready", 2), sem("radial_free", 2)
        factors_ready, factors_free = sem("factors_ready", 2), sem("factors_free", 2)
        hot_ready = sem("hot_ready", 2)
        sum_b_ready, sum_b_wrapped = sem("sum_b_ready", 2), sem("sum_b_wrapped", 2)
        message_ready, part_ready, part_free = sem("message_ready", 2), sem("part_ready", 2), sem("part_free", 2)
        products_made, folded = sem("products_made", 1)[0], sem("folded", 1)[0]
        own, copied, ones_set = (sem(n, 1)[0] for n in ("vector_steps", "scalar_steps", "ones_set"))
        block = ctx.enter_context(nc.Block())
        entry, first_node = k.entry["by_dst"], k.first_node["by_dst"]

        @block.sync
        def _(sp):
            for s in range(SLOTS):
                sp.sem_inc(rows_free[s], 2)
                sp.sem_inc(weights_free[s], 1)
            with sp.Fori(0, TURNS["by_dst"]) as i:
                for s in range(SLOTS):
                    sp.wait_ge(rows_free[s], 2)
                    sp.sem_clear(rows_free[s])
                    load_pieces(sp, k, i, s, rows[s], rows_in[s])
                    sp.wait_ge(weights_free[s], 1)
                    sp.sem_clear(weights_free[s])
                    sp.dma_start(weights[s][:].rearrange("h p j -> h (p j)").unsqueeze(1),
                                 k.weight_by_group[bass.ds(i * SLOTS + s, 1), :].partition_broadcast(HIDDEN)
                                 ).then_inc(weights_in[s], 16)

        @block.gpsimd
        def _(pool):
            for s in range(SLOTS):
                pool.sem_inc(far_free[s], 2)

            def gather(s, columns):
                for j in columns:
                    pool.indirect_dma_start(
                        far[s][:, j, :], None, k.hop_dram[0],
                        bass.IndirectOffsetOnAxis(ap=rows[s][:, j, 0:1].bitcast(I32), axis=0)
                    ).then_inc(gathered[s], 16)

            def gather_and_fold(s, fold=True):
                pool.wait_ge(rows_in[s], 16 * HALVES)
                pool.sem_clear(rows_in[s])
                pool.wait_ge(far_free[s], 2)
                pool.sem_clear(far_free[s])
                gather(s, range(PER // 2))
                if fold:
                    fold_products()
                gather(s, range(PER // 2, PER))

            def fold_products():
                pool.wait_ge(products_made, 1)
                pool.sem_clear(products_made)
                pool.tensor_tensor(folded_a[:], products_a[:, :, :, 0:MUL], products_a[:, :, :, MUL:2 * MUL],
                                   ALU.add).then_inc(folded, 1)

            for s in range(AHEAD):
                gather_and_fold(s, fold=False)
            for s in range(AHEAD, SLOTS):
                gather_and_fold(s)
            with pool.Fori(1, TURNS["by_dst"]):
                for s in range(SLOTS):
                    gather_and_fold(s)
            for s in range(AHEAD):
                fold_products()

        @block.scalar
        def _(act):
            for c in range(2):
                act.activation(hidden[c][HIDDEN:HIDDEN + 1, :, :],
                               k.ident[HIDDEN:HIDDEN + 1, 0:1].unsqueeze(2).broadcast_to([1, P, PER]),
                               ACT.Copy, bias=1.0, scale=0.0).then_inc(ones_set, 1)
                act.sem_inc(factors_free[c], 1)
            act.wait_ge(ones_set, 2)

            def hide(i, s, again):
                c, slot = s % 2, s % SLOTS
                act.wait_ge(weights_in[slot], (i + s // SLOTS) * 16 + 16)
                if again:
                    act.wait_ge(radial_ready[c], turn(i, s - 2, 2))
                act.activation(hidden[c][0:HIDDEN, :, :], weights[slot][:], ACT.Relu,
                               bias=k.b3a[:], scale=k.w3a[:]).then_inc(hidden_ready[c], 1)

            def hidden_done(i, s):
                act.wait_ge(hidden_ready[s % 2], turn(i, s, 2))
                act.sem_inc(weights_free[s % SLOTS], 1)

            def wrap(i, s):
                c = s % 2
                act.wait_ge(sum_b_ready[c], turn(i, s, 2))
                act.copy(sum_b[c][:, 3:5, :, MUL:2 * MUL],
                         sum_b[c][:, 0:2, :, MUL:2 * MUL]).then_inc(sum_b_wrapped[c], 1)

            def one_turn(i, first, last):
                for s in range(SLOTS):
                    c = s % 2
                    ahead = not (last and s == SLOTS - 1)
                    if ahead:
                        hide(i, s + 1, again=not (first and s == 0))
                    act.wait_ge(gathered[s], (i + 1) * (16 * PER))
                    act.wait_ge(factors_free[c], turn(i, s, 2))
                    act.copy(factors[c][:, :, 0:MUL], far[s][:, :, 0:MUL]).then_inc(copied, 1)
                    for h in range(HALVES):
                        cut = slice(h * COLUMNS, (h + 1) * COLUMNS)
                        act.activation(minus_local[c][:, cut], rows[s][:, cut, 1], ACT.Identity,
                                       bias=first_node[:, bass.ds((i * SLOTS + s) * HALVES + h, 1)],
                                       scale=-1.0).then_inc(copied, 1)
                    act.wait_ge(copied, 1)
                    act.sem_inc(factors_ready[c], 1)
                    act.sem_inc(far_free[s], 1)
                    act.wait_ge(copied, 1 + HALVES)
                    act.sem_inc(rows_free[s], 1)
                    for j in range(PER):
                        act.activation(away[:, j, :], k.iota[:], ACT.Abs,
                                       bias=minus_local[c][:, j:j + 1]).then_inc(copied, 1)
                    if not (first and s == 0):
                        wrap(i, s - 1)
                    if ahead:
                        hidden_done(i, s + 1)
                    if not (first and s < 2):
                        act.wait_ge(part_ready[c], turn(i, s - 2, 2))
                    act.wait_ge(copied, 1 + HALVES + PER)
                    act.activation(hot[c][:], away[:], ACT.Relu, bias=k.ones[:, 0:1], scale=-1.0
                                   ).then_inc(hot_ready[c], 1)
                    act.sem_clear(copied)
                    act.wait_ge(hot_ready[c], turn(i, s, 2))

            hide(0, 0, again=False)
            hidden_done(0, 0)
            turns(act, "by_dst", one_turn)
            wrap(TURNS["by_dst"] - 1, SLOTS - 1)

        @block.tensor
        def _(pe):
            for c in range(2):
                pe.sem_inc(radial_free[c], 1)

            def radial(i, s):
                c = s % 2
                pe.wait_ge(hidden_ready[c], turn(i, s, 2))
                pe.wait_ge(radial_free[c], turn(i, s, 2))
                for j in range(PER):
                    pe.matmul(radial_a[:, c, j, :], hidden[c][:, :, j], k.radial[:, 0:256], start=True, stop=True)
                    last = pe.matmul(radial_b[:, c, j, :], hidden[c][:, :, j], k.radial[:, 256:384],
                                     start=True, stop=True)
                last.then_inc(radial_ready[c], 1)

            def sum_nodes(i, s):
                c = s % 2
                pe.wait_ge(hot_ready[c], turn(i, s, 2))
                pe.wait_ge(message_ready[c], turn(i, s, 2))
                pe.wait_ge(part_free[c], turn(i, s, 2))
                for j in range(PER):
                    h = j // COLUMNS
                    last = pe.matmul(part[c][:, h * F:(h + 1) * F], hot[c][:, j, :],
                                     message[c][:, j, 0:4, :].rearrange("p a u -> p (a u)"),
                                     start=(j % COLUMNS == 0), stop=(j % COLUMNS == COLUMNS - 1))
                last.then_inc(part_ready[c], 1)

            def one_turn(i, first, last):
                for s in range(SLOTS):
                    if not (last and s == SLOTS - 1):
                        radial(i, s + 1)
                    if not (first and s == 0):
                        sum_nodes(i, s - 1)

            radial(0, 0)
            turns(pe, "by_dst", one_turn)
            sum_nodes(TURNS["by_dst"] - 1, SLOTS - 1)

        @block.vector
        def _(dve):
            steps = Steps(dve, own)
            step, wait = steps.step, steps.wait
            step(dve.memset(k.sums[:], 0.0))
            wait()
            for c in range(2):
                dve.sem_inc(part_free[c], 1)

            def finish_a(i, s):
                c = s % 2
                dve.wait_ge(folded, i * SLOTS + s + 1)
                return step(dve.tensor_reduce(
                    message[c][:, :, 0:5:4, :], folded_a[:].rearrange("p j (h q) m -> p j h q m", h=2),
                    AX.X, ALU.add))

            def finish_b(i, s):
                dve.wait_ge(radial_free[s % 2], turn(i, s, 2) + 1)
                dve.sem_inc(far_free[s % SLOTS], 1)
                dve.tensor_reduce(sum_b[s % 2][:, 0:3].rearrange("p o j q -> p (o j q)"),
                                  products_b[:].rearrange("p o j q v -> p (o j q) v"),
                                  AX.X, ALU.add).then_inc(sum_b_ready[s % 2], 1)

            def turned(s, at):
                return spread(rows[s % SLOTS][:, :, 3 + at:6 + at].rearrange("p j o -> p o j"), 3, MUL)

            def vector_out(s):
                return message[s % 2][:, :, 1:4, :].rearrange("p j o u -> p o j u")

            def along_r(s):
                return step(dve.tensor_tensor(vector_out(s), turned(s, 0),
                                              spread(message[s % 2][:, :, 4, :], 1, 3), ALU.mult))

            def add_own(s):
                return step(dve.tensor_tensor(vector_out(s), vector_out(s),
                                              sum_b[s % 2][:, 0:3, :, 0:MUL], ALU.add))

            def add_cross(s, part_no, op):
                return dve.tensor_tensor(vector_out(s), vector_out(s), crossed[s % 2][:, part_no], op)

            def cross(s, part_no, r_at, g_at):
                c = s % 2
                return step(dve.tensor_tensor(crossed[c][:, part_no], turned(s, r_at),
                                              sum_b[c][:, g_at:g_at + 3, :, MUL:2 * MUL], ALU.mult))

            def accumulate(i, s, h, at):
                c = s % 2
                dve.wait_ge(part_ready[c], turn(i, s, 2))
                sums = k.sums[:, bass.ds(at * (F + 1), F)]
                return step(dve.tensor_tensor(sums, sums, part[c][:, h * F:(h + 1) * F], ALU.add))

            def one_group(i, s, before, added):
                c, f = s % 2, far[s]
                p = s - 1
                vectors = f[:, :, MUL:F].rearrange("p j (v o) -> p j v o", o=3)
                dve.wait_ge(gathered[s], (i + 1) * (16 * PER))
                n_along = step(dve.tensor_tensor(along[c][:], vectors, spread(rows[s][:, :, 3:6], 2, MUL),
                                                 ALU.mult))
                if before:
                    finish_b(i, p)
                if added:
                    bins = [bin_of(dve, k, i, s - 2, h) for h in range(HALVES)]
                if before:
                    n_a = finish_a(i, p)
                wait(n_along)
                n_factors = step(dve.tensor_reduce(factors[c][:, :, MUL:2 * MUL], along[c][:], AX.X, ALU.add))
                if before:
                    wait(n_a)
                    n_out = along_r(p)
                dve.wait_ge(factors_ready[c], turn(i, s, 2))
                dve.wait_ge(radial_ready[c], turn(i, s, 2))
                wait(n_factors)
                n_products = step(dve.tensor_tensor(
                    products_a[:], radial_a[:, c].rearrange("p j (q m) -> p j q m", m=2 * MUL),
                    spread(factors[c][:], 2, 2 * MUL), ALU.mult))
                if before:
                    dve.wait_ge(sum_b_wrapped[p % 2], turn(i, p, 2))
                    cross(p, 0, 1, 2)
                    n_cross = cross(p, 1, 2, 1)
                    wait(n_out)
                    n_out = add_own(p)

                def product_b(o):
                    return dve.tensor_tensor(
                        products_b[:, o], radial_b[:, c].rearrange("p j (q v) -> p j q v", v=MUL),
                        spread(vectors[:, :, :, o], 2, 2 * MUL), ALU.mult)

                step(product_b(0))
                wait(n_products)
                dve.sem_inc(products_made, 1)
                dve.sem_inc(factors_free[c], 1)
                if before:
                    wait(n_out)
                    dve.sem_inc(rows_free[p % SLOTS], 1)
                    n_out = step(add_cross(p, 0, ALU.add))
                if added:
                    n_added = accumulate(i, s - 2, 0, bins[0])
                step(product_b(1))
                if before:
                    wait(n_out)
                    add_cross(p, 1, ALU.subtract).then_inc(message_ready[p % 2], 1)
                if added:
                    for h in range(1, HALVES):
                        wait(n_added)
                        n_added = accumulate(i, s - 2, h, bins[h])
                product_b(2).then_inc(radial_free[c], 1)
                if added:
                    wait(n_added)
                    dve.sem_inc(part_free[c], 1)

            def one_turn(i, first, last):
                steps.restart()
                for s in range(SLOTS):
                    one_group(i, s, before=not (first and s == 0), added=not (first and s < 2))
                wait()

            turns(dve, "by_dst", one_turn)
            steps.restart()
            i, s = TURNS["by_dst"] - 1, SLOTS - 1
            finish_b(i, s)
            n_a = finish_a(i, s)
            wait(n_a)
            along_r(s)
            dve.wait_ge(sum_b_wrapped[s % 2], turn(i, s, 2))
            cross(s, 0, 1, 2)
            cross(s, 1, 2, 1)
            wait()
            add_own(s)
            wait()
            step(add_cross(s, 0, ALU.add))
            wait()
            add_cross(s, 1, ALU.subtract).then_inc(message_ready[s % 2], 1)
            for n in (s - 1, s):
                for h in range(HALVES):
                    accumulate(i, n, h, bin_of(dve, k, i, n, h))
                    wait()


def last_update(nc, k):
    sums = k.sums[:].rearrange("p (b w) -> p b w", w=F + 1)[:, :, 0:F]

    def before(dve, s):
        s.step(dve.tensor_tensor(k.x[:, :, 0:MUL], k.x[:, :, 0:MUL], sums[:, :, 0:MUL], ALU.add))
        vectors = k.x[:, :, MUL:F].rearrange("p b (u o) -> p b u o", o=3)
        s.step(dve.tensor_tensor(vectors, vectors,
                                 sums[:, :, MUL:F].rearrange("p b (o u) -> p b u o", o=3), ALU.add))
        s.wait()

    normalize(nc, k, "norm3", before=before, store=[(k.out, k.x)])


def gnn_kernel(nc, x, src, dst, edge_attr_3, edge_weight, L0_gnn_W, L0_gnn_b, L1_gnn_w, L1_gnn_fc_w,
               L1_gnn_fc_b, L1_gnn_bias, L3_gnn_w1, L3_gnn_b1, L3_gnn_w2, L3_gnn_b2, out):
    k = Memory()
    k.in_x, k.in_src, k.in_dst, k.in_attr, k.in_weight = x, src, dst, edge_attr_3, edge_weight
    k.in_w0, k.in_b0, k.in_w1, k.in_fc, k.in_fcb, k.in_bias1 = (
        L0_gnn_W, L0_gnn_b, L1_gnn_w, L1_gnn_fc_w, L1_gnn_fc_b, L1_gnn_bias)
    k.in_w3a, k.in_b3a, k.in_w3b, k.in_b3b = L3_gnn_w1, L3_gnn_b1, L3_gnn_w2, L3_gnn_b2
    k.out = out
    k.hops = 0

    def dram(name, shape, dt):
        return nc.dram_tensor(name, shape, dt).ap()

    k.edges_by_dst = dram("edges_by_dst", [EDGES + GROUP, BY_DST], F32)
    k.edges_by_src = dram("edges_by_src", [EDGES + GROUP, BY_SRC], F32)
    k.weight_by_group = dram("weight_by_group", [TURNS["by_dst"] * SLOTS, GROUP], F32)
    k.far_dram = dram("far_rows", [NODES, FAR], F32)
    k.hop_dram = [dram(f"hop_rows{n}", [NODES, F], F32) for n in range(2)]
    k.entry_dram = dram("entries", [TABLE, 2], I32)
    k.node_dram = dram("first_nodes", [TABLE], F32)
    with ExitStack() as ctx:
        def sb(name, shape, dt=F32):
            return ctx.enter_context(nc.sbuf_tensor(name, shape, dt))

        k.iota, k.ident, k.before, k.ones = (sb(n, [P, P]) for n in ("iota", "ident", "before", "ones"))
        k.half_less = sb("half_less", [P, P])
        k.in_order = sb("in_order", [P, 1], I32)
        k.eps = sb("eps", [P, 1])
        k.piece_no = sb("piece_no", [P, TCOLS])
        k.x = sb("x", [P, BINS, F])
        k.w0, k.b0 = sb("w0", [F, F]), sb("b0", [P, F])
        k.w1, k.w1_by_f = sb("w1", [HEADS * F, F]), sb("w1_by_f", [F, HEADS, F])
        k.fc, k.fcb, k.bias1 = sb("fc", [F, 2 * F]), sb("fcb", [P, 1]), sb("bias1", [P, F])
        k.scorer, k.scorer_parts = sb("scorer", [F, 2 * HEADS]), sb("scorer_parts", [F, HEADS, F])
        k.w3a, k.b3a = sb("w3a", [HIDDEN, 1]), sb("b3a", [HIDDEN, 1])
        k.w3, k.radial = sb("w3", [HIDDEN + 1, RADIAL]), sb("radial", [HIDDEN + 1, RADIAL])
        k.entry = {n: sb(f"entry_{n}", [1, TABLE, 2], I32) for n in ("by_dst",)}
        k.first_node = {n: sb(f"first_node_{n}", [P, TABLE]) for n in ("by_dst",)}
        k.degree, k.degree_root, k.inverse = (sb(n, [P, BINS]) for n in ("degree", "degree_root", "inverse"))
        k.own_score = sb("own_score", [P, BINS, HEADS])
        k.maximum = sb("maximum", [P, BINS * HEADS])
        k.node_terms, k.bounded = sb("node_terms", [P, BINS * 2 * HEADS]), sb("bounded", [P, 1], I32)
        k.update = sb("update", [P, BATCH, F])
        setup(nc, k)
        k.place_i = ctx.enter_context(nc.sbuf_tensor("place_i", [P, COLS], I32))
        with ExitStack() as sorting:
            k.rows = sorting.enter_context(nc.sbuf_tensor("rows_by_dst", [P, COLS, BY_DST], F32))
            by_dst = sort_memory(nc, sorting, "dst")
            pack_edges(nc, k, by_dst)
            order_by_dst(nc, k, by_dst)
        k.entry["by_src"] = sb("entry_by_src", [1, TABLE, 2], I32)
        k.first_node["by_src"] = sb("first_node_by_src", [P, TABLE])
        with nc.sbuf_tensor("sums_first", [P, BINS * (F + 1)], F32) as k.sums, \
                nc.sbuf_tensor("far_rows_sb", [P, BINS, FAR], F32) as k.far_rows:
            with ExitStack() as sorting:
                by_src = sort_memory(nc, sorting, "src")
                by_src.place = sorting.enter_context(nc.sbuf_tensor("src_place", [P, COLS], F32))
                by_src.running = sorting.enter_context(nc.sbuf_tensor("src_running", [P, COLS], F32))
                sum_messages(nc, k, k.in_x, by_src)
            with nc.sbuf_tensor("rows_by_src", [P, COLS, BY_SRC], F32) as rows:
                pack_ends(nc, k, rows)
                order_by_src(nc, k, rows)
        with nc.sbuf_tensor("hop_rows", [P, BINS, F], F32) as k.hop_rows:
            with nc.sbuf_tensor("attention", [P, BINS * HEADS * (F + 1)], F32) as k.attention, \
                    nc.sbuf_tensor("denominator", [P, BATCH, HEADS], F32) as k.denominator, \
                    nc.sbuf_tensor("share", [P, BATCH, HEADS], F32) as k.share:
                attend(nc, k)
                attention_update(nc, k)
            with nc.sbuf_tensor("sums", [P, BINS * (F + 1)], F32) as k.sums:
                sum_messages(nc, k, k.hop_dram[0])
                between_hops(nc, k)
                sum_messages(nc, k, k.hop_dram[1])
                after_hops(nc, k)
                radial_weights(nc, k)
                convolve(nc, k)
                last_update(nc, k)


_INS = ["x", "src", "dst", "edge_attr_3", "edge_weight", "L0_gnn_W", "L0_gnn_b", "L1_gnn_w", "L1_gnn_fc_w",
        "L1_gnn_fc_b", "L1_gnn_bias", "L3_gnn_w1", "L3_gnn_b1", "L3_gnn_w2", "L3_gnn_b2"]


def kernel(**inputs):
    import numpy as _np
    import concourse.bacc as _bacc
    from concourse import mybir as _mybir
    from concourse.bass_utils import run_bass_kernel_spmd as _run

    nc = _bacc.Bacc("TRN2", target_bir_lowering=False, num_devices=1)
    arrays, args = {}, []
    for name in _INS:
        a = _np.ascontiguousarray(inputs[name])
        arrays[f"in_{name}_dram"] = a
        args.append(nc.dram_tensor(f"in_{name}_dram", a.shape, _mybir.dt.from_np(a.dtype), kind="ExternalInput").ap())
    args.append(nc.dram_tensor("out_0_dram", (NODES, F), _mybir.dt.from_np(_np.dtype("float32")),
                               kind="ExternalOutput").ap())
    gnn_kernel(nc, *args)
    r = _run(nc, [arrays], core_ids=[0])
    return r.results[0]["out_0_dram"]
```
